# Optimizing a Trainium2 kernel written in Bass

```python
import numpy as np
import jax
import jax.numpy as jnp

def _softmax(x, axis=-1):
    return jax.nn.softmax(x, axis=axis)

def _gelu(x):
    return jax.nn.gelu(x, approximate=True)

def _silu(x):
    return jax.nn.silu(x)

def _sigmoid(x):
    return jax.nn.sigmoid(x)

def _layernorm(x, axis=-1, eps=1e-05):
    m = jnp.mean(x, axis=axis, keepdims=True)
    v = jnp.var(x, axis=axis, keepdims=True)
    return (x - m) / jnp.sqrt(v + eps)

def _scatter_add(tgt, idx, src, axis=0):
    return tgt.at[idx].add(src)

def _segment_sum(src, seg, n):
    return jax.ops.segment_sum(src, seg, n)
kernel_name = 'mk_adaln_attn_ffn_d1_seqx_r8_a20ffe'

def setup_inputs(seed: int=0):
    np.random.seed(seed)
    _w = jnp.asarray

    def _rec_inputs():
        import jax
        import jax.numpy as jnp
        _rk = jax.random.key(seed)
        x = -0.000125 + 0.9999 * jax.random.normal(jax.random.fold_in(_rk, 1), (2, 512, 128), jnp.float32)
        _lenS = 512 - jax.random.randint(jax.random.fold_in(_rk, 7), (2,), 0, max(1, 512 // 4) + 1, jnp.int32)
        _lenS2 = 512 - jax.random.randint(jax.random.fold_in(_rk, 8), (2,), 0, max(1, 512 // 4) + 1, jnp.int32)
        cond_1024 = 0.00513981 + 1.0024 * jax.random.normal(jax.random.fold_in(_rk, 11), (2, 128), jnp.float32)
        return (x, cond_1024)
    x, cond_1024 = _rec_inputs()

    def _L0_cond_setup():
        import jax, jax.numpy as jnp
        import numpy as np
        IN_FEATURES = 128
        OUT_FEATURES = 128
        BATCH = 32
        SEQ = 128
        EPS = 1e-08
        key = jax.random.key(seed)
        k1, k2, k3 = jax.random.split(key, 3)
        Efou = jax.random.normal(k1, (BATCH, SEQ, IN_FEATURES), dtype=jnp.float32)
        y = jax.random.normal(k2, (BATCH, IN_FEATURES), dtype=jnp.float32)
        weight = jax.random.normal(k3, (IN_FEATURES, OUT_FEATURES), dtype=jnp.float32)
        return {'Efou': Efou, 'y': y, 'weight': weight}
    _L0_cond_all = _L0_cond_setup()
    _L0_cond_in = {k: v for k, v in _L0_cond_all.items() if k in ('weight',)}
    del _L0_cond_all

    def _L0_attn_setup():
        import math
        import jax, jax.numpy as jnp
        import numpy as np
        N_HEADS = 16
        THETA = 10000.0

        def _rope_cos_sin(S, head_dim):
            half = head_dim // 2
            inv_freq = 1.0 / THETA ** (jnp.arange(half, dtype=jnp.float32) / half)
            t = jnp.arange(S, dtype=jnp.float32)
            freqs = t[:, None] * inv_freq[None, :]
            return (jnp.cos(freqs), jnp.sin(freqs))

        def _apply_rope(x, cos, sin):
            half = x.shape[-1] // 2
            x1, x2 = (x[..., :half], x[..., half:])
            c = cos[None, None, :, :]
            s = sin[None, None, :, :]
            return jnp.concatenate([x1 * c - x2 * s, x1 * s + x2 * c], axis=-1)
        key = jax.random.key(seed)
        k1, k2, k3 = jax.random.split(key, 3)
        B, S, D = (4, 256, 128)
        x = jax.random.normal(k1, (B, S, D), dtype=jnp.float32)
        w_qkv = jax.random.normal(k2, (3 * D, D), dtype=jnp.float32) * (1.0 / math.sqrt(D))
        w_out = jax.random.normal(k3, (D, D), dtype=jnp.float32) * (1.0 / math.sqrt(D))
        return {'x': x, 'w_qkv': w_qkv, 'w_out': w_out}
    _L0_attn_all = _L0_attn_setup()
    _L0_attn_in = {k: v for k, v in _L0_attn_all.items() if k in ('w_qkv', 'w_out')}
    del _L0_attn_all

    def _L0_cond2_setup():
        import jax, jax.numpy as jnp
        import numpy as np
        D_MODEL = 128
        D_FF = 512
        N_EXPERTS = 8
        TOP_K = 2
        N_SHARED = 2
        B, T = (4, 256)
        key = jax.random.key(seed)
        ks = jax.random.split(key, 9)
        Hs = D_FF // 2
        Hr = D_FF // 4
        inp = {'x': jax.random.normal(ks[0], (B, T, D_MODEL), dtype=jnp.float32), 't_emb': jax.random.normal(ks[1], (B, D_MODEL), dtype=jnp.float32), 'W_router': 0.01 * jax.random.normal(ks[2], (N_EXPERTS, 2 * D_MODEL), dtype=jnp.float32), 'router_bias': jnp.zeros((N_EXPERTS,), dtype=jnp.float32), 's_w1': 0.02 * jax.random.normal(ks[3], (N_SHARED, Hs, D_MODEL), dtype=jnp.float32), 's_w3': 0.02 * jax.random.normal(ks[4], (N_SHARED, Hs, D_MODEL), dtype=jnp.float32), 's_w2': 0.02 * jax.random.normal(ks[5], (N_SHARED, D_MODEL, Hs), dtype=jnp.float32), 'r_w1': 0.02 * jax.random.normal(ks[6], (N_EXPERTS, Hr, D_MODEL), dtype=jnp.float32), 'r_w2': 0.02 * jax.random.normal(ks[7], (N_EXPERTS, D_MODEL, Hr), dtype=jnp.float32)}
        return inp
    _L0_cond2_all = _L0_cond2_setup()
    _L0_cond2_in = {k: v for k, v in _L0_cond2_all.items() if k in ('W_router', 'router_bias', 's_w1', 's_w3', 's_w2', 'r_w1', 'r_w2')}
    del _L0_cond2_all

    def _L0_ffn_setup():
        import jax, jax.numpy as jnp
        import numpy as np
        D_MODEL = 128
        D_FF = 512
        N_ZONES = 8
        TOP_K = 3
        ROUTER_H = 32
        BATCH = 16
        SEQ = 256
        key = jax.random.key(seed)
        ks = jax.random.split(key, 8)
        s = lambda *dims: 1.0 / np.sqrt(dims[-2] if len(dims) > 1 else dims[-1])
        x = jax.random.normal(ks[0], (BATCH, SEQ, D_MODEL), dtype=jnp.float32)
        W1 = jax.random.normal(ks[1], (D_MODEL, ROUTER_H), dtype=jnp.float32) / np.sqrt(D_MODEL)
        b1 = jnp.zeros((ROUTER_H,), dtype=jnp.float32)
        W2 = jax.random.normal(ks[2], (ROUTER_H, N_ZONES), dtype=jnp.float32) / np.sqrt(ROUTER_H)
        b2 = jnp.zeros((N_ZONES,), dtype=jnp.float32)
        Wa = jax.random.normal(ks[3], (N_ZONES, D_MODEL, D_FF), dtype=jnp.float32) / np.sqrt(D_MODEL)
        Wb = jax.random.normal(ks[4], (N_ZONES, D_FF, D_MODEL), dtype=jnp.float32) / np.sqrt(D_FF)
        return {'x': x, 'W1': W1, 'b1': b1, 'W2': W2, 'b2': b2, 'Wa': Wa, 'Wb': Wb}
    _L0_ffn_all = _L0_ffn_setup()
    _L0_ffn_in = {k: v for k, v in _L0_ffn_all.items() if k in ('W1', 'b1', 'W2', 'b2', 'Wa', 'Wb')}
    del _L0_ffn_all
    return {'x': x, 'cond_1024': cond_1024, 'L0_cond_weight': _L0_cond_in['weight'], 'L0_attn_w_qkv': _L0_attn_in['w_qkv'], 'L0_attn_w_out': _L0_attn_in['w_out'], 'L0_cond2_W_router': _L0_cond2_in['W_router'], 'L0_cond2_router_bias': _L0_cond2_in['router_bias'], 'L0_cond2_s_w1': _L0_cond2_in['s_w1'], 'L0_cond2_s_w3': _L0_cond2_in['s_w3'], 'L0_cond2_s_w2': _L0_cond2_in['s_w2'], 'L0_cond2_r_w1': _L0_cond2_in['r_w1'], 'L0_cond2_r_w2': _L0_cond2_in['r_w2'], 'L0_ffn_W1': _L0_ffn_in['W1'], 'L0_ffn_b1': _L0_ffn_in['b1'], 'L0_ffn_W2': _L0_ffn_in['W2'], 'L0_ffn_b2': _L0_ffn_in['b2'], 'L0_ffn_Wa': _L0_ffn_in['Wa'], 'L0_ffn_Wb': _L0_ffn_in['Wb']}

def reference(x, cond_1024, L0_cond_weight, L0_attn_w_qkv, L0_attn_w_out, L0_cond2_W_router, L0_cond2_router_bias, L0_cond2_s_w1, L0_cond2_s_w3, L0_cond2_s_w2, L0_cond2_r_w1, L0_cond2_r_w2, L0_ffn_W1, L0_ffn_b1, L0_ffn_W2, L0_ffn_b2, L0_ffn_Wa, L0_ffn_Wb):
    import jax
    import jax.numpy as jnp

    def _L0_cond_ref(Efou, y, weight):
        import jax, jax.numpy as jnp
        import numpy as np
        IN_FEATURES = 128
        OUT_FEATURES = 128
        BATCH = 32
        SEQ = 128
        EPS = 1e-08
        scale = 1.0 / np.sqrt(np.float32(weight.shape[0]))
        ys = y * scale
        d = jax.lax.rsqrt(jnp.einsum('bi,io->bo', ys * ys, weight * weight) + EPS)
        out = jnp.einsum('bsi,io->bso', Efou * ys[:, None, :], weight) * d[:, None, :]
        return out

    def _L0_attn_ref(x, w_qkv, w_out):
        import math
        import jax, jax.numpy as jnp
        import numpy as np
        N_HEADS = 16
        THETA = 10000.0

        def _rope_cos_sin(S, head_dim):
            half = head_dim // 2
            inv_freq = 1.0 / THETA ** (jnp.arange(half, dtype=jnp.float32) / half)
            t = jnp.arange(S, dtype=jnp.float32)
            freqs = t[:, None] * inv_freq[None, :]
            return (jnp.cos(freqs), jnp.sin(freqs))

        def _apply_rope(x, cos, sin):
            half = x.shape[-1] // 2
            x1, x2 = (x[..., :half], x[..., half:])
            c = cos[None, None, :, :]
            s = sin[None, None, :, :]
            return jnp.concatenate([x1 * c - x2 * s, x1 * s + x2 * c], axis=-1)
        B, S, D = x.shape
        H = N_HEADS
        hd = D // H
        qkv = x @ w_qkv.T
        q, k, v = jnp.split(qkv, 3, axis=-1)

        def reshape(t):
            return t.reshape(B, S, H, hd).transpose(0, 2, 1, 3)
        q, k, v = (reshape(q), reshape(k), reshape(v))
        cos, sin = _rope_cos_sin(S, hd)
        q = _apply_rope(q.astype(jnp.float32), cos, sin).astype(x.dtype)
        k = _apply_rope(k.astype(jnp.float32), cos, sin).astype(x.dtype)
        scale = math.sqrt(hd)
        scores = jnp.einsum('bhsd,bhtd->bhst', q, k) / scale
        causal = jnp.tril(jnp.ones((S, S), dtype=bool))
        scores = jnp.where(causal[None, None], scores, -jnp.inf)
        attn = jax.nn.softmax(scores.astype(jnp.float32), axis=-1).astype(x.dtype)
        out = jnp.einsum('bhst,bhtd->bhsd', attn, v)
        out = out.transpose(0, 2, 1, 3).reshape(B, S, D)
        return out @ w_out.T

    def _L0_cond2_ref(x, t_emb, W_router, router_bias, s_w1, s_w3, s_w2, r_w1, r_w2):
        import jax, jax.numpy as jnp
        import numpy as np
        D_MODEL = 128
        D_FF = 512
        N_EXPERTS = 8
        TOP_K = 2
        N_SHARED = 2
        B, T = (4, 256)
        Bn, Tn, C = x.shape
        N = Bn * Tn
        x_flat = x.reshape(N, C)
        t_flat = jnp.broadcast_to(t_emb[:, None, :], (Bn, Tn, C)).reshape(N, C)
        shared_out = jnp.zeros_like(x_flat)
        for e in range(N_SHARED):
            h = jax.nn.silu(x_flat @ s_w1[e].T) * (x_flat @ s_w3[e].T)
            shared_out = shared_out + h @ s_w2[e].T
        shared_out = shared_out / N_SHARED
        router_in = jnp.concatenate([x_flat, t_flat], axis=-1)
        s = jax.nn.sigmoid((router_in @ W_router.T).astype(jnp.float32))
        sel_scores = s + router_bias
        _, topk_idx = jax.lax.top_k(sel_scores, TOP_K)
        s_sel = jnp.take_along_axis(s, topk_idx, axis=1)
        denom = jnp.sum(s_sel, axis=1, keepdims=True)
        gates = jnp.where(denom > 1e-09, s_sel / (denom + 1e-09), 1.0 / TOP_K).astype(x.dtype)
        gates_full = jnp.sum(jax.nn.one_hot(topk_idx, N_EXPERTS, dtype=x.dtype) * gates[..., None], axis=1)
        routed_out = jnp.zeros_like(x_flat)
        for e in range(N_EXPERTS):
            h = jax.nn.gelu(x_flat @ r_w1[e].T, approximate=False)
            routed_out = routed_out + h @ r_w2[e].T * gates_full[:, e:e + 1]
        out = (shared_out + routed_out) / (N_SHARED + TOP_K)
        return out.reshape(Bn, Tn, C)

    def _L0_ffn_ref(x, W1, b1, W2, b2, Wa, Wb):
        import jax, jax.numpy as jnp
        import numpy as np
        D_MODEL = 128
        D_FF = 512
        N_ZONES = 8
        TOP_K = 3
        ROUTER_H = 32
        BATCH = 16
        SEQ = 256
        pooled = x.mean(axis=1)
        h = jnp.tanh(pooled @ W1 + b1)
        logits = h @ W2 + b2
        probs = jax.nn.softmax(logits, axis=-1)
        top_p, top_i = jax.lax.top_k(probs, TOP_K)
        top_w = top_p / top_p.sum(axis=-1, keepdims=True)
        onehot = jax.nn.one_hot(top_i, N_ZONES, dtype=x.dtype)
        w = jnp.einsum('bk,bke->be', top_w, onehot)
        zone_outputs = jnp.zeros_like(x)
        for e in range(N_ZONES):
            z = jax.nn.gelu(x @ Wa[e]) @ Wb[e]
            zone_outputs = zone_outputs + z * w[:, e, None, None]
        return x + zone_outputs
    x = x + _L0_attn_ref(_L0_cond_ref(x, cond_1024, L0_cond_weight), L0_attn_w_qkv, L0_attn_w_out)
    x = x + _L0_ffn_ref(_L0_cond2_ref(x, cond_1024, L0_cond2_W_router, L0_cond2_router_bias, L0_cond2_s_w1, L0_cond2_s_w3, L0_cond2_s_w2, L0_cond2_r_w1, L0_cond2_r_w2), L0_ffn_W1, L0_ffn_b1, L0_ffn_W2, L0_ffn_b2, L0_ffn_Wa, L0_ffn_Wb)
    return x

_drawn_inputs = setup_inputs


def setup_inputs(seed=0):
    import zlib

    import numpy as np

    out = dict(_drawn_inputs(seed))
    spreads = {'L0_cond2_router_bias': (0.0, 0.8), 'L0_ffn_b1': (0.0, 0.8), 'L0_ffn_b2': (0.0, 0.8)}
    factors = {'L0_cond2_W_router': 8.0,
     'L0_cond2_s_w1': 8.0,
     'L0_cond2_s_w3': 8.0,
     'L0_cond2_s_w2': 8.0,
     'L0_cond2_r_w1': 8.0,
     'L0_cond2_r_w2': 8.0,
     'L0_ffn_W1': 8.0,
     'L0_ffn_W2': 8.0,
     'L0_ffn_Wa': 8.0,
     'L0_ffn_Wb': 8.0}
    for name, (base, spread) in spreads.items():
        noise = np.random.default_rng([zlib.crc32(name.encode()), seed]).standard_normal(out[name].shape)
        drawn = base * np.exp(spread * noise) if base else spread * noise
        out[name] = jnp.asarray(drawn.astype(out[name].dtype))
    for name, factor in factors.items():
        out[name] = (out[name] * factor).astype(out[name].dtype)
    return out
```

```python
import numpy as np
from contextlib import ExitStack

import concourse.bass as bass
from concourse import mybir

ALU = mybir.AluOpType
ACT = mybir.ActivationFunctionType
AX = mybir.AxisListType
F32 = mybir.dt.float32
F32R = mybir.dt.float32r
BF16 = mybir.dt.bfloat16
U32 = mybir.dt.uint32

P = 128
B, S, D = 2, 512, 128
NT = B * S
H, HD = 16, 8
HG = 4
NG = H // HG
GROUPS = B * NG
KB = S // P
MXU = 12
STU = 6
BIG = -1.0e30
BANK = 512

EXPERTS, SHARED, HID_S, HID_R = 8, 2, 256, 128
ZONES, TOPZ, DFF, RH = 8, 3, 512, 32

MX_UNITS = [(0, (0, 1)), (0, (2, 3)), (1, (0, 1)), (1, (2, 3))] + \
           [(qb, (j,)) for qb in (2, 3) for j in range(HG)]

C_SEL, C_ID, C_MASK, C_ONE, C_END = 0, 512, 640, 768, 769


def f32_of(ap):
    return ap.bitcast(F32)


def attention(nc, psum, io, scratch, packed_out, packed_sum, early, loaded):
    ctx = ExitStack()
    with ctx:
        def sba(name, shape, dt=F32):
            return ctx.enter_context(nc.sbuf_tensor("t_" + name, shape, dt))

        def sema(name):
            return ctx.enter_context(nc.semaphore(name))

        w_cond = sba("w_cond", [P, D])
        w_cond_sq = sba("w_cond_sq", [P, D])
        cond = sba("cond", [P, B])
        ys = sba("ys", [P, B])
        ys_sq = sba("ys_sq", [P, B])
        dvar = sba("dvar", [P, B])
        dexp = sba("dexp", [P, B])
        dinv = sba("dinv", [P, B])
        w_qkv = sba("w_qkv", [P, 3 * D])
        w_rot = sba("w_rot", [P, 2 * D])
        consts = sba("consts", [P, C_END])
        sel = sba("sel", [P, NG, 4, P], F32R)
        ident_r = sba("ident_r", [P, P], F32R)
        ident_b = sba("ident_b", [P, P], BF16)
        mask_b = sba("mask_b", [P, P], BF16)
        qk_hi = sba("qk_hi", [P, 2, S], F32R)
        qk_lo = sba("qk_lo", [P, 2, S], F32R)
        stacked = sba("stacked", [P, GROUPS, 2, S], F32R)
        v_all = sba("v_all", [P, GROUPS, KB, HG, 32])
        q_pad = [sba(f"q_pad{s}", [P, HG, S], F32R) for s in range(2)]
        k_pad = [sba(f"k_pad{s}", [P, HG, S], F32R) for s in range(2)]
        q_mov = [sba(f"q_mov{s}", [P, S], F32R) for s in range(2)]
        neg_max = [sba(f"neg_max{s}", [P, KB, HG]) for s in range(2)]
        max_pad = [sba(f"max_pad{s}", [P, KB, HG, 32], BF16) for s in range(2)]
        probs = [sba(f"probs{s}", [P, 3, HG, BANK]) for s in range(2)]
        o_sb = [sba(f"o_sb{s}", [P, S]) for s in range(2)]
        spare = probs[1][:].rearrange("p c j k -> p (c j) k")
        xT = spare[:, 0:2, :].rearrange("p b t -> p (b t)")
        xs = spare[:, 2:4, :].rearrange("p b t -> p (b t)")
        xc = spare[:, 4:6, :].rearrange("p b t -> p (b t)")
        rope_c, rope_s, roped = spare[:, 6:8, :], spare[:, 8:10, :], spare[:, 10:12, :]
        rotary = sba("rotary", [P, 2, S])
        cos_t, sin_t = rotary[:, 0, :], rotary[:, 1, :]

        MX = psum[:, 0:2, :]
        ST = psum[:, 2:6, :]
        PV = psum[:, 6, :]
        QM = psum[:, 7, :]

        ld_cond = sema("ld_cond")
        ld_proj = sema("ld_proj")
        ld_const = sema("ld_const")
        ys_ready = sema("ys_ready")
        sq_ready = sema("sq_ready")
        dsum_ready = sema("dsum_ready")
        dvar_ready = sema("dvar_ready")
        dinv_ready = sema("dinv_ready")
        xs_ready = sema("xs_ready")
        cond_ready = sema("cond_ready")
        xc_ready = sema("xc_ready")
        qk_ready = sema("qk_ready")
        v_ready = sema("v_ready")
        v_copied = sema("v_copied")
        rope_ready = sema("rope_ready")
        roped_ready = sema("roped_ready")
        hi_ready = sema("hi_ready")
        lo_ready = sema("lo_ready")
        sel_zero = sema("sel_zero")
        pads_zero = sema("pads_zero")
        v_ones = sema("v_ones")
        const_ready = sema("const_ready")
        rep_ready = sema("rep_ready")
        rep_copied = sema("rep_copied")
        q_padded = [sema(f"q_padded{s}") for s in range(2)]
        k_padded = [sema(f"k_padded{s}") for s in range(2)]
        stored = [sema(f"stored{s}") for s in range(2)]
        mx_full = sema("mx_full")
        mx_reduced = sema("mx_reduced")
        mhi_ready = sema("mhi_ready")
        m_ready = sema("m_ready")
        qm_full = sema("qm_full")
        qm_copied = sema("qm_copied")
        st_full = sema("st_full")
        exp_done = sema("exp_done")
        masked = sema("masked")
        pv_full = sema("pv_full")
        pv_copied = sema("pv_copied")
        packed = sema("packed")
        block = ctx.enter_context(nc.Block())

        @block.sync
        def _(sp):
            sp.dma_start(cond[:], io["condT"]).then_inc(ld_cond, 16)
            sp.dma_start(w_cond[:], io["L0_cond_weight"]).then_inc(ld_cond, 16)
            sp.dma_start(xT, io["xT"]).then_inc(ld_cond, 16)
            sp.dma_start(w_qkv[:], io["w_qkvT"]).then_inc(ld_proj, 16)
            sp.dma_start(w_rot[:], io["w_rotT"]).then_inc(ld_proj, 16)
            sp.dma_start(cos_t, io["cos"]).then_inc(ld_proj, 16)
            sp.dma_start(sin_t, io["sin"]).then_inc(ld_proj, 16)

            for dst, src in early:
                sp.dma_start(dst, src).then_inc(loaded, 16)

            def pad_q(n):
                s = n % 2
                sp.wait_ge(rep_copied, 2 * n + 1)
                if n >= 2:
                    sp.wait_ge(mx_full, (n - 1) * MXU)
                for j in range(HG):
                    q = slice(32 * j, 32 * j + 32)
                    sp.dma_start(f32_of(q_pad[s][q, j, :]), f32_of(stacked[q, n, 0, :])).then_inc(q_padded[s], 16)

            def pad_k(n):
                s = n % 2
                sp.wait_ge(rep_copied, 2 * n + 2)
                if n >= 2:
                    sp.wait_ge(st_full, (n - 1) * STU)
                for j in range(HG):
                    q = slice(32 * j, 32 * j + 32)
                    sp.dma_start(f32_of(k_pad[s][q, j, :]), f32_of(stacked[q, n, 1, :])).then_inc(k_padded[s], 16)

            def store_sums(n):
                sp.wait_ge(pv_copied, n + 1)
                sp.dma_start(scratch[n], o_sb[n % 2][:]).then_inc(stored[n % 2], 16)

            sp.wait_ge(pads_zero, 1)
            pad_q(0)
            pad_q(1)
            pad_k(0)
            pad_q(2)
            pad_k(1)
            for n in range(GROUPS):
                if n + 3 < GROUPS:
                    pad_q(n + 3)
                if n + 2 < GROUPS:
                    pad_k(n + 2)
                store_sums(n)
                if n % NG == NG - 1:
                    b = n // NG
                    for s in range(2):
                        sp.wait_ge(stored[s], 16 * (n + 1) // 2)
                    rows = scratch[b * NG:(b + 1) * NG].rearrange("g (j r) t -> (g j) r t", j=HG)
                    for dst, r0 in ((packed_out, 0), (packed_sum, HD)):
                        sp.dma_start(dst[:, b * S:(b + 1) * S], rows[:, r0:r0 + HD, :]).then_inc(packed, 16)
            sp.wait_ge(packed, 16 * 2 * B)

        @block.gpsimd
        def _(pool):
            nc.gpsimd.memset(f32_of(sel[:]), 0.0).then_inc(sel_zero, 1)
            pool.wait_ge(ld_cond, 48)
            nc.gpsimd.tensor_tensor(w_cond_sq[:], w_cond[:], w_cond[:], ALU.mult).then_inc(sq_ready, 1)
            nc.gpsimd.memset(dexp[:], -0.5).then_inc(sq_ready, 1)
            pool.wait_ge(sq_ready, 2)
            pool.wait_ge(dvar_ready, 1)
            nc.gpsimd.tensor_tensor(dinv[:], dvar[:], dexp[:], ALU.pow).then_inc(dinv_ready, 1)
            nc.gpsimd.memset(f32_of(k_pad[0][:]), 0.0)
            nc.gpsimd.memset(f32_of(q_pad[1][:]), 0.0)
            nc.gpsimd.memset(f32_of(k_pad[1][:]), 0.0)
            for s in range(2):
                nc.gpsimd.memset(max_pad[s][:], 0.0)
            nc.gpsimd.memset(f32_of(q_pad[0][:]), 0.0).then_inc(pads_zero, 1)
            nc.gpsimd.memset(v_all[:, :, :, :, HD:32], 1.0).then_inc(v_ones, 1)
            for n in range(GROUPS):
                for c in range(3):
                    pool.wait_ge(exp_done, STU * n + 2 * c + 2)
                    if c < 2:
                        tri = probs[n % 2][:, c, :, 0:P]
                        pat = [[0, HG], [1, P]]
                        last = nc.gpsimd.affine_select(out=tri, in_=tri, compare_op=ALU.is_ge, fill=0.0,
                                                       base=0, pattern=pat, channel_multiplier=-1)
                    else:
                        for o in (0, 3 * P):
                            tri = probs[n % 2][:, c, :, o:o + P]
                            last = nc.gpsimd.affine_select(out=tri, in_=tri, compare_op=ALU.is_ge, fill=0.0,
                                                           base=0, pattern=[[0, HG], [1, P]],
                                                           channel_multiplier=-1)
                    last.then_inc(masked, 1)

        @block.vector
        def _(dve):
            V = nc.vector
            dve.wait_ge(ld_cond, 48)
            V.tensor_scalar(ys[:], cond[:], float(np.float32(1.0) / np.sqrt(np.float32(D))), None,
                            ALU.mult).then_inc(ys_ready, 1)
            dve.wait_ge(ys_ready, 1)
            V.tensor_tensor(ys_sq[:], ys[:], ys[:], ALU.mult).then_inc(ys_ready, 1)
            for b in range(B):
                V.tensor_scalar(xs[:, b * S:(b + 1) * S], xT[:, b * S:(b + 1) * S], ys[:, b:b + 1], None,
                                ALU.mult).then_inc(xs_ready, 1)
            dve.wait_ge(dsum_ready, 1)
            V.tensor_scalar(dvar[:], QM[:, 0:B], 1e-8, None, ALU.add).then_inc(dvar_ready, 1)
            dve.wait_ge(dinv_ready, 1)

            def prepare(b):
                cols = slice(b * S, (b + 1) * S)
                dve.wait_ge(cond_ready, b + 1)
                V.tensor_scalar(xc[:, cols], PV, dinv[:, b:b + 1], None, ALU.mult).then_inc(xc_ready, 1)
                if b == 0:
                    dve.wait_ge(ld_proj, 64)
                for i in range(2):
                    dve.wait_ge(qk_ready, 2 * b + i + 1)
                    if b:
                        dve.wait_ge(roped_ready, i + 1)
                    V.tensor_tensor(rope_c[:, i, :], ST[:, 2 * i, :], cos_t, ALU.mult).then_inc(rope_ready, 1)
                    V.tensor_tensor(rope_s[:, i, :], ST[:, 2 * i + 1, :], sin_t, ALU.mult).then_inc(rope_ready, 1)
                    dve.wait_ge(rope_ready, 4 * b + 2 * i + 2)
                    if b:
                        dve.wait_ge(hi_ready, 2)
                        dve.wait_ge(lo_ready, i + 1)
                    V.tensor_tensor(roped[:, i, :], rope_c[:, i, :], rope_s[:, i, :], ALU.add).then_inc(roped_ready, 1)
                for i in range(2):
                    dve.wait_ge(hi_ready, 2 * b + i + 1)
                    if b:
                        dve.wait_ge(rep_ready, 2 * NG)
                    V.tensor_tensor(qk_lo[:, i, :], roped[:, i, :], f32_of(qk_hi[:, i, :]),
                                    ALU.subtract).then_inc(lo_ready, 1)

            def reduce_max(n, s, u):
                qb, heads = MX_UNITS[u]
                width = P * (qb + 1)
                dve.wait_ge(mx_full, MXU * n + u + 1)
                src = MX[:, u % 2, :]
                if len(heads) == 2:
                    src = src.rearrange("p (h k) -> p h k", h=2)[:, :, 0:width]
                    out = neg_max[s][:, qb, heads[0]:heads[0] + 2]
                else:
                    src = src[:, 0:width]
                    out = neg_max[s][:, qb, heads[0]:heads[0] + 1]
                V.tensor_reduce(out, src, AX.X, ALU.max, negate=True).then_inc(mx_reduced, 1)

            def place_max(n, s, first=False):
                dve.wait_ge(mx_reduced, MXU * (n + 1))
                if not first:
                    dve.wait_ge(qm_full, n - 1)
                V.tensor_copy(max_pad[s][:, :, :, 0], neg_max[s][:]).then_inc(mhi_ready, 1)
                dve.wait_ge(mhi_ready, n + 1)
                V.tensor_tensor(max_pad[s][:, :, :, 1], neg_max[s][:], max_pad[s][:, :, :, 0],
                                ALU.subtract).then_inc(m_ready, 1)

            prepare(0)
            dve.wait_ge(pads_zero, 1)
            for u in range(MXU):
                reduce_max(0, 0, u)
            place_max(0, 0, True)
            prepare(1)
            for u in range(MXU):
                reduce_max(1, 1, u)
            place_max(1, 1, True)
            for n in range(2, GROUPS):
                for u in range(MXU):
                    reduce_max(n, n % 2, u)
                place_max(n, n % 2)

        @block.scalar
        def _(act):
            A = nc.scalar
            act.dma_start(consts[:], io["consts"]).then_inc(ld_const, 16)
            act.wait_ge(ld_const, 16)
            act.wait_ge(sel_zero, 1)
            for g in range(NG):
                q = slice(32 * g, 32 * g + 32)
                A.copy(sel[q, g, :, :], consts[q, C_SEL:C_ID].rearrange("p (t m) -> p t m", t=4))
            A.copy(ident_r[:], consts[:, C_ID:C_MASK])
            A.copy(ident_b[:], consts[:, C_ID:C_MASK])
            A.copy(mask_b[:], consts[:, C_MASK:C_ONE]).then_inc(const_ready, 1)

            def prepare(b):
                for i in range(2):
                    act.wait_ge(roped_ready, 2 * b + i + 1)
                    if b:
                        act.wait_ge(rep_ready, 2 * NG)
                    A.copy(qk_hi[:, i, :], roped[:, i, :]).then_inc(hi_ready, 1)
                act.wait_ge(v_ready, b + 1)
                if b == 0:
                    act.wait_ge(v_ones, 1)
                for kb in range(KB):
                    A.copy(v_all[:, b * NG:(b + 1) * NG, kb, :, 0:HD],
                           QM[:, kb * P:(kb + 1) * P].rearrange("p (g j d) -> p g j d", g=NG, j=HG)
                           ).then_inc(v_copied, 1)
                for w in range(2 * NG):
                    g, i = divmod(w, 2)
                    act.wait_ge(rep_ready, 2 * NG * b + w + 1)
                    out = stacked[:, b * NG + g, i, :]
                    if i == 0:
                        A.copy(out, ST[:, w % 4, :]).then_inc(rep_copied, 1)
                    else:
                        A.activation(out, ST[:, w % 4, :], ACT.Identity,
                                     bias=consts[:, C_ONE:C_END]).then_inc(rep_copied, 1)

            def exp(n, s, u):
                c, h2 = divmod(u, 2)
                act.wait_ge(st_full, STU * n + u + 1)
                if isinstance(n, int) and n >= 2 and u == 0:
                    act.wait_ge(pv_full, n - 1)
                w = (BANK, 3 * P, BANK)[c]
                A.activation(probs[s][:, c, 2 * h2:2 * h2 + 2, 0:w],
                             ST[:, 2 * (u % 2):2 * (u % 2) + 2, 0:w], ACT.Exp,
                             scale=float(1.0 / np.sqrt(np.float32(HD)))).then_inc(exp_done, 1)

            def copy_qm(n, s):
                act.wait_ge(qm_full, n + 1)
                A.copy(q_mov[s][:], QM).then_inc(qm_copied, 1)

            def copy_pv(n, s):
                act.wait_ge(pv_full, n + 1)
                if n >= 2:
                    act.wait_ge(stored[s], 16 * (n // 2))
                A.copy(o_sb[s][:], PV).then_inc(pv_copied, 1)

            prepare(0)
            prepare(1)
            copy_qm(0, 0)
            exp(0, 0, 0)
            exp(0, 0, 1)
            for n in range(GROUPS):
                s = n % 2
                exp(n, s, 2)
                exp(n, s, 3)
                if n + 1 < GROUPS:
                    copy_qm(n + 1, 1 - s)
                exp(n, s, 4)
                exp(n, s, 5)
                if n + 1 < GROUPS:
                    exp(n + 1, 1 - s, 0)
                    exp(n + 1, 1 - s, 1)
                copy_pv(n, s)

        @block.tensor
        def _(pe):
            T = nc.tensor
            pe.wait_ge(ys_ready, 2)
            pe.wait_ge(sq_ready, 1)
            T.matmul(QM[:, 0:B], w_cond_sq[:], ys_sq[:], start=True, stop=True).then_inc(dsum_ready, 1)

            def prepare(b):
                cols = slice(b * S, (b + 1) * S)
                pe.wait_ge(xs_ready, b + 1)
                T.matmul(PV, w_cond[:], xs[:, cols], start=True, stop=True).then_inc(cond_ready, 1)
                pe.wait_ge(xc_ready, b + 1)
                if b == 0:
                    pe.wait_ge(ld_proj, 64)
                if b:
                    pe.wait_ge(rep_copied, 2 * NG)
                for i in range(2):
                    T.matmul(ST[:, 2 * i, :], w_qkv[:, i * D:(i + 1) * D], xc[:, cols], start=True, stop=True)
                    T.matmul(ST[:, 2 * i + 1, :], w_rot[:, i * D:(i + 1) * D], xc[:, cols],
                             start=True, stop=True).then_inc(qk_ready, 1)
                if b == 0:
                    pe.wait_ge(dvar_ready, 1)
                for kb in range(KB):
                    last = T.matmul(QM[:, kb * P:(kb + 1) * P], xc[:, b * S + kb * P:b * S + (kb + 1) * P],
                                    w_qkv[:, 2 * D:3 * D], start=True, stop=True)
                last.then_inc(v_ready, 1)
                if b == 0:
                    pe.wait_ge(const_ready, 1)
                for w in range(2 * NG):
                    g, i = divmod(w, 2)
                    if w < 2:
                        pe.wait_ge(lo_ready, 2 * b + w + 1)
                        pe.wait_ge(rope_ready, 4 * b + 4)
                    if w >= 4:
                        pe.wait_ge(rep_copied, 2 * NG * b + w - 3)
                    T.matmul(ST[:, w % 4, :], sel[:, g, 2 * i, :], qk_hi[:, i, :], start=True, stop=False)
                    T.matmul(ST[:, w % 4, :], sel[:, g, 2 * i + 1, :], qk_lo[:, i, :],
                             start=False, stop=True).then_inc(rep_ready, 1)

            def scores_for_max(n, s, u, first=False):
                qb, heads = MX_UNITS[u]
                width = max(2 * P, P * (qb + 1))
                if u == 0:
                    pe.wait_ge(q_padded[s], 16 * HG * (n // 2 + 1))
                    pe.wait_ge(rep_copied, 2 * n + 2)
                if not (first and u < 2):
                    pe.wait_ge(mx_reduced, MXU * n + u - 1)
                for i, j in enumerate(heads):
                    o = MX[:, u % 2, i * 2 * P:i * 2 * P + width]
                    diag = MX[:, u % 2, i * 2 * P + qb * P:i * 2 * P + (qb + 1) * P]
                    T.matmul(o, q_pad[s][:, j, qb * P:(qb + 1) * P], stacked[:, n, 1, 0:width], start=True, stop=True)
                    last = T.matmul(diag, mask_b[:], ident_b[:], start=False, stop=True, skip_group_check=True)
                last.then_inc(mx_full, 1)

            def lay_max_under_q(n, s, first=False):
                pe.wait_ge(m_ready, n + 1)
                if first:
                    pe.wait_ge(v_copied, B * KB)
                else:
                    pe.wait_ge(qm_copied, n)
                T.matmul(QM, ident_r[:], stacked[:, n, 0, :], start=True, stop=True)
                for qb in range(KB):
                    last = T.matmul(QM[:, qb * P:(qb + 1) * P],
                                    max_pad[s][:, qb, :, :].rearrange("p j r -> p (j r)"), ident_b[:],
                                    start=False, stop=True, skip_group_check=True)
                last.then_inc(qm_full, 1)

            def scores_for_exp(n, s, u, first=False):
                c, h2 = divmod(u, 2)
                if u == 0:
                    pe.wait_ge(qm_copied, n + 1)
                    pe.wait_ge(k_padded[s], 16 * HG * (n // 2 + 1))
                if first and u < 2:
                    pe.wait_ge(rep_copied, 2 * GROUPS)
                else:
                    pe.wait_ge(exp_done, STU * n + u - 1)
                for i in range(2):
                    j = 2 * h2 + i
                    bank = ST[:, 2 * (u % 2) + i, :]
                    if c == 0:
                        last = T.matmul(bank, k_pad[s][:, j, 0:P], q_mov[s][:], start=True, stop=True)
                    elif c == 1:
                        last = T.matmul(bank[:, 0:3 * P], k_pad[s][:, j, P:2 * P], q_mov[s][:, P:S],
                                        start=True, stop=True)
                    else:
                        T.matmul(bank[:, 0:2 * P], k_pad[s][:, j, 2 * P:3 * P], q_mov[s][:, 2 * P:S],
                                 start=True, stop=True)
                        last = T.matmul(bank[:, 2 * P:S], k_pad[s][:, j, 3 * P:S], q_mov[s][:, 2 * P:S],
                                        start=True, stop=True)
                last.then_inc(st_full, 1)

            def weigh_v(n, s, c):
                pe.wait_ge(masked, 3 * n + c + 1)
                if c == 0 and n:
                    pe.wait_ge(pv_copied, n)
                if c == 0:
                    pe.wait_ge(v_copied, KB * (n // NG + 1))
                    pe.wait_ge(v_ones, 1)
                blocks = [(0, 0, S)] if c == 0 else [(1, 0, 3 * P)] if c == 1 else [(2, 0, 2 * P), (3, 3 * P, P)]
                for kb, o, w in blocks:
                    for j in range(HG):
                        last = T.matmul(PV[32 * j:32 * j + 32, S - w:S], v_all[:, n, kb, j, :],
                                        probs[s][:, c, j, o:o + w], start=(kb == 0), stop=(kb == KB - 1),
                                        skip_group_check=True)
                if c == 2:
                    last.then_inc(pv_full, 1)

            prepare(0)
            for u in range(MXU):
                scores_for_max(0, 0, u, True)
            prepare(1)
            for u in range(MXU):
                scores_for_max(1, 1, u)
            lay_max_under_q(0, 0, True)
            scores_for_exp(0, 0, 0, True)
            scores_for_exp(0, 0, 1, True)
            for n in range(GROUPS):
                s = n % 2
                more_max = n + 2 < GROUPS

                def mx(u):
                    if more_max:
                        scores_for_max(n + 2, s, u)
                        scores_for_max(n + 2, s, u + 1)

                mx(0)
                scores_for_exp(n, s, 2)
                mx(2)
                scores_for_exp(n, s, 3)
                if n + 1 < GROUPS:
                    lay_max_under_q(n + 1, 1 - s)
                mx(4)
                scores_for_exp(n, s, 4)
                mx(6)
                weigh_v(n, s, 0)
                scores_for_exp(n, s, 5)
                mx(8)
                if n + 1 < GROUPS:
                    scores_for_exp(n + 1, 1 - s, 0)
                weigh_v(n, s, 1)
                mx(10)
                if n + 1 < GROUPS:
                    scores_for_exp(n + 1, 1 - s, 1)
                weigh_v(n, s, 2)


def host_constants():
    pattern = np.zeros((4, 32, P), np.float32)
    for j in range(HG):
        for d in range(HD):
            src = j * HD + d
            for t, blocks in enumerate(((1, 2), (3,), (1, 3), (2,))):
                for r in blocks:
                    pattern[t, src, 32 * j + HD * r + d] = 1.0
    consts = np.zeros((P, C_END), np.float32)
    consts[:, C_SEL:C_ID] = np.tile(pattern.transpose(1, 0, 2).reshape(32, 4 * P), (4, 1))
    consts[:, C_ID:C_MASK] = np.eye(P, dtype=np.float32)
    k, q = np.mgrid[0:P, 0:P]
    consts[:, C_MASK:C_ONE] = np.where(k > q, np.float32(BIG), np.float32(0.0))
    consts[:, C_ONE] = np.isin(np.arange(P) % 32, (0, 1))
    half = HD // 2
    inv = (1.0 / np.power(np.float32(10000.0), np.arange(half, dtype=np.float32) / np.float32(half))).astype(np.float32)
    ang = (np.arange(S, dtype=np.float32)[:, None] * inv[None, :]).astype(np.float64)
    cos = np.cos(ang).astype(np.float32).T
    sin = np.sin(ang).astype(np.float32).T
    cos = np.tile(np.concatenate([cos, cos]), (H, 1))
    sin = np.tile(np.concatenate([-sin, sin]), (H, 1))
    return consts, np.ascontiguousarray(cos), np.ascontiguousarray(sin)


def swapped(w):
    return w.reshape(-1, 2, HD // 2, D)[:, ::-1].reshape(-1, D)


EXP_UNITS = SHARED * HID_S // P + EXPERTS
SH_UNITS = SHARED * HID_S // P
FFN_UNITS = TOPZ * DFF // P
ZM = DFF // P
STEPS = B * TOPZ
E_TOTAL = B * EXP_UNITS
UNITS = [("shared", b, i) for b in range(0)]
for _b in range(B):
    UNITS += [("shared", _b, i) for i in range(SH_UNITS)] + [("routed", _b, e) for e in range(EXPERTS)]
for _b in range(B):
    UNITS += [("zone", _b, i) for i in range(FFN_UNITS)]
N_UNITS = len(UNITS)
RING = 3
W_OUT, W_R, W_RB, W_IOTA, W_Z1, W_Z2, W_B1, W_B2, W_SEL = 0, 128, 144, 152, 160, 192, 200, 201, 209
W_END = W_SEL + EXPERTS * P


def experts_and_zones(nc, psum, io, mem, packed_out, packed_sum, loaded, out):
    ctx = ExitStack()
    with ctx:
        def sba(name, shape, dt=F32):
            return ctx.enter_context(nc.sbuf_tensor("u_" + name, shape, dt))

        def sema(name):
            return ctx.enter_context(nc.semaphore(name))

        small, s_up, r_up, s_dn, r_dn, cond = mem
        zone_a = sba("zone_a", [P, ZONES, DFF])
        zone_b = sba("zone_b", [P, ZONES, ZM, D])
        xT = sba("xT", [P, NT])
        recip = sba("recip", [P, NT])
        o_norm = sba("o_norm", [P, NT])
        x1 = sba("x1", [P, NT])
        x1_hi = sba("x1_hi", [P, NT], F32R)
        x1_lo = sba("x1_lo", [P, NT], F32R)
        x2 = sba("x2", [P, NT])
        x2_hi = sba("x2_hi", [P, NT], F32R)
        x2_lo = sba("x2_lo", [P, NT], F32R)
        x12 = sba("x12", [P, NT])
        y = sba("y", [P, NT])
        up_hi = sba("up_hi", [P, 2048], F32R)
        up_lo = sba("up_lo", [P, 2048], F32R)
        dn_hi = sba("dn_hi", [P, 1536], F32R)
        dn_lo = sba("dn_lo", [P, 1536], F32R)
        sel_e = sba("sel_e", [P, EXPERTS, P], F32R)
        temb = sba("temb", [P, B, P])
        ident = sba("ident", [P, P])
        e_neg = sba("e_neg", [P, B, KB, EXPERTS])
        e_one = sba("e_one", [P, B, KB, EXPERTS])
        sig = sba("sig", [P, B, KB, EXPERTS])
        rank = sba("rank", [P, B, KB, EXPERTS])
        top = sba("top", [P, B, KB, 8])
        top_i = sba("top_i", [P, B, KB, 8], U32)
        top_f = sba("top_f", [P, B, KB, 2])
        eq0 = sba("eq0", [P, B, KB, EXPERTS])
        eq1 = sba("eq1", [P, B, KB, EXPERTS])
        chosen = sba("chosen", [P, B, KB, EXPERTS])
        s_sel = sba("s_sel", [P, B, KB, EXPERTS])
        denom = sba("denom", [P, B, KB])
        okay = sba("okay", [P, B, KB])
        denom_e = sba("denom_e", [P, B, KB])
        inv_d = sba("inv_d", [P, B, KB])
        scale_s = sba("scale_s", [P, B, KB])
        scale_c = sba("scale_c", [P, B, KB])
        part_s = sba("part_s", [P, B, KB, EXPERTS])
        part_c = sba("part_c", [P, B, KB, EXPERTS])
        gate = sba("gate", [P, B, KB, EXPERTS])
        gate_hl = sba("gate_hl", [P, B, KB, 2 * EXPERTS])
        gates_t = [sba(f"gates_t{b}", [P, S], F32R) for b in range(B)]
        pooled = sba("pooled", [P, B])
        hid = sba("hid", [RH, B])
        zl = sba("zl", [1, B, ZONES])
        ztop = sba("ztop", [1, B, 8])
        zidx = sba("zidx", [1, B, 8], U32)
        zdiff = sba("zdiff", [1, B, TOPZ])
        euler = sba("euler", [1, TOPZ])
        zexp = sba("zexp", [1, B, TOPZ])
        zsum = sba("zsum", [1, B])
        zinv = sba("zinv", [1, B])
        zw = sba("zw", [1, B, TOPZ])
        ones_row = sba("ones_row", [1, P])
        zw_all = sba("zw_all", [P, B, TOPZ])
        wa_hi = [sba(f"wa_hi{s}", [P, DFF], F32R) for s in range(2)]
        wa_lo = [sba(f"wa_lo{s}", [P, DFF], F32R) for s in range(2)]
        wb_hi = [sba(f"wb_hi{s}", [P, ZM, D], F32R) for s in range(2)]
        wb_lo = [sba(f"wb_lo{s}", [P, ZM, D], F32R) for s in range(2)]
        act_out = [sba(f"act_out{r}", [P, S]) for r in range(RING)]
        silu = sba("silu", [P, S])
        hidden = [sba(f"hidden{r}", [P, S]) for r in range(RING)]
        h_hi = [sba(f"h_hi{r}", [P, S], F32R) for r in range(RING)]
        h_lo = [sba(f"h_lo{r}", [P, S], F32R) for r in range(RING)]

        OUT, MISC = psum[:, 6, :], psum[:, 7, :]

        ld_x = sema("ld_x")
        ld_zones = sema("ld_zones")
        setup_zero = sema("setup_zero")
        temb_ready = sema("temb_ready")
        recip_ready = sema("recip_ready")
        onorm_ready = sema("onorm_ready")
        proj_ready = sema("proj_ready")
        x1_ready = sema("x1_ready")
        x1_hi_ready = sema("x1_hi_ready")
        x1_lo_ready = sema("x1_lo_ready")
        sel_ready = sema("sel_ready")
        w_hi = sema("w_hi")
        w_lo = sema("w_lo")
        logits = sema("logits")
        expneg = sema("expneg")
        gate_step = sema("gate_step")
        gate_ready = sema("gate_ready")
        gateT_full = sema("gateT_full")
        gateT_copied = sema("gateT_copied")
        up_full = sema("up_full")
        act_done = sema("act_done")
        silu_done = sema("silu_done")
        h_ready = sema("h_ready")
        hi_done = sema("hi_done")
        lo_done = sema("lo_done")
        down_done = sema("down_done")
        x2_ready = sema("x2_ready")
        x2_hi_ready = sema("x2_hi_ready")
        x2_lo_ready = sema("x2_lo_ready")
        x12_ready = sema("x12_ready")
        z_hid = sema("z_hid")
        z_tanh = sema("z_tanh")
        z_logit = sema("z_logit")
        z_step = sema("z_step")
        z_diff = sema("z_diff")
        z_exp = sema("z_exp")
        z_w = sema("z_w")
        z_bc = sema("z_bc")
        z_all = sema("z_all")
        zone_hi = sema("zone_hi")
        zone_lo = sema("zone_lo")
        y_ready = sema("y_ready")
        stored_y = sema("stored_y")
        block = ctx.enter_context(nc.Block())

        def cols(b):
            return slice(b * S, (b + 1) * S)

        def up_cols(kind, i):
            if kind == "shared":
                e, m = divmod(i, HID_S // P)
                return [(2 * e + t) * HID_S + m * P for t in range(2)]
            return [SHARED * 2 * HID_S + i * P]

        def dn_col(kind, i):
            return i * D if kind == "shared" else SH_UNITS * D + i * D

        @block.sync
        def _(sp):
            sp.dma_start(xT[:], io["xT"]).then_inc(ld_x, 16)
            sp.dma_start(ident[:], io["consts"][:, C_ID:C_MASK]).then_inc(ld_x, 16)
            for lo in range(0, ZONES, 4):
                sp.dma_start(zone_a[:, lo:lo + 4, :],
                             io["L0_ffn_Wa"][lo:lo + 4].rearrange("e p f -> p e f")).then_inc(ld_zones, 16)
                sp.dma_start(zone_b[:, lo:lo + 4, :, :],
                             io["L0_ffn_Wb"][lo:lo + 4].rearrange("e (m p) d -> p e m d", p=P)).then_inc(ld_zones, 16)
            for b in range(B):
                sp.wait_ge(y_ready, b + 1)
                sp.dma_start(out[:, cols(b)], y[:, cols(b)]).then_inc(stored_y, 16)
            sp.wait_ge(stored_y, 16 * B)

        @block.gpsimd
        def _(pool):
            G = nc.gpsimd
            G.memset(f32_of(sel_e[:]), 0.0)
            for b in range(B):
                G.memset(f32_of(gates_t[b][:]), 0.0)
            G.memset(ones_row[:], 1.0)
            G.memset(euler[:], float(np.e)).then_inc(setup_zero, 1)
            for b in range(B):
                pool.wait_ge(x1_ready, b + 1)
                pool.wait_ge(x2_ready, b + 1)
                G.tensor_tensor(x12[:, cols(b)], x1[:, cols(b)], x2[:, cols(b)], ALU.add).then_inc(x12_ready, 1)
                pool.wait_ge(z_diff, b + 1)
                G.tensor_tensor(zexp[:, b, :], euler[:], zdiff[:, b, :], ALU.pow).then_inc(z_exp, 1)
                pool.wait_ge(z_all, b + 1)
                if b == 0:
                    pool.wait_ge(ld_zones, 16 * 4)
                for k in range(TOPZ):
                    z = b * TOPZ + k
                    zone = G.value_load(zidx[0:1, b, k:k + 1], min_val=0, max_val=ZONES - 1)
                    if z >= 2:
                        pool.wait_ge(down_done, E_TOTAL + ZM * (z - 1))
                        pool.wait_ge(zone_lo, z - 1)
                    G.tensor_copy(wa_hi[z % 2][:], zone_a[:, bass.ds(zone, 1), :]).then_inc(zone_hi, 1)
                    G.tensor_tensor(wb_hi[z % 2][:].rearrange("p m d -> p (m d)"),
                                    zone_b[:].rearrange("p e m d -> p e (m d)")[:, bass.ds(zone, 1), :],
                                    zw_all[:, b, k:k + 1].broadcast_to([P, DFF]), ALU.mult).then_inc(zone_hi, 1)

        @block.vector
        def _(dve):
            V = nc.vector
            dve.wait_ge(loaded, 16 * N_EARLY)
            for b in range(B):
                V.tensor_copy(temb[:, b, :], cond[:, b:b + 1].broadcast_to([P, P])).then_inc(temb_ready, 1)
            for b in range(B):
                V.reciprocal(recip[:, cols(b)], packed_sum[:, cols(b)]).then_inc(recip_ready, 1)
                dve.wait_ge(recip_ready, b + 1)
                V.tensor_tensor(o_norm[:, cols(b)], packed_out[:, cols(b)], recip[:, cols(b)],
                                ALU.mult).then_inc(onorm_ready, 1)
            dve.wait_ge(ld_x, 32)
            for b in range(B):
                dve.wait_ge(proj_ready, b + 1)
                V.tensor_tensor(x1[:, cols(b)], psum[:, b, :], xT[:, cols(b)], ALU.add).then_inc(x1_ready, 1)
            for b in range(B):
                dve.wait_ge(x1_hi_ready, b + 1)
                V.tensor_tensor(x1_lo[:, cols(b)], x1[:, cols(b)], f32_of(x1_hi[:, cols(b)]),
                                ALU.subtract).then_inc(x1_lo_ready, 1)

            def weights_lo(part):
                hi, lo, src, at = W_PARTS[part]
                dve.wait_ge(w_hi, part + 1)
                V.tensor_tensor(lo[:, at:at + src.shape[1]], src[:], f32_of(hi[:, at:at + src.shape[1]]),
                                ALU.subtract).then_inc(w_lo, 1)

            W_PARTS = [(up_hi, up_lo, s_up, 0), (dn_hi, dn_lo, s_dn, 0),
                       (up_hi, up_lo, r_up, 1024), (dn_hi, dn_lo, r_dn, 512)]

            steps = [0]

            def step(ins):
                steps[0] += 1
                ins.then_inc(gate_step, 1)
                dve.wait_ge(gate_step, steps[0])

            def gates(b):
                dve.wait_ge(expneg, b + 1)
                sg, ch = sig[:, b], chosen[:, b]
                step(V.tensor_scalar(e_one[:, b], e_neg[:, b], 1.0, None, ALU.add))
                step(V.reciprocal(sg, e_one[:, b]))
                bias = small[:, W_RB:W_RB + EXPERTS].unsqueeze(1).broadcast_to([P, KB, EXPERTS])
                step(V.tensor_tensor(rank[:, b], sg, bias, ALU.add))
                for t in range(KB):
                    last = V.max(top[:, b, t, :], rank[:, b, t, :])
                step(last)
                for t in range(KB):
                    last = V.max_index(top_i[:, b, t, :], top[:, b, t, :], rank[:, b, t, :])
                step(last)
                step(V.tensor_copy(top_f[:, b], top_i[:, b, :, 0:2]))
                iota = small[:, W_IOTA:W_IOTA + EXPERTS].unsqueeze(1).broadcast_to([P, KB, EXPERTS])
                for o, eq in ((0, eq0), (1, eq1)):
                    last = V.tensor_tensor(eq[:, b], iota,
                                           top_f[:, b, :, o:o + 1].broadcast_to([P, KB, EXPERTS]), ALU.is_equal)
                step(last)
                step(V.tensor_tensor(ch, eq0[:, b], eq1[:, b], ALU.add))
                step(V.tensor_tensor(s_sel[:, b], ch, sg, ALU.mult))
                step(V.tensor_reduce(denom[:, b], s_sel[:, b], AX.X, ALU.add))
                V.tensor_scalar(okay[:, b], denom[:, b], 1e-9, None, ALU.is_gt)
                step(V.tensor_scalar(denom_e[:, b], denom[:, b], 1e-9, None, ALU.add))
                V.tensor_scalar(scale_c[:, b], okay[:, b], -2.0, 2.0, ALU.mult, ALU.add)
                step(V.reciprocal(inv_d[:, b], denom_e[:, b]))
                step(V.scalar_tensor_tensor(scale_s[:, b], inv_d[:, b], 4.0, okay[:, b], ALU.mult, ALU.mult))
                V.tensor_tensor(part_s[:, b], s_sel[:, b],
                                scale_s[:, b].unsqueeze(2).broadcast_to([P, KB, EXPERTS]), ALU.mult)
                step(V.tensor_tensor(part_c[:, b], ch,
                                     scale_c[:, b].unsqueeze(2).broadcast_to([P, KB, EXPERTS]), ALU.mult))
                step(V.tensor_tensor(gate[:, b], part_s[:, b], part_c[:, b], ALU.add))
                step(V.tensor_copy(gate_hl[:, b, :, 0:EXPERTS].bitcast(F32R), gate[:, b]))
                V.tensor_tensor(gate_hl[:, b, :, EXPERTS:], gate[:, b], gate_hl[:, b, :, 0:EXPERTS],
                                ALU.subtract).then_inc(gate_ready, 1)

            zsteps = [0]

            def zstep(ins):
                zsteps[0] += 1
                ins.then_inc(z_step, 1)
                dve.wait_ge(z_step, zsteps[0])

            def choose_zones(b):
                dve.wait_ge(z_logit, b + 1)
                zstep(V.tensor_tensor(zl[:, b, :], MISC[0:1, 72:80], small[0:1, W_B2:W_B2 + ZONES], ALU.add))
                zstep(V.max(ztop[:, b, :], zl[:, b, :]))
                V.max_index(zidx[:, b, :], ztop[:, b, :], zl[:, b, :])
                V.tensor_scalar(zdiff[:, b, :], ztop[:, b, 0:TOPZ], ztop[:, b, 0:1], None,
                                ALU.subtract).then_inc(z_diff, 1)

            def weigh_zones(b):
                dve.wait_ge(z_exp, b + 1)
                zstep(V.tensor_reduce(zsum[:, b:b + 1], zexp[:, b, :], AX.X, ALU.add))
                zstep(V.reciprocal(zinv[:, b:b + 1], zsum[:, b:b + 1]))
                V.tensor_scalar(zw[:, b, :], zexp[:, b, :], zinv[:, b:b + 1], None, ALU.mult).then_inc(z_w, 1)

            def spread_weights(b):
                dve.wait_ge(z_bc, b + 1)
                V.tensor_copy(zw_all[:, b, :], MISC[:, 80:80 + TOPZ]).then_inc(z_all, 1)

            def zone_weights_lo(z):
                b, k = divmod(z, TOPZ)
                dve.wait_ge(z_diff, b + 1)
                zone = V.value_load(zidx[0:1, b, k:k + 1], min_val=0, max_val=ZONES - 1)
                dve.wait_ge(zone_hi, 2 * z + 2)
                if z >= 2:
                    dve.wait_ge(down_done, E_TOTAL + ZM * (z - 1))
                dve.wait_ge(z_all, b + 1)
                V.tensor_tensor(wa_lo[z % 2][:], zone_a[:, bass.ds(zone, 1), :], f32_of(wa_hi[z % 2][:]),
                                ALU.subtract)
                V.scalar_tensor_tensor(wb_lo[z % 2][:].rearrange("p m d -> p (m d)"),
                                       zone_b[:].rearrange("p e m d -> p e (m d)")[:, bass.ds(zone, 1), :],
                                       zw_all[:, b, k:k + 1],
                                       f32_of(wb_hi[z % 2][:]).rearrange("p m d -> p (m d)"),
                                       ALU.mult, ALU.subtract).then_inc(zone_lo, 1)

            n_silu = [0]

            def finish_hidden(i):
                kind, b, w = UNITS[i]
                r = i % RING
                if kind == "zone":
                    return
                dve.wait_ge(act_done, i + 1)
                if i >= RING:
                    dve.wait_ge(hi_done, i - RING + 1)
                    dve.wait_ge(lo_done, i - RING + 1)
                pair = psum[:, 2 * r:2 * r + 2, :]
                if kind == "shared":
                    if i:
                        dve.wait_ge(h_ready, i)
                    V.scalar_tensor_tensor(silu[:], act_out[r][:], 1.0, pair[:, 0, :], ALU.add,
                                           ALU.mult).then_inc(silu_done, 1)
                    n_silu[0] += 1
                    dve.wait_ge(silu_done, n_silu[0])
                    V.tensor_tensor(hidden[r][:], silu[:], pair[:, 1, :], ALU.mult).then_inc(h_ready, 1)
                else:
                    V.tensor_tensor(hidden[r][:], act_out[r][:], pair[:, 1, :], ALU.mult).then_inc(h_ready, 1)

            def hidden_lo(i):
                r = i % RING
                src = act_out[r] if UNITS[i][0] == "zone" else hidden[r]
                dve.wait_ge(hi_done, i + 1)
                if i >= RING:
                    dve.wait_ge(down_done, i - RING + 1)
                V.tensor_tensor(h_lo[r][:], src[:], f32_of(h_hi[r][:]), ALU.subtract).then_inc(lo_done, 1)

            def x2_low(b):
                dve.wait_ge(x2_hi_ready, b + 1)
                V.tensor_tensor(x2_lo[:, cols(b)], x2[:, cols(b)], f32_of(x2_hi[:, cols(b)]),
                                ALU.subtract).then_inc(x2_lo_ready, 1)

            def add_residual(b):
                dve.wait_ge(down_done, E_TOTAL + (b + 1) * FFN_UNITS)
                dve.wait_ge(x12_ready, b + 1)
                V.tensor_tensor(y[:, cols(b)], OUT, x12[:, cols(b)], ALU.add).then_inc(y_ready, 1)

            weights_lo(0)
            weights_lo(1)
            extras = {0: [lambda: gates(0)], 1: [lambda: weights_lo(2), lambda: gates(1)], 2: [lambda: weights_lo(3)]}
            for b in range(B):
                o = EXP_UNITS * (b + 1)
                for at, what in ((1, lambda b=b: x2_low(b)), (6, lambda b=b: choose_zones(b)),
                                 (7, lambda b=b: weigh_zones(b)), (9, lambda b=b: spread_weights(b))):
                    extras.setdefault(o + at, []).append(what)
            for z in range(STEPS):
                at = EXP_UNITS + 10 + z if z < 2 else E_TOTAL + ZM * (z - 1) + 2
                extras.setdefault(at, []).append(lambda z=z: zone_weights_lo(z))
            extras.setdefault(E_TOTAL + FFN_UNITS + 1, []).append(lambda: add_residual(0))
            for i in range(N_UNITS + 1):
                if i < N_UNITS:
                    finish_hidden(i)
                if i:
                    hidden_lo(i - 1)
                for what in extras.get(i, []):
                    what()
            add_residual(1)

        @block.scalar
        def _(act):
            A = nc.scalar
            act.wait_ge(loaded, 16 * N_EARLY)
            A.copy(up_hi[:, 0:1024], s_up[:]).then_inc(w_hi, 1)
            A.copy(dn_hi[:, 0:512], s_dn[:]).then_inc(w_hi, 1)
            for b in range(B):
                act.wait_ge(x1_ready, b + 1)
                A.copy(x1_hi[:, cols(b)], x1[:, cols(b)]).then_inc(x1_hi_ready, 1)
            for b in range(B):
                act.wait_ge(logits, B)
                A.activation(e_neg[:, b], MISC[:, 32 * b:32 * b + 32].rearrange("p (t e) -> p t e", t=KB),
                             ACT.Exp, scale=-1.0).then_inc(expneg, 1)

            def activate(i):
                kind, b, w = UNITS[i]
                r = i % RING
                act.wait_ge(up_full, i + 1)
                if i >= RING:
                    if UNITS[i - RING][0] != "zone":
                        act.wait_ge(h_ready, i - RING + 1)
                    else:
                        act.wait_ge(lo_done, i - RING + 1)
                if kind == "shared":
                    func, scale = ACT.Tanh, 0.5
                elif kind == "routed":
                    func, scale = ACT.Gelu, 1.0
                else:
                    func, scale = ACT.Gelu_apprx_tanh, 1.0
                A.activation(act_out[r][:], psum[:, 2 * r, :], func, scale=scale).then_inc(act_done, 1)

            def hidden_hi(i):
                r = i % RING
                if UNITS[i][0] == "zone":
                    src = act_out[r]
                    act.wait_ge(act_done, i + 1)
                else:
                    src = hidden[r]
                    act.wait_ge(h_ready, i + 1)
                if i >= RING:
                    act.wait_ge(down_done, i - RING + 1)
                    act.wait_ge(lo_done, i - RING + 1)
                A.copy(h_hi[r][:], src[:]).then_inc(hi_done, 1)

            def gates_t_copy(b):
                act.wait_ge(gateT_full, b + 1)
                if b == 0:
                    act.wait_ge(setup_zero, 1)
                A.copy(gates_t[b][0:2 * EXPERTS, :], MISC[0:2 * EXPERTS, :]).then_inc(gateT_copied, 1)

            def finish_experts(b):
                act.wait_ge(down_done, EXP_UNITS * (b + 1))
                A.activation(x2[:, cols(b)], OUT, ACT.Identity, scale=1.0 / 16.0,
                             accum_out=pooled[:, b:b + 1]).then_inc(x2_ready, 1)
                act.wait_ge(x2_ready, b + 1)
                A.copy(x2_hi[:, cols(b)], x2[:, cols(b)]).then_inc(x2_hi_ready, 1)

            def router_tanh(b):
                act.wait_ge(z_hid, b + 1)
                A.activation(hid[:, b:b + 1], MISC[0:RH, 64:65], ACT.Tanh, scale=1.0 / S,
                             bias=small[0:RH, W_B1:W_B1 + 1]).then_inc(z_tanh, 1)

            def routed_weights():
                A.copy(up_hi[:, 1024:2048], r_up[:]).then_inc(w_hi, 1)
                act.wait_ge(setup_zero, 1)
                A.copy(sel_e[0:2 * EXPERTS, :, :],
                       small[0:2 * EXPERTS, W_SEL:W_END].rearrange("p (e m) -> p e m", e=EXPERTS)).then_inc(sel_ready, 1)

            def routed_down():
                A.copy(dn_hi[:, 512:1536], r_dn[:]).then_inc(w_hi, 1)

            extras = {0: [routed_weights], 1: [routed_down],
                      2: [lambda: gates_t_copy(0)], 6: [lambda: gates_t_copy(1)]}
            for b in range(B):
                o = EXP_UNITS * (b + 1)
                extras.setdefault(o, []).append(lambda b=b: finish_experts(b))
                extras.setdefault(o + 3, []).append(lambda b=b: router_tanh(b))
            for i in range(N_UNITS + 1):
                if i < N_UNITS:
                    activate(i)
                if i:
                    hidden_hi(i - 1)
                for what in extras.get(i, []):
                    what()

        @block.tensor
        def _(pe):
            T = nc.tensor
            for b in range(B):
                pe.wait_ge(onorm_ready, b + 1)
                if b == 0:
                    pe.wait_ge(loaded, 16 * N_EARLY)
                T.matmul(psum[:, b, :], small[:, W_OUT:W_OUT + D], o_norm[:, cols(b)],
                         start=True, stop=True).then_inc(proj_ready, 1)
            pe.wait_ge(temb_ready, B)
            for b in range(B):
                pe.wait_ge(x1_ready, b + 1)
                for t in range(KB):
                    o = MISC[:, 32 * b + t * EXPERTS:32 * b + (t + 1) * EXPERTS]
                    T.matmul(o, x1[:, b * S + t * P:b * S + (t + 1) * P], small[:, W_R:W_R + EXPERTS],
                             start=True, stop=False)
                    last = T.matmul(o, temb[:, b, :], small[:, W_R + EXPERTS:W_R + 2 * EXPERTS],
                                    start=False, stop=True)
                last.then_inc(logits, 1)

            def three(o, hi, lo, x_hi, x_lo, start, stop):
                T.matmul(o, hi, x_hi, start=start, stop=False)
                T.matmul(o, lo, x_hi, start=False, stop=False)
                return T.matmul(o, hi, x_lo, start=False, stop=stop)

            def up(i):
                kind, b, w = UNITS[i]
                r = i % RING
                if i >= RING:
                    if UNITS[i - RING][0] != "zone":
                        pe.wait_ge(h_ready, i - RING + 1)
                    else:
                        pe.wait_ge(act_done, i - RING + 1)
                if kind == "zone":
                    z, m = b * TOPZ + w // ZM, w % ZM
                    if w == 0:
                        pe.wait_ge(x2_lo_ready, b + 1)
                    if m == 0:
                        pe.wait_ge(zone_hi, 2 * z + 2)
                        pe.wait_ge(zone_lo, z + 1)
                    c = slice(m * P, (m + 1) * P)
                    last = three(psum[:, 2 * r, :], wa_hi[z % 2][:, c], wa_lo[z % 2][:, c],
                                 x2_hi[:, cols(b)], x2_lo[:, cols(b)], True, True)
                else:
                    if w == 0:
                        pe.wait_ge(x1_lo_ready, b + 1)
                        pe.wait_ge(x1_ready, B)
                        pe.wait_ge(w_lo, 1 if kind == "shared" else 3)
                    for t, c in enumerate(up_cols(kind, w)):
                        last = three(psum[:, 2 * r + t, :], up_hi[:, c:c + P], up_lo[:, c:c + P],
                                     x1_hi[:, cols(b)], x1_lo[:, cols(b)], True, True)
                    if kind == "routed":
                        if w == 0:
                            pe.wait_ge(gateT_copied, b + 1)
                            pe.wait_ge(sel_ready, 1)
                        last = T.matmul(psum[:, 2 * r + 1, :], sel_e[:, w, :], gates_t[b][:], start=True, stop=True)
                last.then_inc(up_full, 1)

            def down(i):
                kind, b, w = UNITS[i]
                r = i % RING
                pe.wait_ge(lo_done, i + 1)
                first = w == 0 and kind != "routed"
                final = i + 1 == N_UNITS or (UNITS[i + 1][2] == 0 and UNITS[i + 1][0] != "routed")
                if kind == "zone":
                    z, m = b * TOPZ + w // ZM, w % ZM
                    hi, lo = wb_hi[z % 2][:, m, :], wb_lo[z % 2][:, m, :]
                    if first:
                        if b == 0:
                            pe.wait_ge(x2_ready, B)
                        else:
                            pe.wait_ge(y_ready, b)
                else:
                    c = dn_col(kind, w)
                    hi, lo = dn_hi[:, c:c + D], dn_lo[:, c:c + D]
                    if w == 0:
                        pe.wait_ge(w_lo, 2 if kind == "shared" else 4)
                    if first and b:
                        pe.wait_ge(x2_ready, b)
                three(OUT, hi, lo, h_hi[r][:], h_lo[r][:], first, final).then_inc(down_done, 1)

            def transpose_gates(b):
                pe.wait_ge(gate_ready, b + 1)
                pe.wait_ge(expneg, B)
                pe.wait_ge(ld_x, 32)
                if b:
                    pe.wait_ge(gateT_copied, b)
                for t in range(KB):
                    last = T.transpose(MISC[0:2 * EXPERTS, t * P:(t + 1) * P], gate_hl[:, b, t, :], ident[:])
                last.then_inc(gateT_full, 1)

            def zone_hidden(b):
                pe.wait_ge(x2_ready, b + 1)
                if b == 0:
                    pe.wait_ge(gateT_copied, B)
                else:
                    pe.wait_ge(z_all, b)
                T.matmul(MISC[0:RH, 64:65], small[:, W_Z1:W_Z1 + RH], pooled[:, b:b + 1],
                         start=True, stop=True).then_inc(z_hid, 1)

            def zone_logits(b):
                pe.wait_ge(z_tanh, b + 1)
                T.matmul(MISC[0:1, 72:80], hid[:, b:b + 1], small[0:RH, W_Z2:W_Z2 + ZONES],
                         start=True, stop=True).then_inc(z_logit, 1)

            def zone_spread(b):
                pe.wait_ge(z_w, b + 1)
                T.matmul(MISC[:, 80:80 + TOPZ], ones_row[:], zw[:, b, :], start=True, stop=True).then_inc(z_bc, 1)

            extras = {4: [lambda: transpose_gates(0)], 8: [lambda: transpose_gates(1)]}
            for b in range(B):
                o = EXP_UNITS * (b + 1) + 2
                for at, what in ((2, zone_hidden), (4, zone_logits), (7, zone_spread)):
                    extras.setdefault(o + at, []).append(lambda b=b, what=what: what(b))
            for i in range(N_UNITS + 2):
                for what in extras.get(i, []):
                    what()
                if i < N_UNITS:
                    up(i)
                if i >= 2:
                    down(i - 2)


N_EARLY = 6


def program(nc, io, out):
    ctx = ExitStack()
    with ctx:
        def sba(name, shape, dt=F32):
            return ctx.enter_context(nc.sbuf_tensor("t_" + name, shape, dt))

        psum = ctx.enter_context(nc.psum_tensor("psum", [P, 8, BANK], F32))
        loaded = ctx.enter_context(nc.semaphore("loaded"))
        packed_out = sba("packed_out", [P, NT])
        packed_sum = sba("packed_sum", [P, NT])
        small = sba("small", [P, W_END])
        s_up = sba("s_up", [P, 1024])
        r_up = sba("r_up", [P, 1024])
        s_dn = sba("s_dn", [P, 512])
        r_dn = sba("r_dn", [P, 1024])
        cond = sba("cond_b", [P, B])
        scratch = nc.dram_tensor("scratch", (GROUPS, P, S), F32, kind="Internal").ap()
        early = [(small[:], io["small"]), (s_up[:], io["s_up"]), (r_up[:], io["r_up"]), (s_dn[:], io["s_dn"]),
                 (r_dn[:], io["r_dn"]), (cond[:], io["condT"])]
        attention(nc, psum, io, scratch, packed_out, packed_sum, early, loaded)
        experts_and_zones(nc, psum, io, (small, s_up, r_up, s_dn, r_dn, cond), packed_out, packed_sum, loaded, out)


def laid_out(inputs):
    a = {k: np.asarray(v) for k, v in inputs.items()}
    consts, cos, sin = host_constants()
    wq = a["L0_attn_w_qkv"]
    small = np.zeros((P, W_END), np.float32)
    small[:, W_OUT:W_OUT + D] = a["L0_attn_w_out"].T
    wr = a["L0_cond2_W_router"]
    small[:, W_R:W_R + EXPERTS] = wr[:, 0:D].T
    small[:, W_R + EXPERTS:W_R + 2 * EXPERTS] = wr[:, D:2 * D].T
    small[:, W_RB:W_RB + EXPERTS] = a["L0_cond2_router_bias"][None, :]
    small[:, W_IOTA:W_IOTA + EXPERTS] = np.arange(EXPERTS)[None, :]
    small[:, W_Z1:W_Z1 + RH] = a["L0_ffn_W1"]
    small[0:RH, W_Z2:W_Z2 + ZONES] = a["L0_ffn_W2"]
    small[0:RH, W_B1] = a["L0_ffn_b1"]
    small[0, W_B2:W_B2 + ZONES] = a["L0_ffn_b2"]
    for e in range(EXPERTS):
        small[[e, EXPERTS + e], W_SEL + e * P:W_SEL + (e + 1) * P] = 1.0
    up = np.stack([a["L0_cond2_s_w1"], a["L0_cond2_s_w3"]], axis=1)
    arrays = {
        "xT": a["x"].reshape(NT, D).T, "condT": a["cond_1024"].T, "L0_cond_weight": a["L0_cond_weight"],
        "w_qkvT": wq.T, "w_rotT": swapped(wq[:2 * D]).T, "cos": cos, "sin": sin, "consts": consts, "small": small,
        "s_up": up.transpose(3, 0, 1, 2).reshape(D, 1024),
        "r_up": a["L0_cond2_r_w1"].transpose(2, 0, 1).reshape(D, 1024),
        "s_dn": a["L0_cond2_s_w2"].reshape(SHARED, D, HID_S // P, P).transpose(3, 0, 2, 1).reshape(P, 512),
        "r_dn": a["L0_cond2_r_w2"].transpose(2, 0, 1).reshape(HID_R, 1024),
        "L0_ffn_Wa": a["L0_ffn_Wa"], "L0_ffn_Wb": a["L0_ffn_Wb"],
    }
    return {k: np.ascontiguousarray(v) for k, v in arrays.items()}


def kernel(**inputs):
    import concourse.bacc as bacc
    from concourse.bass_utils import run_bass_kernel_spmd

    nc = bacc.Bacc("TRN2", target_bir_lowering=False, num_devices=1)
    arrays = laid_out(inputs)
    io = {n: nc.dram_tensor("in_" + n, a.shape, F32, kind="ExternalInput").ap() for n, a in arrays.items()}
    out = nc.dram_tensor("out_0_dram", (D, NT), F32, kind="ExternalOutput").ap()
    program(nc, io, out)
    r = run_bass_kernel_spmd(nc, [{"in_" + n: a for n, a in arrays.items()}], core_ids=[0])
    return np.ascontiguousarray(r.results[0]["out_0_dram"].T).reshape(B, S, D)
```

```python
import numpy as np
from contextlib import ExitStack

import concourse.bass as bass
from concourse import mybir

ALU = mybir.AluOpType
ACT = mybir.ActivationFunctionType
AX = mybir.AxisListType
F32 = mybir.dt.float32
F32R = mybir.dt.float32r
BF16 = mybir.dt.bfloat16
U32 = mybir.dt.uint32

P = 128
B, S, D = 2, 512, 128
NT = B * S
H, HD = 16, 8
HG = 4
NG = H // HG
GROUPS = B * NG
KB = S // P
VC = 2 * HD
MXU = 12
STU = 6
BIG = -1.0e30
BANK = 512

EXPERTS, SHARED, HID_S, HID_R = 8, 2, 256, 128
ZONES, TOPZ, DFF, RH = 8, 3, 512, 32

MX_UNITS = [(0, (0, 1)), (0, (2, 3)), (1, (0, 1)), (1, (2, 3))] + \
           [(qb, (j,)) for qb in (2, 3) for j in range(HG)]

SH_UNITS = SHARED * HID_S // P
EXP_UNITS = SH_UNITS + EXPERTS
ZM = DFF // P
FFN_UNITS = TOPZ * ZM
E_TOTAL = B * EXP_UNITS
STEPS = B * TOPZ
UNITS = [u for b in range(B) for u in
         [("shared", b, i) for i in range(SH_UNITS)] + [("routed", b, e) for e in range(EXPERTS)]] + \
        [("zone", b, i) for b in range(B) for i in range(FFN_UNITS)]
N_UNITS = len(UNITS)
RING = 3
LO_POOL = range(SH_UNITS, EXP_UNITS + SH_UNITS)
LAG = 3
ZSLOTS = 4
UP_COLS = SHARED * 2 * HID_S + EXPERTS * HID_R
DN_COLS = (SH_UNITS + EXPERTS) * D

C_SEL, C_ID, C_MASK, C_ONE, C_SELE = 0, 512, 640, 768, 1024
C_END = C_SELE + EXPERTS * P
W_OUT, W_R, W_RT, W_RB, W_IOTA, W_Z1, W_Z2, W_B1, W_B2, W_ID = 0, 128, 136, 168, 176, 184, 216, 224, 225, 233
W_END = W_ID + P


def f32_of(ap):
    return ap.bitcast(F32)


def spread(units, others):
    total = sum(c for c, _ in others)
    order, done, k = [], 0.0, 0
    for cost, what in others:
        while k < len(units) and done >= k * total / len(units):
            order.append(units[k])
            k += 1
        order.append(what)
        done += cost
    return order + units[k:]


def program(nc, io, scratch, out):
    ctx = ExitStack()
    with ctx:
        def sb(name, shape, dt=F32):
            return ctx.enter_context(nc.sbuf_tensor("t_" + name, shape, dt))

        def sem(name):
            return ctx.enter_context(nc.semaphore(name))

        psum = ctx.enter_context(nc.psum_tensor("psum", [P, 8, BANK], F32))
        MX, ST, PV, QM = psum[:, 0:2, :], psum[:, 2:6, :], psum[:, 6, :], psum[:, 7, :]
        OUT, MISC = psum[:, 7, :], psum[:, 6, :]

        cond = sb("cond", [P, B])
        ys = sb("ys", [P, B])
        ys_sq = sb("ys_sq", [P, B])
        dvar = sb("dvar", [P, B])
        dexp = sb("dexp", [P, B])
        dinv = sb("dinv", [P, B])
        w_cond_sq = sb("w_cond_sq", [P, D])
        xT = sb("xT", [P, NT])
        small = sb("small", [P, W_END])
        sel = sb("sel", [P, NG, 4, P], F32R)
        ident_r = sb("ident_r", [P, P], F32R)
        ident_b = sb("ident_b", [P, P], BF16)
        mask_b = sb("mask_b", [P, P], BF16)
        qk_hi = sb("qk_hi", [P, 2, S], F32R)
        q_mov = sb("q_mov", [P, 2, S], F32R)
        stacked = sb("stacked", [P, 2 * GROUPS, S], F32R)
        v_all = sb("v_all", [P, (GROUPS * KB * HG + 1) * VC])
        q_pad = [sb(f"q_pad{s}", [P, HG, S], F32R) for s in range(2)]
        k_pad = [sb(f"k_pad{s}", [P, HG, S], F32R) for s in range(2)]
        neg_max = [sb(f"neg_max{s}", [P, KB, HG]) for s in range(2)]
        max_pad = [sb(f"max_pad{s}", [P, KB, HG, 32], BF16) for s in range(2)]
        probs = [sb(f"probs{s}", [P, 3, HG, BANK]) for s in range(2)]
        o_sb = [sb(f"o_sb{s}", [P, S]) for s in range(2)]
        packed_out = sb("packed_out", [P, S])
        packed_sum = sb("packed_sum", [P, S])
        x1 = sb("x1", [P, NT])
        raw = sb("raw", [P, UP_COLS + DN_COLS])
        up_hi = sb("up_hi", [P, UP_COLS], F32R)
        up_lo = sb("up_lo", [P, UP_COLS], F32R)
        dn_hi = sb("dn_hi", [P, DN_COLS], F32R)
        dn_lo = sb("dn_lo", [P, DN_COLS], F32R)

        p0 = probs[0][:].rearrange("p c j k -> p (c j k)")
        p1 = probs[1][:].rearrange("p c j k -> p (c j) k")
        cos_t, sin_t = p0[:, 0:S], p0[:, S:2 * S]
        w_qkv, w_rot = p0[:, 2 * S:2 * S + 3 * D], p0[:, 3 * S:3 * S + 2 * D]
        w_cond = p0[:, 3 * S + 2 * D:3 * S + 3 * D]
        consts = p0[:, 4 * S:4 * S + C_END]
        xs, xc = p1[:, 0:2, :], p1[:, 2:4, :]
        rope_c, rope_s, roped = p1[:, 4:6, :], p1[:, 6:8, :], p1[:, 8:10, :]
        qk_lo = q_mov

        flat = [t[:].rearrange("p c j k -> p (c j) k") for t in probs]
        zone_a, x12, y = flat[0][:, 0:8, :], flat[0][:, 8:10, :], flat[0][:, 10:12, :]
        zone_b, x2 = flat[1][:, 0:8, :], flat[1][:, 8:10, :]
        x1_hi, x1_lo = stacked[:, 0:2, :], stacked[:, 2:4, :]
        x2_hi, x2_lo = stacked[:, 4:6, :], stacked[:, 6:8, :]
        zone_w = [stacked[:, 8:12, :], stacked[:, 12:16, :], k_pad[0][:], k_pad[1][:]]
        h_hi = [q_pad[0][:, r, :] for r in range(RING)]
        h_lo = [q_pad[1][:, r, :] for r in range(RING)]
        gates_t = [q_pad[b][:, RING, :] for b in range(B)]
        sel_e = sel[:].rearrange("p g t m -> p (g t) m")[:, 0:EXPERTS, :]
        act_out = [raw[:, r * S:(r + 1) * S] for r in range(RING)]
        hidden = [raw[:, (RING + r) * S:(RING + r + 1) * S] for r in range(RING)]
        silu = raw[:, 2 * RING * S:(2 * RING + 1) * S]

        temb = sb("temb", [P, B, P])
        shape_g = [P, B, KB, EXPERTS]
        e_neg, e_one, sig, rank = (sb(x, shape_g) for x in ("e_neg", "e_one", "sig", "rank"))
        top = sb("top", [P, B, KB, 8])
        top_i = sb("top_i", [P, B, KB, 8], U32)
        top_f = sb("top_f", [P, B, KB, 2])
        eq0, eq1, chosen, s_sel = (sb(x, shape_g) for x in ("eq0", "eq1", "chosen", "s_sel"))
        denom, okay, denom_e, inv_d, scale_s, scale_c = (
            sb(x, [P, B, KB]) for x in ("denom", "okay", "denom_e", "inv_d", "scale_s", "scale_c"))
        part_s, part_c, gate = (sb(x, shape_g) for x in ("part_s", "part_c", "gate"))
        gate_hl = sb("gate_hl", [P, B, KB, 2 * EXPERTS])
        euler = sb("euler", [P, KB, EXPERTS])
        pooled = sb("pooled", [P, B])
        hid = sb("hid", [RH, B])
        zl = sb("zl", [1, B, ZONES])
        ztop = sb("ztop", [1, B, 8])
        zidx = sb("zidx", [1, B, 8], U32)
        zdiff = sb("zdiff", [1, B, TOPZ])
        zexp = sb("zexp", [1, B, TOPZ])
        zsum = sb("zsum", [1, B])
        zinv = sb("zinv", [1, B])
        zw = sb("zw", [1, B, TOPZ])
        ones_row = sb("ones_row", [1, P])
        zw_all = sb("zw_all", [P, B, TOPZ])

        names = """
            ld_cond ld_x1 ld_proj ld_rot ld_const ld_raw ld_small ld_zones
            pads_early ys_ready sq_ready dsum_ready dvar_ready dinv_ready xs_ready cond_ready xc_ready
            qk_ready v_ready v_copied rope_ready roped_ready hi_ready lo_ready sel_zero pad0_zero pads_zero v_ones
            const_ready rep_ready rep_copied mx_full mx_reduced mhi_ready m_ready qm_full qm_copied st_full
            exp_done masked pv_full pv_copied packed
            temb_ready w_hi w_lo inv_ready onorm_ready proj_ready x1_ready x1_hi_ready x1_lo_ready sele_zero
            sele_ready gates_zero logits expneg gate_step gate_ready gateT_full gateT_copied
            up_full act_done silu_done h_ready hi_done lo_done down_done x2_ready x2_hi_ready x2_lo_ready
            x12_ready z_hid z_tanh z_logit z_step z_diff z_exp z_w z_bc z_all a_hi b_hi a_lo b_lo y_ready stored_y
            euler_ready""".split()
        sems = {n: sem(n) for n in names}
        (ld_cond, ld_x1, ld_proj, ld_rot, ld_const, ld_raw, ld_small, ld_zones,
         pads_early, ys_ready, sq_ready, dsum_ready, dvar_ready, dinv_ready, xs_ready, cond_ready, xc_ready,
         qk_ready, v_ready, v_copied, rope_ready, roped_ready, hi_ready, lo_ready, sel_zero, pad0_zero, pads_zero,
         v_ones, const_ready, rep_ready, rep_copied, mx_full, mx_reduced, mhi_ready, m_ready, qm_full, qm_copied,
         st_full, exp_done, masked, pv_full, pv_copied, packed,
         temb_ready, w_hi, w_lo, inv_ready, onorm_ready, proj_ready, x1_ready, x1_hi_ready, x1_lo_ready, sele_zero,
         sele_ready, gates_zero, logits, expneg, gate_step, gate_ready, gateT_full, gateT_copied,
         up_full, act_done, silu_done, h_ready, hi_done, lo_done, down_done, x2_ready, x2_hi_ready, x2_lo_ready,
         x12_ready, z_hid, z_tanh, z_logit, z_step, z_diff, z_exp, z_w, z_bc, z_all, a_hi, b_hi, a_lo, b_lo, y_ready,
         stored_y, euler_ready) = (sems[n] for n in names)
        q_padded = [sem(f"q_padded{s}") for s in range(2)]
        k_padded = [sem(f"k_padded{s}") for s in range(2)]
        stored = [sem(f"stored{s}") for s in range(2)]
        block = ctx.enter_context(nc.Block())

        def cols(b):
            return slice(b * S, (b + 1) * S)

        def up_cols(kind, i):
            if kind == "shared":
                e, m = divmod(i, HID_S // P)
                return [(2 * e + t) * HID_S + m * P for t in range(2)]
            return [SHARED * 2 * HID_S + i * P]

        def dn_col(kind, i):
            return i * D if kind == "shared" else (SH_UNITS + i) * D

        def pair_of(i):
            r = 0 if i < SH_UNITS else i % RING
            return psum[:, 2 * r:2 * r + 2, :]

        def run(extras, i):
            for what in extras.get(i, []):
                what()

        @block.sync
        def _(sp):
            sp.dma_start(cond[:], io["condT"]).then_inc(ld_cond, 16)
            sp.dma_start(w_cond, io["L0_cond_weight"]).then_inc(ld_cond, 16)
            sp.dma_start(xT[:, cols(0)], io["xT"][:, cols(0)]).then_inc(ld_cond, 16)
            sp.dma_start(w_qkv, io["w_qkvT"]).then_inc(ld_proj, 16)
            sp.dma_start(w_rot, io["w_rotT"]).then_inc(ld_proj, 16)
            sp.dma_start(p0[:, 0:2 * S], io["rotary"]).then_inc(ld_rot, 16)
            sp.dma_start(consts, io["consts"]).then_inc(ld_const, 16)
            sp.dma_start(xT[:, cols(1)], io["xT"][:, cols(1)]).then_inc(ld_x1, 16)
            sp.dma_start(raw[:], io["experts"]).then_inc(ld_raw, 16)
            sp.dma_start(small[:], io["small"]).then_inc(ld_small, 16)

            def pad_q(n):
                s = n % 2
                sp.wait_ge(rep_copied, 2 * n + 1)
                if n >= 2:
                    sp.wait_ge(mx_full, (n - 1) * MXU)
                for j in range(HG):
                    q = slice(32 * j, 32 * j + 32)
                    sp.dma_start(f32_of(q_pad[s][q, j, :]), f32_of(stacked[q, 2 * n, :])).then_inc(q_padded[s], 16)

            def pad_k(n):
                s = n % 2
                sp.wait_ge(rep_copied, 2 * n + 2)
                if n >= 2:
                    sp.wait_ge(st_full, (n - 1) * STU)
                for j in range(HG):
                    q = slice(32 * j, 32 * j + 32)
                    sp.dma_start(f32_of(k_pad[s][q, j, :]), f32_of(stacked[q, 2 * n + 1, :])).then_inc(k_padded[s], 16)

            def store_sums(n):
                sp.wait_ge(pv_copied, n + 1)
                sp.dma_start(scratch[n], o_sb[n % 2][:]).then_inc(stored[n % 2], 16)

            sp.wait_ge(pad0_zero, 1)
            pad_q(0)
            sp.wait_ge(pads_zero, 1)
            pad_q(1)
            pad_k(0)
            pad_q(2)
            pad_k(1)
            for n in range(GROUPS):
                if n + 3 < GROUPS:
                    pad_q(n + 3)
                if n + 2 < GROUPS:
                    pad_k(n + 2)
                store_sums(n)
                if n % NG == NG - 1:
                    b = n // NG
                    for s in range(2):
                        sp.wait_ge(stored[s], 16 * (n + 1) // 2)
                    if b:
                        sp.wait_ge(onorm_ready, b)
                        sp.wait_ge(proj_ready, b)
                    rows = scratch[b * NG:(b + 1) * NG].rearrange("g (j r) t -> (g j) r t", j=HG)
                    for dst, r0 in ((packed_sum, HD), (packed_out, 0)):
                        sp.dma_start(dst[:], rows[:, r0:r0 + HD, :]).then_inc(packed, 16)
            sp.wait_ge(pv_full, GROUPS)
            for lo in range(0, ZONES, 4):
                sp.dma_start(zone_a[:, lo:lo + 4, :],
                             io["L0_ffn_Wa"][lo:lo + 4].rearrange("e p f -> p e f")).then_inc(ld_zones, 16)
                sp.dma_start(zone_b[:, lo:lo + 4, :].rearrange("p e (m d) -> p e m d", m=ZM),
                             io["L0_ffn_Wb"][lo:lo + 4].rearrange("e (m p) d -> p e m d", p=P)).then_inc(ld_zones, 16)
            for b in range(B):
                sp.wait_ge(y_ready, b + 1)
                sp.dma_start(out[:, cols(b)], y[:, b, :]).then_inc(stored_y, 16)
            sp.wait_ge(stored_y, 16 * B)

        @block.gpsimd
        def _(pool):
            G = nc.gpsimd
            for s in range(2):
                last = G.memset(max_pad[s][:], 0.0)
            last.then_inc(pads_early, 1)
            G.memset(f32_of(sel[:]), 0.0).then_inc(sel_zero, 1)
            G.memset(dexp[:], -0.5).then_inc(sq_ready, 1)
            pool.wait_ge(ld_cond, 48)
            G.tensor_tensor(w_cond_sq[:], w_cond, w_cond, ALU.mult).then_inc(sq_ready, 1)
            pool.wait_ge(sq_ready, 2)
            pool.wait_ge(dvar_ready, 1)
            G.tensor_tensor(dinv[:], dvar[:], dexp[:], ALU.pow).then_inc(dinv_ready, 1)
            G.memset(f32_of(k_pad[0][:]), 0.0)
            G.memset(v_all[:], 1.0).then_inc(v_ones, 1)
            G.memset(f32_of(q_pad[1][:]), 0.0)
            G.memset(f32_of(k_pad[1][:]), 0.0).then_inc(pads_zero, 1)
            G.memset(ones_row[:], 1.0)
            G.memset(euler[:], float(np.e)).then_inc(euler_ready, 1)

            chunks = [(up_hi, up_lo, c, c) for c in range(0, UP_COLS, S)] + \
                     [(dn_hi, dn_lo, c, UP_COLS + c) for c in range(0, DN_COLS, S)]

            def split(k):
                hi, lo, c, at = chunks[k]
                if k == 0:
                    pool.wait_ge(ld_raw, 16)
                G.tensor_copy(hi[:, c:c + S], raw[:, at:at + S]).then_inc(w_hi, 1)
                pool.wait_ge(w_hi, k + 1)
                G.tensor_tensor(lo[:, c:c + S], raw[:, at:at + S], f32_of(hi[:, c:c + S]),
                                ALU.subtract).then_inc(w_lo, 1)

            split(0)
            for i in range(2):
                pool.wait_ge(rope_ready, 4 + 2 * i + 2)
                pool.wait_ge(lo_ready, 2)
                G.tensor_tensor(roped[:, i, :], rope_c[:, i, :], rope_s[:, i, :], ALU.add).then_inc(roped_ready, 1)
            for i in range(2):
                pool.wait_ge(hi_ready, 2 + i + 1)
                pool.wait_ge(rep_ready, 2 * NG)
                G.tensor_tensor(qk_lo[:, i, :], roped[:, i, :], f32_of(qk_hi[:, i, :]),
                                ALU.subtract).then_inc(lo_ready, 1)
            next_split = 1
            pool.wait_ge(rep_ready, 2 * GROUPS)
            G.memset(f32_of(sel_e), 0.0).then_inc(sele_zero, 1)
            for n in range(GROUPS):
                for c in range(3):
                    pool.wait_ge(exp_done, STU * n + 2 * c + 2)
                    for o in ((0,) if c < 2 else (0, 3 * P)):
                        tri = probs[n % 2][:, c, :, o:o + P]
                        last = G.affine_select(out=tri, in_=tri, compare_op=ALU.is_ge, fill=0.0, base=0,
                                               pattern=[[0, HG], [1, P]], channel_multiplier=-1)
                    last.then_inc(masked, 1)
                    if c == 2 and next_split < len(chunks):
                        split(next_split)
                        next_split += 1
                if n == GROUPS - 2:
                    for b in range(B):
                        pool.wait_ge(mx_full, GROUPS * MXU)
                        G.memset(f32_of(gates_t[b]), 0.0).then_inc(gates_zero, 1)
            for i in LO_POOL:
                pool.wait_ge(hi_done, i + 1)
                pool.wait_ge(lo_done, i)
                pool.wait_ge(down_done, i - RING + 1)
                G.tensor_tensor(h_lo[i % RING], hidden[i % RING], f32_of(h_hi[i % RING]),
                                ALU.subtract).then_inc(lo_done, 1)
            for b in range(B):
                pool.wait_ge(x1_ready, b + 1)
                pool.wait_ge(x2_ready, b + 1)
                G.tensor_tensor(x12[:, b, :], x1[:, cols(b)], x2[:, b, :], ALU.add).then_inc(x12_ready, 1)
                pool.wait_ge(z_diff, b + 1)
                G.tensor_tensor(zexp[:, b, :], euler[0:1, 0, 0:TOPZ], zdiff[:, b, :], ALU.pow).then_inc(z_exp, 1)
                for k in range(TOPZ):
                    z = b * TOPZ + k
                    w = zone_w[z % ZSLOTS]
                    zone = G.value_load(zidx[0:1, b, k:k + 1], min_val=0, max_val=ZONES - 1)
                    pool.wait_ge(a_hi, z + 1)
                    G.tensor_tensor(w[:, 1, :], zone_a[:, bass.ds(zone, 1), :], f32_of(w[:, 0, :]),
                                    ALU.subtract).then_inc(a_lo, 1)
                    pool.wait_ge(z_all, b + 1)
                    G.tensor_tensor(w[:, 2, :], zone_b[:, bass.ds(zone, 1), :],
                                    zw_all[:, b, k:k + 1].broadcast_to([P, DFF]), ALU.mult).then_inc(b_hi, 1)

        @block.vector
        def _(dve):
            V = nc.vector
            V.memset(f32_of(q_pad[0][:]), 0.0).then_inc(pad0_zero, 1)
            dve.wait_ge(ld_cond, 48)
            V.tensor_scalar(ys[:], cond[:], float(np.float32(1.0) / np.sqrt(np.float32(D))), None,
                            ALU.mult).then_inc(ys_ready, 1)
            dve.wait_ge(ys_ready, 1)
            V.tensor_scalar(xs[:, 0, :], xT[:, cols(0)], ys[:, 0:1], None, ALU.mult).then_inc(xs_ready, 1)
            V.tensor_tensor(ys_sq[:], ys[:], ys[:], ALU.mult).then_inc(ys_ready, 1)
            dve.wait_ge(dsum_ready, 1)
            V.tensor_scalar(dvar[:], QM[:, 0:B], 1e-8, None, ALU.add).then_inc(dvar_ready, 1)
            dve.wait_ge(dinv_ready, 1)

            def modulate(b):
                dve.wait_ge(cond_ready, b + 1)
                V.tensor_scalar(xc[:, b, :], psum[:, 6 + b, :], dinv[:, b:b + 1], None, ALU.mult).then_inc(xc_ready, 1)

            def rotate(b, i):
                dve.wait_ge(qk_ready, 2 * b + i + 1)
                if b:
                    dve.wait_ge(roped_ready, i + 1)
                V.tensor_tensor(rope_c[:, i, :], ST[:, 2 * i, :], cos_t, ALU.mult).then_inc(rope_ready, 1)
                V.tensor_tensor(rope_s[:, i, :], ST[:, 2 * i + 1, :], sin_t, ALU.mult).then_inc(rope_ready, 1)

            def reduce_max(n, u):
                s = n % 2
                qb, heads = MX_UNITS[u]
                width = P * (qb + 1)
                dve.wait_ge(mx_full, MXU * n + u + 1)
                src = MX[:, u % 2, :]
                if len(heads) == 2:
                    src = src.rearrange("p (h k) -> p h k", h=2)
                    out_ = neg_max[s][:, qb, heads[0]:heads[0] + 2]
                    V.tensor_reduce(out_, src[:, :, 0:width], AX.X, ALU.max, negate=True).then_inc(mx_reduced, 1)
                else:
                    out_ = neg_max[s][:, qb, heads[0]:heads[0] + 1]
                    V.tensor_reduce(out_, src[:, 0:width], AX.X, ALU.max, negate=True).then_inc(mx_reduced, 1)

            def place_max(n):
                s = n % 2
                dve.wait_ge(mx_reduced, MXU * (n + 1))
                if n >= 2:
                    dve.wait_ge(qm_full, n - 1)
                else:
                    dve.wait_ge(pads_early, 1)
                V.tensor_copy(max_pad[s][:, :, :, 0], neg_max[s][:]).then_inc(mhi_ready, 1)
                dve.wait_ge(mhi_ready, n + 1)
                V.tensor_tensor(max_pad[s][:, :, :, 1], neg_max[s][:], max_pad[s][:, :, :, 0],
                                ALU.subtract).then_inc(m_ready, 1)

            modulate(0)
            dve.wait_ge(ld_rot, 16)
            for i in range(2):
                rotate(0, i)
                dve.wait_ge(rope_ready, 2 * i + 2)
                V.tensor_tensor(roped[:, i, :], rope_c[:, i, :], rope_s[:, i, :], ALU.add).then_inc(roped_ready, 1)
                if i == 0:
                    dve.wait_ge(ld_x1, 16)
                    V.tensor_scalar(xs[:, 1, :], xT[:, cols(1)], ys[:, 1:2], None, ALU.mult).then_inc(xs_ready, 1)
                dve.wait_ge(hi_ready, i + 1)
                V.tensor_tensor(qk_lo[:, i, :], roped[:, i, :], f32_of(qk_hi[:, i, :]),
                                ALU.subtract).then_inc(lo_ready, 1)
            modulate(1)
            for n in range(2):
                for u in range(MXU):
                    reduce_max(n, u)
                    if (n, u) in ((0, 9), (0, 11)):
                        rotate(1, (u - 9) // 2)
                place_max(n)
            def normalise(b, part, parts):
                c = slice(part * S // parts, (part + 1) * S // parts)
                dve.wait_ge(packed, 32 * (b + 1))
                done = b * P + (part + 1) * P // parts
                V.reciprocal(packed_sum[:, c], packed_sum[:, c]).then_inc(inv_ready, P // parts)
                if part == parts - 1:
                    dve.wait_ge(inv_ready, done)
                    V.tensor_tensor(packed_out[:], packed_out[:], packed_sum[:], ALU.mult).then_inc(onorm_ready, 1)

            def residual(b):
                dve.wait_ge(proj_ready, b + 1)
                bank = psum[:, 0, :] if b == 0 else MISC
                V.tensor_tensor(x1[:, cols(b)], bank, xT[:, cols(b)], ALU.add).then_inc(x1_ready, 1)

            def x1_low(b):
                dve.wait_ge(x1_hi_ready, b + 1)
                V.tensor_tensor(x1_lo[:, b, :], x1[:, cols(b)], f32_of(x1_hi[:, b, :]),
                                ALU.subtract).then_inc(x1_lo_ready, 1)

            steps = [0]

            def step(ins):
                steps[0] += 1
                ins.then_inc(gate_step, 1)
                dve.wait_ge(gate_step, steps[0])

            def gates(b, part):
                sg, ch = sig[:, b], chosen[:, b]
                if part == 0:
                    dve.wait_ge(expneg, b + 1)
                    step(V.tensor_scalar(e_one[:, b], e_neg[:, b], 1.0, None, ALU.add))
                    step(V.reciprocal(sg, e_one[:, b]))
                    bias = small[:, W_RB:W_RB + EXPERTS].unsqueeze(1).broadcast_to([P, KB, EXPERTS])
                    step(V.tensor_tensor(rank[:, b], sg, bias, ALU.add))
                    for t in range(KB):
                        last = V.max(top[:, b, t, :], rank[:, b, t, :])
                    step(last)
                elif part == 1:
                    for t in range(KB):
                        last = V.max_index(top_i[:, b, t, :], top[:, b, t, :], rank[:, b, t, :])
                    step(last)
                    step(V.tensor_copy(top_f[:, b], top_i[:, b, :, 0:2]))
                    iota = small[:, W_IOTA:W_IOTA + EXPERTS].unsqueeze(1).broadcast_to([P, KB, EXPERTS])
                    for o, eq in ((0, eq0), (1, eq1)):
                        last = V.tensor_tensor(eq[:, b], iota,
                                               top_f[:, b, :, o:o + 1].broadcast_to([P, KB, EXPERTS]), ALU.is_equal)
                    step(last)
                elif part == 2:
                    step(V.tensor_tensor(ch, eq0[:, b], eq1[:, b], ALU.add))
                    step(V.tensor_tensor(s_sel[:, b], ch, sg, ALU.mult))
                    step(V.tensor_reduce(denom[:, b], s_sel[:, b], AX.X, ALU.add))
                    V.tensor_scalar(okay[:, b], denom[:, b], 1e-9, None, ALU.is_gt)
                    step(V.tensor_scalar(denom_e[:, b], denom[:, b], 1e-9, None, ALU.add))
                    V.tensor_scalar(scale_c[:, b], okay[:, b], -2.0, 2.0, ALU.mult, ALU.add)
                    step(V.reciprocal(inv_d[:, b], denom_e[:, b]))
                else:
                    step(V.scalar_tensor_tensor(scale_s[:, b], inv_d[:, b], 4.0, okay[:, b], ALU.mult, ALU.mult))
                    V.tensor_tensor(part_s[:, b], s_sel[:, b],
                                    scale_s[:, b].unsqueeze(2).broadcast_to([P, KB, EXPERTS]), ALU.mult)
                    step(V.tensor_tensor(part_c[:, b], ch,
                                         scale_c[:, b].unsqueeze(2).broadcast_to([P, KB, EXPERTS]), ALU.mult))
                    step(V.tensor_tensor(gate[:, b], part_s[:, b], part_c[:, b], ALU.add))
                    step(V.tensor_copy(gate_hl[:, b, :, 0:EXPERTS].bitcast(F32R), gate[:, b]))
                    V.tensor_tensor(gate_hl[:, b, :, EXPERTS:], gate[:, b], gate_hl[:, b, :, 0:EXPERTS],
                                    ALU.subtract).then_inc(gate_ready, 1)

            zsteps = [0]

            def zstep(ins):
                zsteps[0] += 1
                ins.then_inc(z_step, 1)
                dve.wait_ge(z_step, zsteps[0])

            def choose_zones(b):
                dve.wait_ge(z_logit, b + 1)
                zstep(V.tensor_tensor(zl[:, b, :], MISC[0:1, 72:80], small[0:1, W_B2:W_B2 + ZONES], ALU.add))
                zstep(V.max(ztop[:, b, :], zl[:, b, :]))
                V.max_index(zidx[:, b, :], ztop[:, b, :], zl[:, b, :])
                V.tensor_scalar(zdiff[:, b, :], ztop[:, b, 0:TOPZ], ztop[:, b, 0:1], None,
                                ALU.subtract).then_inc(z_diff, 1)

            def weigh_zones(b):
                dve.wait_ge(z_exp, b + 1)
                zstep(V.tensor_reduce(zsum[:, b:b + 1], zexp[:, b, :], AX.X, ALU.add))
                zstep(V.reciprocal(zinv[:, b:b + 1], zsum[:, b:b + 1]))
                V.tensor_scalar(zw[:, b, :], zexp[:, b, :], zinv[:, b:b + 1], None, ALU.mult).then_inc(z_w, 1)

            def spread_weights(b):
                dve.wait_ge(z_bc, b + 1)
                V.tensor_copy(zw_all[:, b, :], MISC[:, 80:80 + TOPZ]).then_inc(z_all, 1)

            def zone_b_low(z):
                b, k = divmod(z, TOPZ)
                w = zone_w[z % ZSLOTS]
                dve.wait_ge(z_diff, b + 1)
                zone = V.value_load(zidx[0:1, b, k:k + 1], min_val=0, max_val=ZONES - 1)
                dve.wait_ge(b_hi, z + 1)
                V.scalar_tensor_tensor(w[:, 3, :], zone_b[:, bass.ds(zone, 1), :], zw_all[:, b, k:k + 1],
                                       f32_of(w[:, 2, :]), ALU.mult, ALU.subtract).then_inc(b_lo, 1)

            n_silu = [0]

            def finish_hidden(i):
                kind, b, w = UNITS[i]
                r = i % RING
                if kind == "zone":
                    return
                dve.wait_ge(act_done, i + 1)
                if i >= RING:
                    dve.wait_ge(hi_done, i - RING + 1)
                    dve.wait_ge(lo_done, i - RING + 1)
                pair = pair_of(i)
                if kind == "shared":
                    if i:
                        dve.wait_ge(h_ready, i)
                    V.scalar_tensor_tensor(silu, act_out[r], 1.0, pair[:, 0, :], ALU.add,
                                           ALU.mult).then_inc(silu_done, 1)
                    n_silu[0] += 1
                    dve.wait_ge(silu_done, n_silu[0])
                    V.tensor_tensor(hidden[r], silu, pair[:, 1, :], ALU.mult).then_inc(h_ready, 1)
                else:
                    V.tensor_tensor(hidden[r], act_out[r], pair[:, 1, :], ALU.mult).then_inc(h_ready, 1)

            def hidden_lo(i):
                r = i % RING
                src_ = act_out[r] if UNITS[i][0] == "zone" else hidden[r]
                if i in LO_POOL:
                    return
                dve.wait_ge(hi_done, i + 1)
                if i == LO_POOL.stop:
                    dve.wait_ge(lo_done, i)
                if i >= RING:
                    dve.wait_ge(down_done, i - RING + 1)
                V.tensor_tensor(h_lo[r], src_, f32_of(h_hi[r]), ALU.subtract).then_inc(lo_done, 1)

            def x2_low(b):
                dve.wait_ge(x2_hi_ready, b + 1)
                V.tensor_tensor(x2_lo[:, b, :], x2[:, b, :], f32_of(x2_hi[:, b, :]),
                                ALU.subtract).then_inc(x2_lo_ready, 1)

            def add_residual(b):
                dve.wait_ge(down_done, E_TOTAL + (b + 1) * FFN_UNITS)
                dve.wait_ge(x12_ready, b + 1)
                V.tensor_tensor(y[:, b, :], OUT, x12[:, b, :], ALU.add).then_inc(y_ready, 1)

            for n in range(2, GROUPS):
                for u in range(MXU):
                    reduce_max(n, u)
                    if n == GROUPS - 1 and u % 3 != 2:
                        normalise(0, u // 3 * 2 + u % 3, 8)
                place_max(n)
            dve.wait_ge(ld_small, 16)
            for b in range(B):
                V.tensor_copy(temb[:, b, :], cond[:, b:b + 1].broadcast_to([P, P])).then_inc(temb_ready, 1)
            residual(0)
            x1_low(0)
            dve.wait_ge(w_lo, len(range(0, UP_COLS, S)) + len(range(0, DN_COLS, S)))
            for part in range(4):
                gates(0, part)
            extras = {i: [(lambda i=i: normalise(1, i - 4, 4))] for i in range(4, 8)}
            extras[8] = [lambda: residual(1)]
            extras[9] = [lambda: x1_low(1)]
            for i, parts in ((12, (0, 1)), (13, (2, 3))):
                extras[i] = [lambda part=part: gates(1, part) for part in parts]
            for b in range(B):
                o = EXP_UNITS * (b + 1) + b
                for at, what in ((3, x2_low), (5, choose_zones), (6, weigh_zones), (8, spread_weights)):
                    extras.setdefault(o + at, []).append(lambda b=b, what=what: what(b))
            for z, at in enumerate((21, 22, 24, 34, 36, 39)):
                extras.setdefault(at, []).append(lambda z=z: zone_b_low(z))
            extras.setdefault(E_TOTAL + FFN_UNITS + 1, []).append(lambda: add_residual(0))
            for i in range(N_UNITS + 1):
                if i < N_UNITS:
                    finish_hidden(i)
                if i:
                    hidden_lo(i - 1)
                run(extras, i)
            add_residual(1)

        @block.scalar
        def _(act):
            A = nc.scalar
            act.wait_ge(ld_const, 16)
            act.wait_ge(sel_zero, 1)
            for g in range(NG):
                q = slice(32 * g, 32 * g + 32)
                A.copy(sel[q, g, :, :], consts[q, C_SEL:C_ID].rearrange("p (t m) -> p t m", t=4))
            A.copy(ident_b[:], consts[:, C_ID:C_MASK])
            A.copy(mask_b[:], consts[:, C_MASK:C_ONE]).then_inc(const_ready, 1)

            def take_hi(b, i):
                act.wait_ge(roped_ready, 2 * b + i + 1)
                if b:
                    act.wait_ge(rep_ready, 2 * NG)
                A.copy(qk_hi[:, i, :], roped[:, i, :]).then_inc(hi_ready, 1)

            def copy_v(b):
                act.wait_ge(v_ready, b + 1)
                if b == 0:
                    act.wait_ge(v_ones, 1)
                v_cols = v_all[:, 0:GROUPS * KB * HG * VC].rearrange("p (n k j c) -> p n k j c", n=GROUPS, k=KB, j=HG)
                for kb in range(KB):
                    A.copy(v_cols[:, b * NG:(b + 1) * NG, kb, :, 0:HD],
                           QM[:, kb * P:(kb + 1) * P].rearrange("p (g j d) -> p g j d", g=NG, j=HG)
                           ).then_inc(v_copied, 1)

            def copy_stacked(w):
                i = w % 2
                act.wait_ge(rep_ready, w + 1)
                if i == 0:
                    A.copy(stacked[:, w, :], ST[:, w % 4, :]).then_inc(rep_copied, 1)
                else:
                    A.activation(stacked[:, w, :], ST[:, w % 4, :], ACT.Identity,
                                 bias=consts[:, C_ONE:C_ONE + 1]).then_inc(rep_copied, 1)

            def exp(n, u):
                s = n % 2
                c, h2 = divmod(u, 2)
                act.wait_ge(st_full, STU * n + u + 1)
                if n >= 2 and u == 0:
                    act.wait_ge(pv_full, n - 1)
                w = (BANK, 3 * P, BANK)[c]
                A.activation(probs[s][:, c, 2 * h2:2 * h2 + 2, 0:w],
                             ST[:, 2 * (u % 2):2 * (u % 2) + 2, 0:w], ACT.Exp,
                             scale=float(1.0 / np.sqrt(np.float32(HD)))).then_inc(exp_done, 1)

            def copy_qm(n):
                act.wait_ge(qm_full, n + 1)
                A.copy(q_mov[:, n % 2, :], QM).then_inc(qm_copied, 1)

            def copy_pv(n):
                act.wait_ge(pv_full, n + 1)
                if n >= 2:
                    act.wait_ge(stored[n % 2], 16 * (n // 2))
                A.copy(o_sb[n % 2][:], PV).then_inc(pv_copied, 1)

            def x1_high(b):
                act.wait_ge(x1_ready, b + 1)
                A.copy(x1_hi[:, b, :], x1[:, cols(b)]).then_inc(x1_hi_ready, 1)

            def activate(i):
                kind, b, w = UNITS[i]
                r = i % RING
                act.wait_ge(up_full, i + 1)
                if i == 0:
                    act.wait_ge(w_lo, (UP_COLS + DN_COLS) // S)
                if i >= RING:
                    if UNITS[i - RING][0] != "zone":
                        act.wait_ge(h_ready, i - RING + 1)
                    else:
                        act.wait_ge(lo_done, i - RING + 1)
                if kind == "shared":
                    func, scale = ACT.Tanh, 0.5
                elif kind == "routed":
                    func, scale = ACT.Gelu, 1.0
                else:
                    func, scale = ACT.Gelu_apprx_tanh, 1.0
                A.activation(act_out[r], pair_of(i)[:, 0, :], func, scale=scale).then_inc(act_done, 1)

            def hidden_hi(i):
                r = i % RING
                if UNITS[i][0] == "zone":
                    src_ = act_out[r]
                    act.wait_ge(act_done, i + 1)
                else:
                    src_ = hidden[r]
                    act.wait_ge(h_ready, i + 1)
                if i >= RING:
                    act.wait_ge(down_done, i - RING + 1)
                    act.wait_ge(lo_done, i - RING + 1)
                A.copy(h_hi[r], src_).then_inc(hi_done, 1)

            def gates_t_copy(b):
                act.wait_ge(gateT_full, b + 1)
                act.wait_ge(gates_zero, B)
                A.copy(gates_t[b][0:2 * EXPERTS, :], psum[0:2 * EXPERTS, 7 - b, :]).then_inc(gateT_copied, 1)

            def finish_experts(b):
                act.wait_ge(down_done, EXP_UNITS * (b + 1))
                A.activation(x2[:, b, :], OUT, ACT.Identity, scale=1.0 / 16.0,
                             accum_out=pooled[:, b:b + 1]).then_inc(x2_ready, 1)
                act.wait_ge(x2_ready, b + 1)
                A.copy(x2_hi[:, b, :], x2[:, b, :]).then_inc(x2_hi_ready, 1)

            def zone_a_high(z):
                b, k = divmod(z, TOPZ)
                act.wait_ge(z_diff, b + 1)
                zone = A.value_load(zidx[0:1, b, k:k + 1], min_val=0, max_val=ZONES - 1)
                if z == 0:
                    act.wait_ge(ld_zones, 16 * 4)
                if z >= ZSLOTS:
                    act.wait_ge(down_done, E_TOTAL + ZM * (z - ZSLOTS + 1))
                A.copy(zone_w[z % ZSLOTS][:, 0, :], zone_a[:, bass.ds(zone, 1), :]).then_inc(a_hi, 1)

            def router_tanh(b):
                act.wait_ge(z_hid, b + 1)
                A.activation(hid[:, b:b + 1], MISC[0:RH, 64:65], ACT.Tanh, scale=1.0 / S,
                             bias=small[0:RH, W_B1:W_B1 + 1]).then_inc(z_tanh, 1)

            def exp_of_minus_logits(b):
                act.wait_ge(logits, b + 1)
                bank = psum[:, 1, 0:KB * EXPERTS] if b == 0 else MISC[:, 0:KB * EXPERTS]
                A.activation(e_neg[:, b], bank.rearrange("p (t e) -> p t e", t=KB), ACT.Exp,
                             scale=-1.0).then_inc(expneg, 1)

            take_hi(0, 0)
            take_hi(0, 1)
            for w in range(4):
                copy_stacked(w)
            A.copy(ident_r[:], consts[:, C_ID:C_MASK]).then_inc(const_ready, 1)
            copy_v(0)
            for w in range(4, 2 * NG):
                copy_stacked(w)
            take_hi(1, 0)
            take_hi(1, 1)
            copy_v(1)
            for w in range(2 * NG, 2 * GROUPS):
                copy_stacked(w)
            copy_qm(0)
            act.wait_ge(sele_zero, 1)
            A.copy(sel_e[0:2 * EXPERTS, :, :],
                   consts[0:2 * EXPERTS, C_SELE:C_END].rearrange("p (e m) -> p e m", e=EXPERTS)).then_inc(sele_ready, 1)
            exp(0, 0)
            exp(0, 1)
            for n in range(GROUPS - 1):
                exp(n, 2)
                exp(n, 3)
                if n == GROUPS - 2:
                    x1_high(0)
                copy_qm(n + 1)
                exp(n, 4)
                exp(n, 5)
                if n == GROUPS - 2:
                    exp_of_minus_logits(0)
                exp(n + 1, 0)
                exp(n + 1, 1)
                if n == GROUPS - 2:
                    activate(0)
                copy_pv(n)
            for u in range(2, STU):
                exp(n + 1, u)
            hidden_hi(0)
            activate(1)
            hidden_hi(1)
            gates_t_copy(0)
            activate(2)
            copy_pv(n + 1)
            hidden_hi(2)

            extras = {9: [lambda: x1_high(1)], 15: [lambda: gates_t_copy(1)],
                      11: [lambda: exp_of_minus_logits(1)]}
            for b in range(B):
                o = EXP_UNITS * (b + 1)
                extras.setdefault(o + 2, []).append(lambda b=b: finish_experts(b))
                extras.setdefault(o + 4 + b, []).append(lambda b=b: router_tanh(b))
            for z, at in enumerate((19, 20, 21, 32, 34, 37)):
                extras.setdefault(at, []).append(lambda z=z: zone_a_high(z))
            for i in range(3, N_UNITS):
                activate(i)
                if UNITS[i][0] != "zone":
                    if i > 3:
                        hidden_hi(i - 1)
                else:
                    if UNITS[i - 1][0] != "zone":
                        hidden_hi(i - 1)
                    hidden_hi(i)
                run(extras, i)

        @block.tensor
        def _(pe):
            T = nc.tensor
            pe.wait_ge(pads_early, 1)
            warm = max_pad[0][:].rearrange("p a b c -> p (a b c)")
            for _ in range(WARM):
                T.matmul(ST[:, 0, :], warm[:, 0:P], warm, start=True, stop=True)
            pe.wait_ge(ys_ready, 1)
            pe.wait_ge(xs_ready, 1)
            T.matmul(PV, w_cond, xs[:, 0, :], start=True, stop=True).then_inc(cond_ready, 1)
            pe.wait_ge(ys_ready, 2)
            pe.wait_ge(sq_ready, 2)
            T.matmul(QM[:, 0:B], w_cond_sq[:], ys_sq[:], start=True, stop=True).then_inc(dsum_ready, 1)

            def modulate(b):
                pe.wait_ge(xs_ready, b + 1)
                pe.wait_ge(dvar_ready, 1)
                T.matmul(psum[:, 6 + b, :], w_cond, xs[:, b, :], start=True, stop=True).then_inc(cond_ready, 1)

            def project(b, i):
                pe.wait_ge(xc_ready, b + 1)
                if b == 0:
                    pe.wait_ge(ld_proj, 32)
                else:
                    pe.wait_ge(rep_copied, 2 * NG)
                T.matmul(ST[:, 2 * i, :], w_qkv[:, i * D:(i + 1) * D], xc[:, b, :], start=True, stop=True)
                T.matmul(ST[:, 2 * i + 1, :], w_rot[:, i * D:(i + 1) * D], xc[:, b, :],
                         start=True, stop=True).then_inc(qk_ready, 1)

            def project_v(b):
                if b == 0:
                    pe.wait_ge(xc_ready, 2)
                else:
                    pe.wait_ge(v_copied, KB)
                for kb in range(KB):
                    last = T.matmul(QM[:, kb * P:(kb + 1) * P], xc[:, b, kb * P:(kb + 1) * P],
                                    w_qkv[:, 2 * D:3 * D], start=True, stop=True)
                last.then_inc(v_ready, 1)

            def stack(w):
                b, g, i = w // (2 * NG), w // 2 % NG, w % 2
                if w == 0:
                    pe.wait_ge(const_ready, 1)
                if w % (2 * NG) < 2:
                    pe.wait_ge(lo_ready, 2 * b + i + 1)
                if w % (2 * NG) == 2 or w == 2 * NG:
                    pe.wait_ge(rope_ready, 4 * b + 4)
                if w % (2 * NG) >= 4:
                    pe.wait_ge(rep_copied, w - 3)
                T.matmul(ST[:, w % 4, :], sel[:, g, 2 * i, :], qk_hi[:, i, :], start=True, stop=False)
                T.matmul(ST[:, w % 4, :], sel[:, g, 2 * i + 1, :], qk_lo[:, i, :],
                         start=False, stop=True).then_inc(rep_ready, 1)

            def scores_for_max(n, u):
                s = n % 2
                qb, heads = MX_UNITS[u]
                width = max(2 * P, P * (qb + 1))
                if u == 0:
                    pe.wait_ge(q_padded[s], 16 * HG * (n // 2 + 1))
                    pe.wait_ge(rep_copied, 2 * n + 2)
                if n or u > 1:
                    pe.wait_ge(mx_reduced, MXU * n + u - 1)
                for i, j in enumerate(heads):
                    o = MX[:, u % 2, i * 2 * P:i * 2 * P + width]
                    diag = MX[:, u % 2, i * 2 * P + qb * P:i * 2 * P + (qb + 1) * P]
                    T.matmul(o, q_pad[s][:, j, qb * P:(qb + 1) * P], stacked[:, 2 * n + 1, 0:width],
                             start=True, stop=True)
                    last = T.matmul(diag, mask_b[:], ident_b[:], start=False, stop=True, skip_group_check=True)
                last.then_inc(mx_full, 1)

            def lay_max_under_q(n):
                pe.wait_ge(m_ready, n + 1)
                if n == 0:
                    pe.wait_ge(v_copied, B * KB)
                    pe.wait_ge(const_ready, 2)
                else:
                    pe.wait_ge(qm_copied, n)
                T.matmul(QM, ident_r[:], stacked[:, 2 * n, :], start=True, stop=True)
                for qb in range(KB):
                    last = T.matmul(QM[:, qb * P:(qb + 1) * P],
                                    max_pad[n % 2][:, qb, :, :].rearrange("p j r -> p (j r)"), ident_b[:],
                                    start=False, stop=True, skip_group_check=True)
                last.then_inc(qm_full, 1)

            def scores_for_exp(n, u, i):
                s = n % 2
                c, h2 = divmod(u, 2)
                if i == 0:
                    if u == 0:
                        pe.wait_ge(qm_copied, n + 1)
                        pe.wait_ge(k_padded[s], 16 * HG * (n // 2 + 1))
                    if n == 0 and u < 2:
                        pe.wait_ge(rep_copied, 2 * GROUPS)
                    else:
                        pe.wait_ge(exp_done, STU * n + u - 1)
                j = 2 * h2 + i
                bank = ST[:, 2 * (u % 2) + i, :]
                q = q_mov[:, s, :]
                if c == 0:
                    last = T.matmul(bank, k_pad[s][:, j, 0:P], q, start=True, stop=True)
                elif c == 1:
                    last = T.matmul(bank[:, 0:3 * P], k_pad[s][:, j, P:2 * P], q[:, P:S], start=True, stop=True)
                else:
                    T.matmul(bank[:, 0:2 * P], k_pad[s][:, j, 2 * P:3 * P], q[:, 2 * P:S], start=True, stop=True)
                    last = T.matmul(bank[:, 2 * P:S], k_pad[s][:, j, 3 * P:S], q[:, 2 * P:S], start=True, stop=True)
                if i == 1:
                    last.then_inc(st_full, 1)

            def weigh_v(n, kb):
                c = min(kb, 2)
                if kb < 3:
                    pe.wait_ge(masked, 3 * n + c + 1)
                if kb == 0:
                    pe.wait_ge(v_copied, KB * (n // NG + 1))
                    if n:
                        pe.wait_ge(pv_copied, n)
                o, w = ((0, S), (0, 3 * P), (0, 2 * P), (3 * P, P))[kb]
                for j in range(HG):
                    v0 = ((n * KB + kb) * HG + j) * VC
                    last = T.matmul(PV[32 * j:32 * j + 32, S - w:S], v_all[:, v0:v0 + 32],
                                    probs[n % 2][:, c, j, o:o + w], start=(kb == 0), stop=(kb == KB - 1),
                                    skip_group_check=True)
                if kb == 3:
                    last.then_inc(pv_full, 1)

            project(0, 0)
            project(0, 1)
            modulate(1)
            stack(0)
            stack(1)
            rest = {0: [lambda: stack(2)], 1: [lambda: stack(3)], 2: [lambda: project_v(0)]}
            for k in range(4):
                rest[3 + k] = [lambda k=k: stack(4 + k)]
            rest[7] = [lambda: project(1, 0)]
            rest[9] = [lambda: project(1, 1)]
            rest[11] = [lambda: project_v(1)]
            for k in range(2 * NG):
                rest[13 + k] = [lambda k=k: stack(2 * NG + k)]
            rest[21] = [lambda: lay_max_under_q(0)]
            for k in range(2 * MXU):
                scores_for_max(k // MXU, k % MXU)
                run(rest, k)
            for u in range(2):
                for i in range(2):
                    scores_for_exp(0, u, i)

            def project_out(b):
                pe.wait_ge(onorm_ready, b + 1)
                pe.wait_ge(ld_small, 16)
                if b == 0:
                    pe.wait_ge(mx_reduced, GROUPS * MXU)
                T.matmul(psum[:, 0, :] if b == 0 else MISC, small[:, W_OUT:W_OUT + D], packed_out[:],
                         start=True, stop=True).then_inc(proj_ready, 1)

            def route_experts(b):
                pe.wait_ge(temb_ready, B)
                pe.wait_ge(x1_ready, b + 1)
                bank = psum[:, 1, :] if b == 0 else MISC
                T.matmul(bank[:, 0:KB * EXPERTS], temb[:, b, :], small[:, W_RT:W_RB], start=True, stop=True)
                for t in range(KB):
                    last = T.matmul(bank[:, t * EXPERTS:(t + 1) * EXPERTS],
                                    x1[:, b * S + t * P:b * S + (t + 1) * P], small[:, W_R:W_RT],
                                    start=False, stop=True, skip_group_check=True)
                last.then_inc(logits, 1)

            def three(o, hi, lo, x_hi, x_lo, start, stop):
                T.matmul(o, hi, x_hi, start=start, stop=False)
                T.matmul(o, lo, x_hi, start=False, stop=False)
                return T.matmul(o, hi, x_lo, start=False, stop=stop)

            def up(i):
                kind, b, w = UNITS[i]
                r = i % RING
                if i == 0:
                    pe.wait_ge(expneg, 1)
                    pe.wait_ge(w_lo, (UP_COLS + DN_COLS) // S)
                elif i < SH_UNITS:
                    pe.wait_ge(h_ready, i)
                elif i < SH_UNITS + RING - 1:
                    pe.wait_ge(exp_done, GROUPS * STU)
                else:
                    if UNITS[i - RING][0] != "zone":
                        pe.wait_ge(h_ready, i - RING + 1)
                    else:
                        pe.wait_ge(act_done, i - RING + 1)
                if kind == "zone":
                    z, m = b * TOPZ + w // ZM, w % ZM
                    if w == 0:
                        pe.wait_ge(x2_lo_ready, b + 1)
                    if m == 0:
                        pe.wait_ge(a_lo, z + 1)
                    c = slice(m * P, (m + 1) * P)
                    zw_ = zone_w[z % ZSLOTS]
                    last = three(pair_of(i)[:, 0, :], zw_[:, 0, c], zw_[:, 1, c], x2_hi[:, b, :], x2_lo[:, b, :], True, True)
                else:
                    if w == 0 and kind == "shared":
                        pe.wait_ge(x1_lo_ready, b + 1)
                    for t, c in enumerate(up_cols(kind, w)):
                        last = three(pair_of(i)[:, t, :], up_hi[:, c:c + P], up_lo[:, c:c + P],
                                     x1_hi[:, b, :], x1_lo[:, b, :], True, True)
                    if kind == "routed":
                        if w == 0:
                            pe.wait_ge(gateT_copied, b + 1)
                            pe.wait_ge(sele_ready, 1)
                        last = T.matmul(pair_of(i)[:, 1, :], sel_e[:, w, :], gates_t[b], start=True, stop=True)
                last.then_inc(up_full, 1)

            def down(i):
                kind, b, w = UNITS[i]
                r = i % RING
                pe.wait_ge(lo_done, i + 1)
                first = w == 0 and kind != "routed"
                final = i + 1 == N_UNITS or (UNITS[i + 1][2] == 0 and UNITS[i + 1][0] != "routed")
                if first:
                    if i == 0:
                        pe.wait_ge(gateT_copied, 1)
                    elif kind == "shared":
                        pe.wait_ge(x2_ready, b)
                    elif b == 0:
                        pe.wait_ge(x2_ready, B)
                    else:
                        pe.wait_ge(y_ready, b)
                if kind == "zone":
                    z, m = b * TOPZ + w // ZM, w % ZM
                    c = slice(m * P, (m + 1) * P)
                    hi, lo = zone_w[z % ZSLOTS][:, 2, c], zone_w[z % ZSLOTS][:, 3, c]
                    if m == 0:
                        pe.wait_ge(b_lo, z + 1)
                else:
                    c = dn_col(kind, w)
                    hi, lo = dn_hi[:, c:c + D], dn_lo[:, c:c + D]
                three(OUT, hi, lo, h_hi[r], h_lo[r], first, final).then_inc(down_done, 1)

            def transpose_gates(b):
                pe.wait_ge(gate_ready, b + 1)
                if b == 0:
                    pe.wait_ge(qm_copied, GROUPS)
                pe.wait_ge(expneg, b + 1)
                for t in range(KB):
                    last = T.transpose(psum[:, 7 - b, :][0:2 * EXPERTS, t * P:(t + 1) * P], gate_hl[:, b, t, :],
                                       small[:, W_ID:W_ID + P])
                last.then_inc(gateT_full, 1)

            def zone_hidden(b):
                pe.wait_ge(x2_ready, b + 1)
                if b == 0:
                    pe.wait_ge(gateT_copied, B)
                else:
                    pe.wait_ge(z_all, b)
                T.matmul(MISC[0:RH, 64:65], small[:, W_Z1:W_Z1 + RH], pooled[:, b:b + 1],
                         start=True, stop=True).then_inc(z_hid, 1)

            def zone_logits(b):
                pe.wait_ge(z_tanh, b + 1)
                T.matmul(MISC[0:1, 72:80], hid[:, b:b + 1], small[0:RH, W_Z2:W_Z2 + ZONES],
                         start=True, stop=True).then_inc(z_logit, 1)

            def zone_spread(b):
                pe.wait_ge(z_w, b + 1)
                T.matmul(MISC[:, 80:80 + TOPZ], ones_row[:], zw[:, b, :], start=True, stop=True).then_inc(z_bc, 1)

            for n in range(GROUPS):
                def ex(n_, u):
                    cost = (0.21, 0.16, 0.21)[u // 2]
                    return [(cost, lambda i=i: scores_for_exp(n_, u, i)) for i in range(2)] if n_ < GROUPS else []

                def pv(kb):
                    return [((0.9, 0.7, 0.5, 0.25)[kb], lambda: weigh_v(n, kb))]

                others = ex(n, 2) + ex(n, 3)
                if n + 1 < GROUPS:
                    others.append((0.43, lambda: lay_max_under_q(n + 1)))
                others += ex(n, 4) + pv(0) + ex(n, 5) + ex(n + 1, 0) + pv(1) + ex(n + 1, 1) + pv(2) + pv(3)
                if n == GROUPS - 2:
                    others.insert(4, (0.9, lambda: project_out(0)))
                    others.insert(10, (0.9, lambda: route_experts(0)))
                    others.insert(-2, (1.3, lambda: up(0)))
                if n == GROUPS - 1:
                    others = ex(n, 2) + ex(n, 3) + ex(n, 4) + ex(n, 5) + pv(0) + [(1.3, lambda: up(1))] + pv(1) + \
                        [(0.2, lambda: transpose_gates(0)), (1.3, lambda: up(2))] + pv(2) + pv(3)
                units = [lambda u=u: scores_for_max(n + 2, u) for u in range(MXU)] if n + 2 < GROUPS else []
                for what in spread(units, others):
                    what()

            extras = {9: [lambda: project_out(1)], 11: [lambda: route_experts(1)],
                      16: [lambda: transpose_gates(1)]}
            for b in range(B):
                o = EXP_UNITS * (b + 1) + b
                for at, what in ((4, zone_hidden), (6, zone_logits), (9, zone_spread)):
                    extras.setdefault(o + at, []).append(lambda b=b, what=what: what(b))
            for i in range(3, N_UNITS + LAG):
                run(extras, i)
                if i < N_UNITS:
                    up(i)
                down(i - LAG)


WARM = 10


def host_constants():
    pattern = np.zeros((4, 32, P), np.float32)
    for j in range(HG):
        for d in range(HD):
            src = j * HD + d
            for t, blocks in enumerate(((1, 2), (3,), (1, 3), (2,))):
                for r in blocks:
                    pattern[t, src, 32 * j + HD * r + d] = 1.0
    consts = np.zeros((P, C_END), np.float32)
    consts[:, C_SEL:C_ID] = np.tile(pattern.transpose(1, 0, 2).reshape(32, 4 * P), (4, 1))
    consts[:, C_ID:C_MASK] = np.eye(P, dtype=np.float32)
    k, q = np.mgrid[0:P, 0:P]
    consts[:, C_MASK:C_ONE] = np.where(k > q, np.float32(BIG), np.float32(0.0))
    consts[:, C_ONE] = np.isin(np.arange(P) % 32, (0, 1))
    for e in range(EXPERTS):
        consts[[e, EXPERTS + e], C_SELE + e * P:C_SELE + (e + 1) * P] = 1.0
    half = HD // 2
    inv = (1.0 / np.power(np.float32(10000.0), np.arange(half, dtype=np.float32) / np.float32(half))).astype(np.float32)
    ang = (np.arange(S, dtype=np.float32)[:, None] * inv[None, :]).astype(np.float64)
    cos = np.cos(ang).astype(np.float32).T
    sin = np.sin(ang).astype(np.float32).T
    cos = np.tile(np.concatenate([cos, cos]), (H, 1))
    sin = np.tile(np.concatenate([-sin, sin]), (H, 1))
    return consts, np.concatenate([cos, sin], axis=1)


def swapped(w):
    return w.reshape(-1, 2, HD // 2, D)[:, ::-1].reshape(-1, D)


def laid_out(inputs):
    a = {k: np.asarray(v) for k, v in inputs.items()}
    consts, rotary = host_constants()
    wq = a["L0_attn_w_qkv"]
    small = np.zeros((P, W_END), np.float32)
    small[:, W_OUT:W_OUT + D] = a["L0_attn_w_out"].T
    wr = a["L0_cond2_W_router"]
    small[:, W_R:W_R + EXPERTS] = wr[:, 0:D].T
    small[:, W_RT:W_RB] = np.tile(wr[:, D:2 * D].T, (1, KB))
    small[:, W_RB:W_RB + EXPERTS] = a["L0_cond2_router_bias"][None, :]
    small[:, W_IOTA:W_IOTA + EXPERTS] = np.arange(EXPERTS)[None, :]
    small[:, W_Z1:W_Z1 + RH] = a["L0_ffn_W1"]
    small[0:RH, W_Z2:W_Z2 + ZONES] = a["L0_ffn_W2"]
    small[0:RH, W_B1] = a["L0_ffn_b1"]
    small[0, W_B2:W_B2 + ZONES] = a["L0_ffn_b2"]
    small[:, W_ID:W_END] = np.eye(P, dtype=np.float32)
    up = np.stack([a["L0_cond2_s_w1"], a["L0_cond2_s_w3"]], axis=1)
    experts = [up.transpose(3, 0, 1, 2).reshape(D, -1), a["L0_cond2_r_w1"].transpose(2, 0, 1).reshape(D, -1),
               a["L0_cond2_s_w2"].reshape(SHARED, D, HID_S // P, P).transpose(3, 0, 2, 1).reshape(P, -1),
               a["L0_cond2_r_w2"].transpose(2, 0, 1).reshape(HID_R, -1)]
    arrays = {
        "xT": a["x"].reshape(NT, D).T, "condT": a["cond_1024"].T, "L0_cond_weight": a["L0_cond_weight"],
        "w_qkvT": wq.T, "w_rotT": swapped(wq[:2 * D]).T, "rotary": rotary, "consts": consts, "small": small,
        "experts": np.concatenate(experts, axis=1),
        "L0_ffn_Wa": a["L0_ffn_Wa"], "L0_ffn_Wb": a["L0_ffn_Wb"],
    }
    return {k: np.ascontiguousarray(v) for k, v in arrays.items()}


def kernel(**inputs):
    import concourse.bacc as bacc
    from concourse.bass_utils import run_bass_kernel_spmd

    nc = bacc.Bacc("TRN2", target_bir_lowering=False, num_devices=1)
    arrays = laid_out(inputs)
    io = {n: nc.dram_tensor("in_" + n, a.shape, F32, kind="ExternalInput").ap() for n, a in arrays.items()}
    scratch = nc.dram_tensor("scratch", (GROUPS, P, S), F32, kind="Internal").ap()
    out = nc.dram_tensor("out_0_dram", (D, NT), F32, kind="ExternalOutput").ap()
    program(nc, io, scratch, out)
    r = run_bass_kernel_spmd(nc, [{"in_" + n: a for n, a in arrays.items()}], core_ids=[0])
    return np.ascontiguousarray(r.results[0]["out_0_dram"].T).reshape(B, S, D)
```

```python
import numpy as np
from contextlib import ExitStack

import concourse.bass as bass
from concourse import mybir

ALU = mybir.AluOpType
ACT = mybir.ActivationFunctionType
AX = mybir.AxisListType
F32 = mybir.dt.float32
F32R = mybir.dt.float32r
BF16 = mybir.dt.bfloat16
U32 = mybir.dt.uint32

P = 128
B, S, D = 2, 512, 128
NT = B * S
H, HD = 16, 8
HG = 4
NG = H // HG
GROUPS = B * NG
KB = S // P
VC = 2 * HD
MXU = 12
STU = 6
BIG = -1.0e30
BANK = 512

EXPERTS, SHARED, HID_S, HID_R = 8, 2, 256, 128
ZONES, TOPZ, DFF, RH = 8, 3, 512, 32

MX_UNITS = [(0, (0, 1)), (0, (2, 3)), (1, (0, 1)), (1, (2, 3))] + \
           [(qb, (j,)) for qb in (2, 3) for j in range(HG)]

SH_UNITS = SHARED * HID_S // P
EXP_UNITS = SH_UNITS + EXPERTS
ZM = DFF // P
FFN_UNITS = TOPZ * ZM
E_TOTAL = B * EXP_UNITS
UNITS = [u for b in range(B) for u in
         [("shared", b, i) for i in range(SH_UNITS)] + [("routed", b, e) for e in range(EXPERTS)]] + \
        [("zone", b, i) for b in range(B) for i in range(FFN_UNITS)]
N_UNITS = len(UNITS)
AHEAD = MXU + 9
ST_ORDER = [("exp", 0, 0), ("exp", 0, 1), ("project", 0), ("project", 1)]
for _n in range(GROUPS):
    ST_ORDER += [("exp", _n, 2), ("exp", _n, 3)] + ([("stack", 2 * _n + 2)] if _n in (1, 2) else [])
    ST_ORDER += [("exp", _n, 4), ("exp", _n, 5)] + ([("stack", 2 * _n + 3)] if _n in (1, 2) else [])
    ST_ORDER += [("exp", _n + 1, 0), ("exp", _n + 1, 1)] if _n + 1 < GROUPS else []
AT = {
    "invert 1": [3],
    "normalise 1": [6],
    "residual 1": [9],
    "x1 low 1": [11],
    "gates 1": [11, 11, 12, 13],
    "x2 low": [14, 28],
    "choose zones": [17, 30],
    "weigh zones": [18, 32],
    "spread weights": [19, 32],
    "b low": [21, 22, 25, 34, 37, 40],
    "copy gates": [1, 15],
    "x1 high 1": [9],
    "exp 1": [11],
    "finish experts": [14, 25],
    "router tanh": [16, 26],
    "a high": [19, 20, 21, 32, 34, 37],
    "transpose gates": [2, 16],
    "project 1": [10],
    "route 1": [12],
    "zone hidden": [17, 28],
    "zone logits": [18, 31],
    "zone spread": [21, 34],
}
INV_AT = [78, 92]
ROTATE_AT = [16, 18]
FIRST_AT = [1, 2, 4, 6, 11, 12, 14, 15, 16, 18]
SPLITS = {(2, 0): 0, (2, 2): 1, (3, 0): 2, (3, 2): 3, (4, 0): 4, (4, 2): 5, (5, 0): 6}
GROUP_COST = {0: 5.75, 1: 6.82, 2: 6.82, GROUPS - 2: 6.9}
USUAL_COST = 5.1
WARM = 7
RING = 3
LO_POOL = range(EXP_UNITS + SH_UNITS)
LAG = 3
ZSLOTS = 4
UP_COLS = SHARED * 2 * HID_S + EXPERTS * HID_R
DN_COLS = (SH_UNITS + EXPERTS) * D

C_SEL, C_ID, C_MASK, C_ONE, C_END = 0, 512, 640, 768, 769
W_OUT, W_R, W_RT, W_RB, W_IOTA, W_Z1, W_Z2, W_B1, W_B2 = 0, 128, 136, 168, 176, 184, 216, 224, 225
W_END = W_B2 + ZONES


def f32_of(ap):
    return ap.bitcast(F32)


def due(name, i):
    return [k for k, at_ in enumerate(AT[name]) if at_ == i]


def program(nc, io, scratch, out):
    ctx = ExitStack()
    with ctx:
        def sb(name, shape, dt=F32):
            return ctx.enter_context(nc.sbuf_tensor("t_" + name, shape, dt))

        def sem(name):
            return ctx.enter_context(nc.semaphore(name))

        psum = ctx.enter_context(nc.psum_tensor("psum", [P, 8, BANK], F32))
        MX, ST, PV, QM = psum[:, 0:2, :], psum[:, 2:6, :], psum[:, 6, :], psum[:, 7, :]
        OUT, MISC = psum[:, 7, :], psum[:, 6, :]

        cond = sb("cond", [P, B])
        ys = sb("ys", [P, B])
        ys_sq = sb("ys_sq", [P, B])
        dvar = sb("dvar", [P, B])
        dexp = sb("dexp", [P, B])
        dinv = sb("dinv", [P, B])
        xT = sb("xT", [P, NT])
        small = sb("small", [P, W_END])
        sel = sb("sel", [P, NG, 4, P], F32R)
        ident_r = sb("ident_r", [P, P], F32R)
        gate_rows = sb("gate_rows", [2 * EXPERTS, EXPERTS * P])
        one_col = sb("one_col", [P, 1])
        ident_b = sb("ident_b", [P, P], BF16)
        causal = sb("causal", [P, S])
        q_mov = sb("q_mov", [P, 2, S], F32R)
        stacked = sb("stacked", [P, 2 * GROUPS, S], F32R)
        v_all = sb("v_all", [P, (GROUPS * KB * HG + 1) * VC])
        q_pad = [sb(f"q_pad{s}", [P, HG, S], F32R) for s in range(2)]
        k_pad = [sb(f"k_pad{s}", [P, HG, S], F32R) for s in range(2)]
        row_max = [sb(f"row_max{s}", [P, KB, HG]) for s in range(2)]
        max_pad = [sb(f"max_pad{s}", [P, KB, HG, 32], BF16) for s in range(2)]
        probs = [sb(f"probs{s}", [P, 3, HG, BANK]) for s in range(2)]
        o_sb = [sb(f"o_sb{s}", [P, S]) for s in range(2)]
        packed_out = sb("packed_out", [P, S])
        packed_sum = sb("packed_sum", [P, S])
        sums = sb("sums", [P, B, S // HD])
        x1 = sb("x1", [P, NT])
        raw = sb("raw", [P, UP_COLS + DN_COLS])
        up_hi = sb("up_hi", [P, UP_COLS], F32R)
        up_lo = sb("up_lo", [P, UP_COLS], F32R)
        dn_hi = sb("dn_hi", [P, DN_COLS], F32R)
        dn_lo = sb("dn_lo", [P, DN_COLS], F32R)

        p0 = probs[0][:].rearrange("p c j k -> p (c j k)")
        p1 = probs[1][:].rearrange("p c j k -> p (c j) k")
        consts, xs, w_cond_sq = p0[:, 0:C_END], p1[:, 0:2, :], p1[:, 10, 0:D]
        cos_t, sin_t = raw[:, 0:S], raw[:, S:2 * S]
        w_qkv, w_rot = raw[:, 2 * S:2 * S + 3 * D], raw[:, 2 * S + 3 * D:2 * S + 5 * D]
        w_cond = raw[:, 2 * S + 5 * D:2 * S + 6 * D]
        at = 2 * S + 6 * D
        xc = raw[:, at:at + B * S].rearrange("p (b t) -> p b t", b=B)
        rope_c, rope_s = [raw[:, at + B * S:at + B * S + S], o_sb[1][:]], [packed_sum[:], packed_out[:]]
        roped = x1[:].rearrange("p (i t) -> p i t", i=2)
        qk_hi = dn_hi[:, 0:2 * S].rearrange("p (i t) -> p i t", i=2)
        qk_lo = dn_lo[:, 0:2 * S].rearrange("p (i t) -> p i t", i=2)

        flat = [t[:].rearrange("p c j k -> p (c j) k") for t in probs]
        zone_a, x12, y = flat[0][:, 0:8, :], flat[0][:, 8:10, :], flat[0][:, 10:12, :]
        zone_b, x2 = flat[1][:, 0:8, :], flat[1][:, 8:10, :]
        x1_hi, x1_lo = stacked[:, 0:2, :], stacked[:, 2:4, :]
        x2_hi, x2_lo = stacked[:, 4:6, :], stacked[:, 6:8, :]
        zone_w = [stacked[:, 8:12, :], stacked[:, 12:16, :], k_pad[0][:], k_pad[1][:]]
        h_hi = [q_pad[0][:, r, :] for r in range(RING)]
        h_lo = [q_pad[1][:, r, :] for r in range(RING)]
        gates_t = [q_pad[b][:, RING, :] for b in range(B)]
        sel_e = sel[:].rearrange("p g t m -> p (g t) m")[:, 0:EXPERTS, :]
        act_out = [raw[:, r * S:(r + 1) * S] for r in range(RING)]
        hidden = [raw[:, (RING + r) * S:(RING + r + 1) * S] for r in range(RING)]
        silu = raw[:, 2 * RING * S:(2 * RING + 1) * S]

        temb = causal[:, 0:B * P].rearrange("p (b t) -> p b t", b=B)
        shape_g = [P, B, KB, EXPERTS]
        e_neg, e_one, sig, rank = (sb(x, shape_g) for x in ("e_neg", "e_one", "sig", "rank"))
        top = sb("top", [P, B, KB, 8])
        top_i = sb("top_i", [P, B, KB, 8], U32)
        top_f = sb("top_f", [P, B, KB, 2])
        eq0, eq1, chosen, s_sel = (sb(x, shape_g) for x in ("eq0", "eq1", "chosen", "s_sel"))
        denom, okay, denom_e, inv_d, scale_s, scale_c = (
            sb(x, [P, B, KB]) for x in ("denom", "okay", "denom_e", "inv_d", "scale_s", "scale_c"))
        part_s, part_c, gate = (sb(x, shape_g) for x in ("part_s", "part_c", "gate"))
        gate_hl = sb("gate_hl", [P, B, KB, 2 * EXPERTS])
        euler = sb("euler", [P, KB, EXPERTS])
        pooled = sb("pooled", [P, B])
        hid = sb("hid", [RH, B])
        zl = sb("zl", [1, B, ZONES])
        ztop = sb("ztop", [1, B, 8])
        zidx = sb("zidx", [1, B, 8], U32)
        zdiff = sb("zdiff", [1, B, TOPZ])
        zexp = sb("zexp", [1, B, TOPZ])
        zsum = sb("zsum", [1, B])
        zinv = sb("zinv", [1, B])
        zw = sb("zw", [1, B, TOPZ])
        ones_row = sb("ones_row", [1, P])
        zw_all = sb("zw_all", [P, B, TOPZ])

        names = """
            ld_cond ld_x1 ld_proj ld_rot ld_const ld_raw ld_small ld_zones
            pads_early ys_ready sq_ready dsum_ready dvar_ready dinv_ready xs_ready cond_ready xc_ready
            qk_ready v_ready v_copied rope_ready roped_ready hi_ready lo_ready sel_zero pad0_zero pads_zero q0_placed v_ones
            const_ready rep_ready rep_copied mx_full mx_reduced mhi_ready m_ready qm_full qm_copied st_full
            exp_done masked pv_full pv_copied packed
            temb_ready w_hi w_lo ld_sums inv_ready inv_stored onorm_ready proj_ready x1_ready x1_hi_ready x1_lo_ready
            ld_sele sele_zero sele_ready gates_zero logits expneg gate_step gate_ready gateT_full gateT_copied
            up_full act_done silu_done h_ready hi_done lo_done down_done x2_ready x2_hi_ready x2_lo_ready
            x12_ready z_hid z_tanh z_logit z_step z_diff z_exp z_w z_bc z_all a_hi b_hi a_lo b_lo y_ready stored_y
            euler_ready""".split()
        sems = {n: sem(n) for n in names}
        (ld_cond, ld_x1, ld_proj, ld_rot, ld_const, ld_raw, ld_small, ld_zones,
         pads_early, ys_ready, sq_ready, dsum_ready, dvar_ready, dinv_ready, xs_ready, cond_ready, xc_ready,
         qk_ready, v_ready, v_copied, rope_ready, roped_ready, hi_ready, lo_ready, sel_zero, pad0_zero, pads_zero, q0_placed,
         v_ones, const_ready, rep_ready, rep_copied, mx_full, mx_reduced, mhi_ready, m_ready, qm_full, qm_copied,
         st_full, exp_done, masked, pv_full, pv_copied, packed,
         temb_ready, w_hi, w_lo, ld_sums, inv_ready, inv_stored, onorm_ready, proj_ready, x1_ready, x1_hi_ready, x1_lo_ready,
         ld_sele, sele_zero, sele_ready, gates_zero, logits, expneg, gate_step, gate_ready, gateT_full, gateT_copied,
         up_full, act_done, silu_done, h_ready, hi_done, lo_done, down_done, x2_ready, x2_hi_ready, x2_lo_ready,
         x12_ready, z_hid, z_tanh, z_logit, z_step, z_diff, z_exp, z_w, z_bc, z_all, a_hi, b_hi, a_lo, b_lo, y_ready,
         stored_y, euler_ready) = (sems[n] for n in names)
        q_padded = [sem(f"q_padded{s}") for s in range(2)]
        k_padded = [sem(f"k_padded{s}") for s in range(2)]
        stored = [sem(f"stored{s}") for s in range(2)]
        block = ctx.enter_context(nc.Block())

        def cols(b):
            return slice(b * S, (b + 1) * S)

        def up_cols(kind, i):
            if kind == "shared":
                e, m = divmod(i, HID_S // P)
                return [(2 * e + t) * HID_S + m * P for t in range(2)]
            return [SHARED * 2 * HID_S + i * P]

        def dn_col(kind, i):
            return i * D if kind == "shared" else (SH_UNITS + i) * D

        chunks = [(up_hi, up_lo, c, c) for c in range(0, UP_COLS, S)] + \
                 [(dn_hi, dn_lo, c, UP_COLS + c) for c in range(0, DN_COLS, S)]

        def pair_of(i):
            r = i % RING
            return psum[:, 2 * r:2 * r + 2, :]

        def slot_of(*item):
            return 2 * (ST_ORDER.index(item) % 2)

        @block.sync
        def _(sp):
            sp.dma_start(cond[:], io["condT"]).then_inc(ld_cond, 16)
            sp.dma_start(w_cond, io["L0_cond_weight"]).then_inc(ld_cond, 16)
            sp.dma_start(xT[:, cols(0)], io["xT"][:, cols(0)]).then_inc(ld_cond, 16)
            sp.dma_start(w_qkv, io["w_qkvT"]).then_inc(ld_proj, 16)
            sp.dma_start(w_rot, io["w_rotT"]).then_inc(ld_proj, 16)
            sp.dma_start(raw[:, 0:2 * S], io["rotary"]).then_inc(ld_rot, 16)
            sp.dma_start(consts, io["consts"]).then_inc(ld_const, 16)
            sp.dma_start(xT[:, cols(1)], io["xT"][:, cols(1)]).then_inc(ld_x1, 16)
            sp.dma_start(small[:], io["small"]).then_inc(ld_small, 16)
            sp.dma_start(gate_rows[:], io["sel_e"]).then_inc(ld_sele, 16)

            def pad_q(n):
                s = n % 2
                sp.wait_ge(rep_copied, 2 * n + 1)
                if n >= 2:
                    sp.wait_ge(mx_full, (n - 1) * MXU)
                for j in range(HG):
                    q = slice(32 * j, 32 * j + 32)
                    sp.dma_start(f32_of(q_pad[s][q, j, :]), f32_of(stacked[q, 2 * n, :])).then_inc(q_padded[s], 16)

            def pad_k(n):
                s = n % 2
                sp.wait_ge(rep_copied, 2 * n + 2)
                if n >= 2:
                    sp.wait_ge(st_full, (n - 1) * STU)
                for j in range(HG):
                    q = slice(32 * j, 32 * j + 32)
                    sp.dma_start(f32_of(k_pad[s][q, j, :]), f32_of(stacked[q, 2 * n + 1, :])).then_inc(k_padded[s], 16)

            def store_sums(n):
                sp.wait_ge(pv_copied, n + 1)
                sp.dma_start(scratch[n], o_sb[n % 2][:]).then_inc(stored[n % 2], 16)

            def pack(b):
                for s in range(2):
                    sp.wait_ge(stored[s], 16 * NG * (b + 1) // 2)
                heads = scratch[b * NG:(b + 1) * NG].rearrange("g (j r) t -> (g j) r t", j=HG)
                inverse = scratch[GROUPS][b * H:(b + 1) * H, :]
                sp.dma_start(sums[:, b, :], heads[:, HD, :].rearrange("h (c t) -> h c t", c=HD)).then_inc(ld_sums, 16)
                if b:
                    sp.wait_ge(onorm_ready, b)
                    sp.wait_ge(proj_ready, b)
                sp.dma_start(packed_out[:], heads[:, 0:HD, :]).then_inc(packed, 16)
                sp.wait_ge(inv_ready, b + 1)
                sp.dma_start(inverse.rearrange("h (c t) -> (h c) t", c=HD), sums[:, b, :]).then_inc(inv_stored, 16)
                sp.wait_ge(inv_stored, 16 * (b + 1))
                sp.dma_start(packed_sum[:], inverse.unsqueeze(1).broadcast_to([H, HD, S])).then_inc(packed, 16)

            sp.wait_ge(pads_zero, 1)
            pad_k(0)
            pad_q(1)
            pad_k(1)
            pad_q(2)
            for n in range(GROUPS):
                if n + 3 < GROUPS and n != NG:
                    pad_q(n + 3)
                if n + 2 < GROUPS:
                    pad_k(n + 2)
                store_sums(n)
                if n == 0:
                    sp.wait_ge(v_ready, B)
                    sp.wait_ge(roped_ready, 2 * B)
                    sp.dma_start(raw[:], io["experts"]).then_inc(ld_raw, 16)
                if n == NG - 1:
                    pad_q(n + 4)
                    pack(0)
            pack(1)
            sp.wait_ge(pv_full, GROUPS)
            for lo in range(0, ZONES, 4):
                sp.dma_start(zone_a[:, lo:lo + 4, :],
                             io["L0_ffn_Wa"][lo:lo + 4].rearrange("e p f -> p e f")).then_inc(ld_zones, 16)
                sp.dma_start(zone_b[:, lo:lo + 4, :].rearrange("p e (m d) -> p e m d", m=ZM),
                             io["L0_ffn_Wb"][lo:lo + 4].rearrange("e (m p) d -> p e m d", p=P)).then_inc(ld_zones, 16)
            for b in range(B):
                sp.wait_ge(y_ready, b + 1)
                sp.dma_start(out[:, cols(b)], y[:, b, :]).then_inc(stored_y, 16)
            sp.wait_ge(stored_y, 16 * B)

        @block.gpsimd
        def _(pool):
            G = nc.gpsimd
            G.memset(causal[:, 0:S - P], 0.0)
            for s in range(2):
                last = G.memset(max_pad[s][:], 0.0)
            last.then_inc(pads_early, 1)
            G.memset(f32_of(sel[:]), 0.0).then_inc(sel_zero, 1)
            G.memset(dexp[:], -0.5).then_inc(sq_ready, 1)
            pool.wait_ge(ld_cond, 48)
            G.tensor_tensor(w_cond_sq, w_cond, w_cond, ALU.mult).then_inc(sq_ready, 1)
            pool.wait_ge(sq_ready, 2)
            pool.wait_ge(dvar_ready, 1)
            G.tensor_tensor(dinv[:], dvar[:], dexp[:], ALU.pow).then_inc(dinv_ready, 1)
            G.memset(f32_of(k_pad[0][:]), 0.0)
            G.memset(v_all[:], 1.0).then_inc(v_ones, 1)
            G.memset(f32_of(q_pad[1][:]), 0.0)
            G.memset(f32_of(k_pad[1][:]), 0.0).then_inc(pads_zero, 1)
            G.memset(ones_row[:], 1.0)
            G.memset(euler[:], float(np.e)).then_inc(euler_ready, 1)

            def split_low(k):
                hi, lo, c, at_ = chunks[k]
                pool.wait_ge(w_hi, k + 1)
                if k == UP_COLS // S:
                    pool.wait_ge(rep_ready, 2 * GROUPS)
                G.tensor_tensor(lo[:, c:c + S], raw[:, at_:at_ + S], f32_of(hi[:, c:c + S]),
                                ALU.subtract).then_inc(w_lo, 1)

            for n in range(GROUPS):
                for c in range(3):
                    pool.wait_ge(exp_done, STU * n + 2 * c + 2)
                    for o in ((0,) if c < 2 else (0, 3 * P)):
                        tri = probs[n % 2][:, c, :, o:o + P]
                        last = G.affine_select(out=tri, in_=tri, compare_op=ALU.is_ge, fill=0.0, base=0,
                                               pattern=[[0, HG], [1, P]], channel_multiplier=-1)
                    last.then_inc(masked, 1)
                    if n == 0 and c == 0:
                        pool.wait_ge(lo_ready, 2)
                        for i in range(2):
                            pool.wait_ge(rope_ready, 4 + 2 * i + 2)
                            G.tensor_tensor(roped[:, i, :], rope_c[i], rope_s[i], ALU.add).then_inc(roped_ready, 1)
                    if n == 0 and c:
                        pool.wait_ge(hi_ready, 2 + c)
                        pool.wait_ge(rep_ready, 2 * NG)
                        G.tensor_tensor(qk_lo[:, c - 1, :], roped[:, c - 1, :], f32_of(qk_hi[:, c - 1, :]),
                                        ALU.subtract).then_inc(lo_ready, 1)
                    if (n, c) in SPLITS:
                        split_low(SPLITS[n, c])
                if n == 4:
                    pool.wait_ge(rep_ready, 2 * GROUPS)
                    G.memset(f32_of(sel_e), 0.0).then_inc(sele_zero, 1)
                if n == GROUPS - 2:
                    for b in range(B):
                        pool.wait_ge(mx_full, GROUPS * MXU)
                        G.memset(f32_of(gates_t[b]), 0.0).then_inc(gates_zero, 1)
            for i in LO_POOL:
                pool.wait_ge(hi_done, i + 1)
                if i >= RING:
                    pool.wait_ge(down_done, i - RING + 1)
                G.tensor_tensor(h_lo[i % RING], hidden[i % RING], f32_of(h_hi[i % RING]),
                                ALU.subtract).then_inc(lo_done, 1)
            for b in range(B):
                pool.wait_ge(x1_ready, b + 1)
                pool.wait_ge(x2_ready, b + 1)
                G.tensor_tensor(x12[:, b, :], x1[:, cols(b)], x2[:, b, :], ALU.add).then_inc(x12_ready, 1)
                if b == 0:
                    pool.wait_ge(euler_ready, 1)
                pool.wait_ge(z_diff, b + 1)
                G.tensor_tensor(zexp[:, b, :], euler[0:1, 0, 0:TOPZ], zdiff[:, b, :], ALU.pow).then_inc(z_exp, 1)
                for k in range(TOPZ):
                    z = b * TOPZ + k
                    w = zone_w[z % ZSLOTS]
                    zone = G.value_load(zidx[0:1, b, k:k + 1], min_val=0, max_val=ZONES - 1)
                    pool.wait_ge(a_hi, z + 1)
                    G.tensor_tensor(w[:, 1, :], zone_a[:, bass.ds(zone, 1), :], f32_of(w[:, 0, :]),
                                    ALU.subtract).then_inc(a_lo, 1)
                    pool.wait_ge(z_all, b + 1)
                    G.tensor_tensor(w[:, 2, :], zone_b[:, bass.ds(zone, 1), :],
                                    zw_all[:, b, k:k + 1].broadcast_to([P, DFF]), ALU.mult).then_inc(b_hi, 1)

        @block.vector
        def _(dve):
            V = nc.vector
            V.memset(f32_of(q_pad[0][:]), 0.0).then_inc(pad0_zero, 1)
            dve.wait_ge(ld_cond, 48)
            V.tensor_scalar(ys[:], cond[:], float(np.float32(1.0) / np.sqrt(np.float32(D))), None,
                            ALU.mult).then_inc(ys_ready, 1)
            dve.wait_ge(ys_ready, 1)
            V.tensor_tensor(ys_sq[:], ys[:], ys[:], ALU.mult).then_inc(ys_ready, 1)
            V.tensor_scalar(xs[:, 0, :], xT[:, cols(0)], ys[:, 0:1], None, ALU.mult).then_inc(xs_ready, 1)
            dve.wait_ge(dsum_ready, 1)
            V.tensor_scalar(dvar[:], QM[:, 0:B], 1e-8, None, ALU.add).then_inc(dvar_ready, 1)
            dve.wait_ge(dinv_ready, 1)

            def modulate(b):
                dve.wait_ge(cond_ready, b + 1)
                V.tensor_scalar(xc[:, b, :], PV, dinv[:, b:b + 1], None, ALU.mult).then_inc(xc_ready, 1)

            def rotate(b, i):
                dve.wait_ge(qk_ready, 2 * b + i + 1)
                if b:
                    dve.wait_ge(roped_ready, i + 1)
                V.tensor_tensor(rope_c[i], ST[:, 2 * i, :], cos_t, ALU.mult).then_inc(rope_ready, 1)
                V.tensor_tensor(rope_s[i], ST[:, 2 * i + 1, :], sin_t, ALU.mult).then_inc(rope_ready, 1)

            def reduce_max(n, u):
                s = n % 2
                qb, heads = MX_UNITS[u]
                width = P * (qb + 1)
                dve.wait_ge(mx_full, MXU * n + u + 1)
                for i, j in enumerate(heads):
                    scores = MX[:, u % 2, i * 2 * P:i * 2 * P + width]
                    last = V.tensor_tensor_reduce(scores, scores,
                                                  causal[:, S - width:S], 1.0, 3 * BIG, ALU.add, ALU.max,
                                                  row_max[s][:, qb, j:j + 1])
                last.then_inc(mx_reduced, 1)

            def place_max(n):
                s = n % 2
                dve.wait_ge(mx_reduced, MXU * (n + 1))
                if n >= 2:
                    dve.wait_ge(qm_full, n - 1)
                else:
                    dve.wait_ge(pads_early, 1)
                V.tensor_scalar(max_pad[s][:, :, :, 0], row_max[s][:], -1.0, None, ALU.mult).then_inc(mhi_ready, 1)
                dve.wait_ge(mhi_ready, n + 1)
                V.scalar_tensor_tensor(max_pad[s][:, :, :, 1], row_max[s][:], -1.0, max_pad[s][:, :, :, 0],
                                       ALU.mult, ALU.subtract).then_inc(m_ready, 1)

            def invert(b):
                dve.wait_ge(ld_sums, 16 * (b + 1))
                V.reciprocal(sums[:, b, :], sums[:, b, :]).then_inc(inv_ready, 1)

            def normalise(b):
                dve.wait_ge(packed, 32 * (b + 1))
                V.tensor_tensor(packed_out[:], packed_out[:], packed_sum[:], ALU.mult).then_inc(onorm_ready, 1)

            def residual(b):
                dve.wait_ge(proj_ready, b + 1)
                bank = psum[:, 0, :] if b == 0 else MISC
                V.tensor_tensor(x1[:, cols(b)], bank, xT[:, cols(b)], ALU.add).then_inc(x1_ready, 1)

            def x1_low(b):
                dve.wait_ge(x1_hi_ready, b + 1)
                V.tensor_tensor(x1_lo[:, b, :], x1[:, cols(b)], f32_of(x1_hi[:, b, :]),
                                ALU.subtract).then_inc(x1_lo_ready, 1)

            steps = [0]

            def step(ins):
                steps[0] += 1
                ins.then_inc(gate_step, 1)
                dve.wait_ge(gate_step, steps[0])

            def gates(b, part):
                sg, ch = sig[:, b], chosen[:, b]
                if part == 0:
                    dve.wait_ge(expneg, b + 1)
                    step(V.tensor_scalar(e_one[:, b], e_neg[:, b], 1.0, None, ALU.add))
                    step(V.reciprocal(sg, e_one[:, b]))
                    bias = small[:, W_RB:W_RB + EXPERTS].unsqueeze(1).broadcast_to([P, KB, EXPERTS])
                    step(V.tensor_tensor(rank[:, b], sg, bias, ALU.add))
                    for t in range(KB):
                        last = V.max(top[:, b, t, :], rank[:, b, t, :])
                    step(last)
                elif part == 1:
                    for t in range(KB):
                        last = V.max_index(top_i[:, b, t, :], top[:, b, t, :], rank[:, b, t, :])
                    step(last)
                    step(V.tensor_copy(top_f[:, b], top_i[:, b, :, 0:2]))
                    iota = small[:, W_IOTA:W_IOTA + EXPERTS].unsqueeze(1).broadcast_to([P, KB, EXPERTS])
                    for o, eq in ((0, eq0), (1, eq1)):
                        last = V.tensor_tensor(eq[:, b], iota,
                                               top_f[:, b, :, o:o + 1].broadcast_to([P, KB, EXPERTS]), ALU.is_equal)
                    step(last)
                elif part == 2:
                    step(V.tensor_tensor(ch, eq0[:, b], eq1[:, b], ALU.add))
                    step(V.tensor_tensor(s_sel[:, b], ch, sg, ALU.mult))
                    step(V.tensor_reduce(denom[:, b], s_sel[:, b], AX.X, ALU.add))
                    V.tensor_scalar(okay[:, b], denom[:, b], 1e-9, None, ALU.is_gt)
                    step(V.tensor_scalar(denom_e[:, b], denom[:, b], 1e-9, None, ALU.add))
                    V.tensor_scalar(scale_c[:, b], okay[:, b], -2.0, 2.0, ALU.mult, ALU.add)
                    step(V.reciprocal(inv_d[:, b], denom_e[:, b]))
                else:
                    step(V.scalar_tensor_tensor(scale_s[:, b], inv_d[:, b], 4.0, okay[:, b], ALU.mult, ALU.mult))
                    V.tensor_tensor(part_s[:, b], s_sel[:, b],
                                    scale_s[:, b].unsqueeze(2).broadcast_to([P, KB, EXPERTS]), ALU.mult)
                    step(V.tensor_tensor(part_c[:, b], ch,
                                         scale_c[:, b].unsqueeze(2).broadcast_to([P, KB, EXPERTS]), ALU.mult))
                    step(V.tensor_tensor(gate[:, b], part_s[:, b], part_c[:, b], ALU.add))
                    step(V.tensor_copy(gate_hl[:, b, :, 0:EXPERTS].bitcast(F32R), gate[:, b]))
                    V.tensor_tensor(gate_hl[:, b, :, EXPERTS:], gate[:, b], gate_hl[:, b, :, 0:EXPERTS],
                                    ALU.subtract).then_inc(gate_ready, 1)

            zsteps = [0]

            def zstep(ins):
                zsteps[0] += 1
                ins.then_inc(z_step, 1)
                dve.wait_ge(z_step, zsteps[0])

            def choose_zones(b):
                dve.wait_ge(z_logit, b + 1)
                zstep(V.tensor_tensor(zl[:, b, :], MISC[0:1, 72:80], small[0:1, W_B2:W_B2 + ZONES], ALU.add))
                zstep(V.max(ztop[:, b, :], zl[:, b, :]))
                V.max_index(zidx[:, b, :], ztop[:, b, :], zl[:, b, :])
                V.tensor_scalar(zdiff[:, b, :], ztop[:, b, 0:TOPZ], ztop[:, b, 0:1], None,
                                ALU.subtract).then_inc(z_diff, 1)

            def weigh_zones(b):
                dve.wait_ge(z_exp, b + 1)
                zstep(V.tensor_reduce(zsum[:, b:b + 1], zexp[:, b, :], AX.X, ALU.add))
                zstep(V.reciprocal(zinv[:, b:b + 1], zsum[:, b:b + 1]))
                V.tensor_scalar(zw[:, b, :], zexp[:, b, :], zinv[:, b:b + 1], None, ALU.mult).then_inc(z_w, 1)

            def spread_weights(b):
                dve.wait_ge(z_bc, b + 1)
                V.tensor_copy(zw_all[:, b, :], MISC[:, 80:80 + TOPZ]).then_inc(z_all, 1)

            def zone_b_low(z):
                b, k = divmod(z, TOPZ)
                w = zone_w[z % ZSLOTS]
                dve.wait_ge(z_diff, b + 1)
                zone = V.value_load(zidx[0:1, b, k:k + 1], min_val=0, max_val=ZONES - 1)
                dve.wait_ge(b_hi, z + 1)
                V.scalar_tensor_tensor(w[:, 3, :], zone_b[:, bass.ds(zone, 1), :], zw_all[:, b, k:k + 1],
                                       f32_of(w[:, 2, :]), ALU.mult, ALU.subtract).then_inc(b_lo, 1)

            n_silu = [0]

            def finish_hidden(i):
                kind, b, w = UNITS[i]
                r = i % RING
                if kind == "zone":
                    return
                dve.wait_ge(act_done, i + 1)
                if i >= RING:
                    dve.wait_ge(hi_done, i - RING + 1)
                    dve.wait_ge(lo_done, i - RING + 1)
                pair = pair_of(i)
                if kind == "shared":
                    if i:
                        dve.wait_ge(h_ready, i)
                    V.scalar_tensor_tensor(silu, act_out[r], 1.0, pair[:, 0, :], ALU.add,
                                           ALU.mult).then_inc(silu_done, 1)
                    n_silu[0] += 1
                    dve.wait_ge(silu_done, n_silu[0])
                    V.tensor_tensor(hidden[r], silu, pair[:, 1, :], ALU.mult).then_inc(h_ready, 1)
                else:
                    V.tensor_tensor(hidden[r], act_out[r], pair[:, 1, :], ALU.mult).then_inc(h_ready, 1)

            def hidden_lo(i):
                r = i % RING
                src_ = act_out[r] if UNITS[i][0] == "zone" else hidden[r]
                if i in LO_POOL:
                    return
                dve.wait_ge(hi_done, i + 1)
                if i == LO_POOL.stop:
                    dve.wait_ge(lo_done, i)
                if i >= RING:
                    dve.wait_ge(down_done, i - RING + 1)
                V.tensor_tensor(h_lo[r], src_, f32_of(h_hi[r]), ALU.subtract).then_inc(lo_done, 1)

            def x2_low(b):
                dve.wait_ge(x2_hi_ready, b + 1)
                V.tensor_tensor(x2_lo[:, b, :], x2[:, b, :], f32_of(x2_hi[:, b, :]),
                                ALU.subtract).then_inc(x2_lo_ready, 1)

            def add_residual(b):
                dve.wait_ge(down_done, E_TOTAL + (b + 1) * FFN_UNITS)
                dve.wait_ge(x12_ready, b + 1)
                V.tensor_tensor(y[:, b, :], OUT, x12[:, b, :], ALU.add).then_inc(y_ready, 1)

            modulate(0)
            dve.wait_ge(ld_rot, 16)
            rotate(0, 0)
            dve.wait_ge(rope_ready, 2)
            V.tensor_tensor(roped[:, 0, :], rope_c[0], rope_s[0], ALU.add).then_inc(roped_ready, 1)
            rotate(0, 1)
            dve.wait_ge(hi_ready, 1)
            V.tensor_tensor(qk_lo[:, 0, :], roped[:, 0, :], f32_of(qk_hi[:, 0, :]), ALU.subtract).then_inc(lo_ready, 1)
            dve.wait_ge(rope_ready, 4)
            V.tensor_tensor(roped[:, 1, :], rope_c[1], rope_s[1], ALU.add).then_inc(roped_ready, 1)
            dve.wait_ge(ld_x1, 16)
            V.tensor_scalar(xs[:, 1, :], xT[:, cols(1)], ys[:, 1:2], None, ALU.mult).then_inc(xs_ready, 1)
            dve.wait_ge(hi_ready, 2)
            V.tensor_tensor(qk_lo[:, 1, :], roped[:, 1, :], f32_of(qk_hi[:, 1, :]), ALU.subtract).then_inc(lo_ready, 1)
            modulate(1)
            for k in range(GROUPS * MXU):
                reduce_max(k // MXU, k % MXU)
                if k in ROTATE_AT:
                    rotate(1, ROTATE_AT.index(k))
                if k % MXU == MXU - 1:
                    place_max(k // MXU)
                if k == INV_AT[0]:
                    invert(0)
                if k == INV_AT[1]:
                    normalise(0)
            dve.wait_ge(ld_small, 16)
            dve.wait_ge(mx_reduced, GROUPS * MXU)
            for b in range(B):
                V.tensor_copy(temb[:, b, :], cond[:, b:b + 1].broadcast_to([P, P])).then_inc(temb_ready, 1)
            residual(0)
            x1_low(0)
            dve.wait_ge(w_lo, len(range(0, UP_COLS, S)) + len(range(0, DN_COLS, S)))
            for part in range(4):
                gates(0, part)
            for i in range(N_UNITS + 1):
                if i < N_UNITS:
                    finish_hidden(i)
                if i:
                    hidden_lo(i - 1)
                for _ in due("invert 1", i):
                    invert(1)
                for _ in due("normalise 1", i):
                    normalise(1)
                for _ in due("residual 1", i):
                    residual(1)
                for _ in due("x1 low 1", i):
                    x1_low(1)
                for part in due("gates 1", i):
                    gates(1, part)
                for b in due("x2 low", i):
                    x2_low(b)
                for b in due("choose zones", i):
                    choose_zones(b)
                for b in due("weigh zones", i):
                    weigh_zones(b)
                for b in due("spread weights", i):
                    spread_weights(b)
                for z in due("b low", i):
                    zone_b_low(z)
                if i == E_TOTAL + FFN_UNITS + 1:
                    add_residual(0)
            add_residual(1)

        @block.scalar
        def _(act):
            A = nc.scalar
            act.wait_ge(ld_const, 16)
            act.wait_ge(sel_zero, 1)
            A.copy(one_col[:], consts[:, C_ONE:C_ONE + 1])
            for g in range(NG):
                q = slice(32 * g, 32 * g + 32)
                A.copy(sel[q, g, :, :], consts[q, C_SEL:C_ID].rearrange("p (t m) -> p t m", t=4))
            A.copy(ident_b[:], consts[:, C_ID:C_MASK])
            A.copy(causal[:, S - P:S], consts[:, C_MASK:C_ONE]).then_inc(const_ready, 1)

            def take_hi(b, i):
                act.wait_ge(roped_ready, 2 * b + i + 1)
                if b:
                    act.wait_ge(rep_ready, 2 * NG)
                A.copy(qk_hi[:, i, :], roped[:, i, :]).then_inc(hi_ready, 1)

            def copy_v(b):
                act.wait_ge(v_ready, b + 1)
                if b == 0:
                    act.wait_ge(v_ones, 1)
                v_cols = v_all[:, 0:GROUPS * KB * HG * VC].rearrange("p (n k j c) -> p n k j c", n=GROUPS, k=KB, j=HG)
                for kb in range(KB):
                    A.copy(v_cols[:, b * NG:(b + 1) * NG, kb, :, 0:HD],
                           QM[:, kb * P:(kb + 1) * P].rearrange("p (g j d) -> p g j d", g=NG, j=HG)
                           ).then_inc(v_copied, 1)

            def copy_stacked(w):
                i = w % 2
                act.wait_ge(rep_ready, w + 1)
                bank = ST[:, w % 4 if w < 2 * NG else slot_of("stack", w // 2) + i, :]
                if i == 0:
                    A.copy(stacked[:, w, :], bank).then_inc(rep_copied, 1)
                else:
                    A.activation(stacked[:, w, :], bank, ACT.Identity, bias=one_col[:]).then_inc(rep_copied, 1)

            def exp(n, u):
                s = n % 2
                c, h2 = divmod(u, 2)
                act.wait_ge(st_full, STU * n + u + 1)
                if n >= 2 and u == 0:
                    act.wait_ge(pv_full, n - 1)
                w = (BANK, 3 * P, BANK)[c]
                A.activation(probs[s][:, c, 2 * h2:2 * h2 + 2, 0:w],
                             ST[:, slot_of("exp", n, u):slot_of("exp", n, u) + 2, 0:w], ACT.Exp,
                             scale=float(1.0 / np.sqrt(np.float32(HD)))).then_inc(exp_done, 1)

            def copy_qm(n):
                act.wait_ge(qm_full, n + 1)
                A.copy(q_mov[:, n % 2, :], QM).then_inc(qm_copied, 1)

            def copy_pv(n):
                act.wait_ge(pv_full, n + 1)
                if n >= 2:
                    act.wait_ge(stored[n % 2], 16 * (n // 2))
                A.copy(o_sb[n % 2][:], PV).then_inc(pv_copied, 1)

            def x1_high(b):
                act.wait_ge(x1_ready, b + 1)
                A.copy(x1_hi[:, b, :], x1[:, cols(b)]).then_inc(x1_hi_ready, 1)

            def activate(i):
                kind, b, w = UNITS[i]
                r = i % RING
                act.wait_ge(up_full, i + 1)
                if i == 0:
                    act.wait_ge(w_lo, (UP_COLS + DN_COLS) // S)
                if i >= RING:
                    if UNITS[i - RING][0] != "zone":
                        act.wait_ge(h_ready, i - RING + 1)
                    else:
                        act.wait_ge(lo_done, i - RING + 1)
                if kind == "shared":
                    func, scale = ACT.Tanh, 0.5
                elif kind == "routed":
                    func, scale = ACT.Gelu, 1.0
                else:
                    func, scale = ACT.Gelu_apprx_tanh, 1.0
                A.activation(act_out[r], pair_of(i)[:, 0, :], func, scale=scale).then_inc(act_done, 1)

            def hidden_hi(i):
                r = i % RING
                if UNITS[i][0] == "zone":
                    src_ = act_out[r]
                    act.wait_ge(act_done, i + 1)
                else:
                    src_ = hidden[r]
                    act.wait_ge(h_ready, i + 1)
                if i >= RING:
                    act.wait_ge(down_done, i - RING + 1)
                    act.wait_ge(lo_done, i - RING + 1)
                A.copy(h_hi[r], src_).then_inc(hi_done, 1)

            def gates_t_copy(b):
                act.wait_ge(gateT_full, b + 1)
                act.wait_ge(gates_zero, B)
                A.copy(gates_t[b][0:2 * EXPERTS, :], psum[0:2 * EXPERTS, 7 - b, :]).then_inc(gateT_copied, 1)

            def finish_experts(b):
                act.wait_ge(down_done, EXP_UNITS * (b + 1))
                A.activation(x2[:, b, :], OUT, ACT.Identity, scale=1.0 / 16.0,
                             accum_out=pooled[:, b:b + 1]).then_inc(x2_ready, 1)
                act.wait_ge(x2_ready, b + 1)
                A.copy(x2_hi[:, b, :], x2[:, b, :]).then_inc(x2_hi_ready, 1)

            def zone_a_high(z):
                b, k = divmod(z, TOPZ)
                act.wait_ge(z_diff, b + 1)
                zone = A.value_load(zidx[0:1, b, k:k + 1], min_val=0, max_val=ZONES - 1)
                if z == 0:
                    act.wait_ge(ld_zones, 16 * 4)
                if z >= ZSLOTS:
                    act.wait_ge(down_done, E_TOTAL + ZM * (z - ZSLOTS + 1))
                A.copy(zone_w[z % ZSLOTS][:, 0, :], zone_a[:, bass.ds(zone, 1), :]).then_inc(a_hi, 1)

            def router_tanh(b):
                act.wait_ge(z_hid, b + 1)
                A.activation(hid[:, b:b + 1], MISC[0:RH, 64:65], ACT.Tanh, scale=1.0 / S,
                             bias=small[0:RH, W_B1:W_B1 + 1]).then_inc(z_tanh, 1)

            def exp_of_minus_logits(b):
                act.wait_ge(logits, b + 1)
                bank = psum[:, 1, 0:KB * EXPERTS] if b == 0 else MISC[:, 0:KB * EXPERTS]
                A.activation(e_neg[:, b], bank.rearrange("p (t e) -> p t e", t=KB), ACT.Exp,
                             scale=-1.0).then_inc(expneg, 1)

            def split_high(k):
                hi, lo, c, at_ = chunks[k]
                if k == 0:
                    act.wait_ge(ld_raw, 16)
                if k == UP_COLS // S:
                    act.wait_ge(rep_ready, 2 * GROUPS)
                A.copy(hi[:, c:c + S], raw[:, at_:at_ + S]).then_inc(w_hi, 1)

            take_hi(0, 0)
            take_hi(0, 1)
            act.wait_ge(rep_ready, 1)
            act.wait_ge(pad0_zero, 1)
            for j in range(HG):
                q = slice(32 * j, 32 * j + 32)
                A.copy(q_pad[0][q, j, :], ST[q, 0, :]).then_inc(q0_placed, 1)
            copy_stacked(1)
            copy_stacked(0)
            A.copy(ident_r[:], consts[:, C_ID:C_MASK]).then_inc(const_ready, 1)
            copy_stacked(2)
            copy_stacked(3)
            copy_v(0)
            for w in range(4, 2 * NG):
                copy_stacked(w)
            copy_qm(0)
            exp(0, 0)
            exp(0, 1)
            for n in range(GROUPS):
                exp(n, 2)
                if n == 0:
                    take_hi(1, 0)
                if n:
                    copy_pv(n - 1)
                if n == GROUPS - 1:
                    exp_of_minus_logits(0)
                if (n, 0) in SPLITS:
                    split_high(SPLITS[n, 0])
                exp(n, 3)
                if n == 0:
                    take_hi(1, 1)
                if n in (1, 2):
                    copy_stacked(4 * n + 4)
                    copy_stacked(4 * n + 5)
                exp(n, 4)
                if n + 1 < GROUPS:
                    copy_qm(n + 1)
                exp(n, 5)
                if n == 5:
                    act.wait_ge(ld_sele, 16)
                    act.wait_ge(sele_zero, 1)
                    A.copy(sel_e[0:2 * EXPERTS, :, :],
                           gate_rows[:].rearrange("p (e m) -> p e m", m=P)).then_inc(sele_ready, 1)
                if n == GROUPS - 2:
                    x1_high(0)
                if n in (1, 2):
                    copy_stacked(4 * n + 6)
                    copy_stacked(4 * n + 7)
                if n + 1 < GROUPS:
                    exp(n + 1, 0)
                    if (n, 2) in SPLITS:
                        split_high(SPLITS[n, 2])
                    exp(n + 1, 1)
                if n == 0:
                    copy_v(1)
            activate(0)
            copy_pv(GROUPS - 1)
            hidden_hi(0)
            for i in range(1, N_UNITS):
                activate(i)
                if UNITS[i][0] != "zone":
                    if i > 1:
                        hidden_hi(i - 1)
                else:
                    if UNITS[i - 1][0] != "zone":
                        hidden_hi(i - 1)
                    hidden_hi(i)
                for b in due("copy gates", i):
                    gates_t_copy(b)
                for _ in due("x1 high 1", i):
                    x1_high(1)
                for _ in due("exp 1", i):
                    exp_of_minus_logits(1)
                for b in due("finish experts", i):
                    finish_experts(b)
                for b in due("router tanh", i):
                    router_tanh(b)
                for z in due("a high", i):
                    zone_a_high(z)

        @block.tensor
        def _(pe):
            T = nc.tensor
            pe.wait_ge(pads_early, 1)
            warm = max_pad[0][:].rearrange("p a b c -> p (a b c)")
            for _ in range(WARM):
                T.matmul(ST[:, 0, :], warm[:, 0:P], warm, start=True, stop=True)
            pe.wait_ge(ys_ready, 2)
            pe.wait_ge(sq_ready, 2)
            T.matmul(QM[:, 0:B], w_cond_sq, ys_sq[:], start=True, stop=True).then_inc(dsum_ready, 1)

            def modulate(b):
                pe.wait_ge(xs_ready, b + 1)
                if b:
                    pe.wait_ge(xc_ready, b)
                T.matmul(PV, w_cond, xs[:, b, :], start=True, stop=True).then_inc(cond_ready, 1)

            def wait_slot(*item):
                k = ST_ORDER.index(item)
                if k < 2:
                    pe.wait_ge(rep_copied, 2 * NG)
                    return
                kind, n, *u = ST_ORDER[k - 2]
                if kind == "exp":
                    pe.wait_ge(exp_done, STU * n + u[0] + 1)
                elif kind == "project":
                    pe.wait_ge(rope_ready, 4 + 2 * (n + 1))
                else:
                    pe.wait_ge(rep_copied, 2 * (n + 1))

            def project(b, i):
                pe.wait_ge(xc_ready, b + 1)
                if b == 0:
                    pe.wait_ge(ld_proj, 32)
                    at_ = 2 * i
                else:
                    wait_slot("project", i)
                    at_ = slot_of("project", i)
                T.matmul(ST[:, at_, :], w_qkv[:, i * D:(i + 1) * D], xc[:, b, :], start=True, stop=True)
                T.matmul(ST[:, at_ + 1, :], w_rot[:, i * D:(i + 1) * D], xc[:, b, :],
                         start=True, stop=True).then_inc(qk_ready, 1)

            def project_v(b):
                if b == 0:
                    pe.wait_ge(dvar_ready, 1)
                else:
                    pe.wait_ge(qm_copied, 2)
                for kb in range(KB):
                    last = T.matmul(QM[:, kb * P:(kb + 1) * P], xc[:, b, kb * P:(kb + 1) * P],
                                    w_qkv[:, 2 * D:3 * D], start=True, stop=True)
                last.then_inc(v_ready, 1)

            def stack(w):
                b, g, i = w // (2 * NG), w // 2 % NG, w % 2
                if w == 0:
                    pe.wait_ge(const_ready, 1)
                if w % (2 * NG) < 2:
                    pe.wait_ge(lo_ready, 2 * b + i + 1)
                if b == 0:
                    bank = ST[:, w % 4, :]
                    if w == 2:
                        pe.wait_ge(rope_ready, 4)
                    if w >= 4:
                        pe.wait_ge(rep_copied, max(w - 3, 2))
                else:
                    bank = ST[:, slot_of("stack", w // 2) + i, :]
                    if i == 0:
                        wait_slot("stack", w // 2)
                T.matmul(bank, sel[:, g, 2 * i, :], qk_hi[:, i, :], start=True, stop=False)
                T.matmul(bank, sel[:, g, 2 * i + 1, :], qk_lo[:, i, :], start=False, stop=True).then_inc(rep_ready, 1)

            def scores_for_max(n, u):
                s = n % 2
                qb, heads = MX_UNITS[u]
                width = max(2 * P, P * (qb + 1))
                if u == 0:
                    if n == 0:
                        pe.wait_ge(q0_placed, HG)
                    else:
                        pe.wait_ge(q_padded[s], 16 * HG * ((n + 1) // 2))
                    pe.wait_ge(rep_copied, 2 * n + 2 if n else 1)
                if n or u > 1:
                    pe.wait_ge(mx_reduced, MXU * n + u - 1)
                for i, j in enumerate(heads):
                    o = MX[:, u % 2, i * 2 * P:i * 2 * P + width]
                    last = T.matmul(o, q_pad[s][:, j, qb * P:(qb + 1) * P], stacked[:, 2 * n + 1, 0:width],
                                    start=True, stop=True)
                last.then_inc(mx_full, 1)

            def lay_max_under_q(n):
                pe.wait_ge(m_ready, n + 1)
                if n == 0:
                    pe.wait_ge(v_copied, KB)
                    pe.wait_ge(const_ready, 2)
                else:
                    pe.wait_ge(qm_copied, n)
                if n == 2:
                    pe.wait_ge(v_copied, B * KB)
                T.matmul(QM, ident_r[:], stacked[:, 2 * n, :], start=True, stop=True)
                for qb in range(KB):
                    last = T.matmul(QM[:, qb * P:(qb + 1) * P],
                                    max_pad[n % 2][:, qb, :, :].rearrange("p j r -> p (j r)"), ident_b[:],
                                    start=False, stop=True, skip_group_check=True)
                last.then_inc(qm_full, 1)

            def scores_of_head(n, u, i):
                s = n % 2
                c, h2 = divmod(u, 2)
                if i == 0:
                    if u == 0:
                        pe.wait_ge(qm_copied, n + 1)
                        pe.wait_ge(k_padded[s], 16 * HG * (n // 2 + 1))
                    wait_slot("exp", n, u)
                j = 2 * h2 + i
                bank = ST[:, slot_of("exp", n, u) + i, :]
                q = q_mov[:, s, :]
                if c == 0:
                    last = T.matmul(bank, k_pad[s][:, j, 0:P], q, start=True, stop=True)
                elif c == 1:
                    last = T.matmul(bank[:, 0:3 * P], k_pad[s][:, j, P:2 * P], q[:, P:S], start=True, stop=True)
                else:
                    T.matmul(bank[:, 0:2 * P], k_pad[s][:, j, 2 * P:3 * P], q[:, 2 * P:S], start=True, stop=True)
                    last = T.matmul(bank[:, 2 * P:S], k_pad[s][:, j, 3 * P:S], q[:, 2 * P:S], start=True, stop=True)
                if i == 1:
                    last.then_inc(st_full, 1)

            def scores_for_exp(n, u):
                for i in range(2):
                    scores_of_head(n, u, i)

            def weigh_v(n, kb, heads=range(HG)):
                c = min(kb, 2)
                if kb < 3 and heads[0] == 0:
                    pe.wait_ge(masked, 3 * n + c + 1)
                if kb == 0 and heads[0] == 0:
                    pe.wait_ge(v_copied, KB * (n // NG + 1))
                    if n:
                        pe.wait_ge(pv_copied, n)
                o, w = ((0, S), (0, 3 * P), (0, 2 * P), (3 * P, P))[kb]
                for j in heads:
                    v0 = ((n * KB + kb) * HG + j) * VC
                    last = T.matmul(PV[32 * j:32 * j + 32, S - w:S], v_all[:, v0:v0 + 32],
                                    probs[n % 2][:, c, j, o:o + w], start=(kb == 0), stop=(kb == KB - 1),
                                    skip_group_check=True)
                if kb == 3:
                    last.then_inc(pv_full, 1)

            modulate(0)
            project(0, 0)
            project(0, 1)
            stack(0)
            project_v(0)
            modulate(1)
            stack(1)
            stack(2)
            for k in range(AHEAD):
                scores_for_max(k // MXU, k % MXU)
                for step, at_ in enumerate(FIRST_AT):
                    if at_ != k:
                        continue
                    if step < 5:
                        stack(3 + step)
                    elif step == 5:
                        lay_max_under_q(0)
                    elif step < 8:
                        scores_for_exp(0, step - 6)
                    else:
                        project(1, step - 8)

            def project_out(b):
                pe.wait_ge(onorm_ready, b + 1)
                pe.wait_ge(ld_small, 16)
                if b == 0:
                    pe.wait_ge(mx_reduced, GROUPS * MXU)
                T.matmul(psum[:, 0, :] if b == 0 else MISC, small[:, W_OUT:W_OUT + D], packed_out[:],
                         start=True, stop=True).then_inc(proj_ready, 1)

            def route_experts(b):
                pe.wait_ge(temb_ready, B)
                pe.wait_ge(x1_ready, b + 1)
                bank = psum[:, 1, :] if b == 0 else MISC
                T.matmul(bank[:, 0:KB * EXPERTS], temb[:, b, :], small[:, W_RT:W_RB], start=True, stop=True)
                for t in range(KB):
                    last = T.matmul(bank[:, t * EXPERTS:(t + 1) * EXPERTS],
                                    x1[:, b * S + t * P:b * S + (t + 1) * P], small[:, W_R:W_RT],
                                    start=False, stop=True, skip_group_check=True)
                last.then_inc(logits, 1)

            def three(o, hi, lo, x_hi, x_lo, start, stop):
                T.matmul(o, hi, x_hi, start=start, stop=False)
                T.matmul(o, lo, x_hi, start=False, stop=False)
                return T.matmul(o, hi, x_lo, start=False, stop=stop)

            def up(i):
                kind, b, w = UNITS[i]
                r = i % RING
                if i == 0:
                    pe.wait_ge(expneg, 1)
                    pe.wait_ge(w_lo, (UP_COLS + DN_COLS) // S)
                elif i < RING:
                    pe.wait_ge(exp_done, GROUPS * STU)
                else:
                    if UNITS[i - RING][0] != "zone":
                        pe.wait_ge(h_ready, i - RING + 1)
                    else:
                        pe.wait_ge(act_done, i - RING + 1)
                if kind == "zone":
                    z, m = b * TOPZ + w // ZM, w % ZM
                    if w == 0:
                        pe.wait_ge(x2_lo_ready, b + 1)
                    if m == 0:
                        pe.wait_ge(a_lo, z + 1)
                    c = slice(m * P, (m + 1) * P)
                    zw_ = zone_w[z % ZSLOTS]
                    last = three(pair_of(i)[:, 0, :], zw_[:, 0, c], zw_[:, 1, c], x2_hi[:, b, :], x2_lo[:, b, :], True, True)
                else:
                    if w == 0 and kind == "shared":
                        pe.wait_ge(x1_lo_ready, b + 1)
                    for t, c in enumerate(up_cols(kind, w)):
                        last = three(pair_of(i)[:, t, :], up_hi[:, c:c + P], up_lo[:, c:c + P],
                                     x1_hi[:, b, :], x1_lo[:, b, :], True, True)
                    if kind == "routed":
                        if w == 0:
                            pe.wait_ge(gateT_copied, b + 1)
                            pe.wait_ge(sele_ready, 1)
                        last = T.matmul(pair_of(i)[:, 1, :], sel_e[:, w, :], gates_t[b], start=True, stop=True)
                last.then_inc(up_full, 1)

            def down(i):
                kind, b, w = UNITS[i]
                r = i % RING
                pe.wait_ge(lo_done, i + 1)
                first = w == 0 and kind != "routed"
                final = i + 1 == N_UNITS or (UNITS[i + 1][2] == 0 and UNITS[i + 1][0] != "routed")
                if first:
                    if i == 0:
                        pe.wait_ge(gateT_copied, 1)
                    elif kind == "shared":
                        pe.wait_ge(x2_ready, b)
                    elif b == 0:
                        pe.wait_ge(x2_ready, B)
                    else:
                        pe.wait_ge(y_ready, b)
                if kind == "zone":
                    z, m = b * TOPZ + w // ZM, w % ZM
                    c = slice(m * P, (m + 1) * P)
                    hi, lo = zone_w[z % ZSLOTS][:, 2, c], zone_w[z % ZSLOTS][:, 3, c]
                    if m == 0:
                        pe.wait_ge(b_lo, z + 1)
                else:
                    c = dn_col(kind, w)
                    hi, lo = dn_hi[:, c:c + D], dn_lo[:, c:c + D]
                three(OUT, hi, lo, h_hi[r], h_lo[r], first, final).then_inc(down_done, 1)

            def transpose_gates(b):
                pe.wait_ge(gate_ready, b + 1)
                if b == 0:
                    pe.wait_ge(qm_copied, GROUPS)
                pe.wait_ge(expneg, b + 1)
                for t in range(KB):
                    last = T.transpose(psum[:, 7 - b, :][0:2 * EXPERTS, t * P:(t + 1) * P], gate_hl[:, b, t, :],
                                       f32_of(ident_r[:]))
                last.then_inc(gateT_full, 1)

            def zone_hidden(b):
                pe.wait_ge(x2_ready, b + 1)
                if b == 0:
                    pe.wait_ge(gateT_copied, B)
                else:
                    pe.wait_ge(z_all, b)
                T.matmul(MISC[0:RH, 64:65], small[:, W_Z1:W_Z1 + RH], pooled[:, b:b + 1],
                         start=True, stop=True).then_inc(z_hid, 1)

            def zone_logits(b):
                pe.wait_ge(z_tanh, b + 1)
                T.matmul(MISC[0:1, 72:80], hid[:, b:b + 1], small[0:RH, W_Z2:W_Z2 + ZONES],
                         start=True, stop=True).then_inc(z_logit, 1)

            def zone_spread(b):
                pe.wait_ge(z_w, b + 1)
                T.matmul(MISC[:, 80:80 + TOPZ], ones_row[:], zw[:, b, :], start=True, stop=True).then_inc(z_bc, 1)

            for n in range(GROUPS):
                spent, unit = 0.0, 0

                def maxima(cost):
                    nonlocal spent, unit
                    while unit < MXU and spent >= unit * GROUP_COST.get(n, USUAL_COST) / MXU - 1e-9:
                        k = MXU * n + AHEAD + unit
                        if k < GROUPS * MXU:
                            scores_for_max(k // MXU, k % MXU)
                        unit += 1
                    spent += cost

                def scores(m, u):
                    for i in range(2):
                        maxima((0.21, 0.16, 0.21)[u // 2])
                        scores_of_head(m, u, i)

                def weigh(m, kb, heads=range(HG)):
                    maxima((0.9, 0.7, 0.5, 0.25)[kb] * len(heads) / HG)
                    weigh_v(m, kb, heads)

                def stack_pair(g):
                    for i in range(2):
                        maxima(0.43)
                        stack(2 * g + i)

                scores(n, 2)
                if n:
                    weigh(n - 1, 3)
                scores(n, 3)
                if n in (1, 2):
                    stack_pair(2 * n + 2)
                if n + 1 < GROUPS:
                    weigh(n, 0, range(0, 2))
                    scores(n, 4)
                    weigh(n, 0, range(2, 4))
                    maxima(0.43)
                    lay_max_under_q(n + 1)
                    if n == GROUPS - 2:
                        maxima(0.9)
                        project_out(0)
                    scores(n, 5)
                    if n in (1, 2):
                        stack_pair(2 * n + 3)
                    weigh(n, 1, range(0, 2))
                    scores(n + 1, 0)
                    weigh(n, 1, range(2, 4))
                    scores(n + 1, 1)
                    if n == GROUPS - 2:
                        maxima(0.9)
                        route_experts(0)
                    weigh(n, 2)
                    if n == 0:
                        maxima(0.9)
                        project_v(1)
                    maxima(0.0)
                else:
                    scores(n, 4)
                    weigh(n, 0)
                    scores(n, 5)
                    weigh(n, 1)
                    up(0)
                    weigh(n, 2)
                    weigh(n, 3)

            for i in range(1, N_UNITS + LAG):
                for b in due("transpose gates", i):
                    transpose_gates(b)
                for _ in due("project 1", i):
                    project_out(1)
                for _ in due("route 1", i):
                    route_experts(1)
                for b in due("zone hidden", i):
                    zone_hidden(b)
                for b in due("zone logits", i):
                    zone_logits(b)
                for b in due("zone spread", i):
                    zone_spread(b)
                if i < N_UNITS:
                    up(i)
                if i >= LAG:
                    down(i - LAG)


def host_constants():
    pattern = np.zeros((4, 32, P), np.float32)
    for j in range(HG):
        for d in range(HD):
            src = j * HD + d
            for t, blocks in enumerate(((1, 2), (3,), (1, 3), (2,))):
                for r in blocks:
                    pattern[t, src, 32 * j + HD * r + d] = 1.0
    consts = np.zeros((P, C_END), np.float32)
    consts[:, C_SEL:C_ID] = np.tile(pattern.transpose(1, 0, 2).reshape(32, 4 * P), (4, 1))
    consts[:, C_ID:C_MASK] = np.eye(P, dtype=np.float32)
    k, q = np.mgrid[0:P, 0:P]
    consts[:, C_MASK:C_ONE] = np.where(k > q, np.float32(BIG), np.float32(0.0)).T
    consts[:, C_ONE] = np.isin(np.arange(P) % 32, (0, 1))
    sel_e = np.zeros((2 * EXPERTS, EXPERTS * P), np.float32)
    for e in range(EXPERTS):
        sel_e[[e, EXPERTS + e], e * P:(e + 1) * P] = 1.0
    half = HD // 2
    inv = (1.0 / np.power(np.float32(10000.0), np.arange(half, dtype=np.float32) / np.float32(half))).astype(np.float32)
    ang = (np.arange(S, dtype=np.float32)[:, None] * inv[None, :]).astype(np.float64)
    cos = np.cos(ang).astype(np.float32).T
    sin = np.sin(ang).astype(np.float32).T
    cos = np.tile(np.concatenate([cos, cos]), (H, 1))
    sin = np.tile(np.concatenate([-sin, sin]), (H, 1))
    return consts, sel_e, np.concatenate([cos, sin], axis=1)


def swapped(w):
    return w.reshape(-1, 2, HD // 2, D)[:, ::-1].reshape(-1, D)


def laid_out(inputs):
    a = {k: np.asarray(v) for k, v in inputs.items()}
    consts, sel_e, rotary = host_constants()
    wq = a["L0_attn_w_qkv"]
    small = np.zeros((P, W_END), np.float32)
    small[:, W_OUT:W_OUT + D] = a["L0_attn_w_out"].T
    wr = a["L0_cond2_W_router"]
    small[:, W_R:W_R + EXPERTS] = wr[:, 0:D].T
    small[:, W_RT:W_RB] = np.tile(wr[:, D:2 * D].T, (1, KB))
    small[:, W_RB:W_RB + EXPERTS] = a["L0_cond2_router_bias"][None, :]
    small[:, W_IOTA:W_IOTA + EXPERTS] = np.arange(EXPERTS)[None, :]
    small[:, W_Z1:W_Z1 + RH] = a["L0_ffn_W1"]
    small[0:RH, W_Z2:W_Z2 + ZONES] = a["L0_ffn_W2"]
    small[0:RH, W_B1] = a["L0_ffn_b1"]
    small[0, W_B2:W_B2 + ZONES] = a["L0_ffn_b2"]
    up = np.stack([a["L0_cond2_s_w1"], a["L0_cond2_s_w3"]], axis=1)
    experts = [up.transpose(3, 0, 1, 2).reshape(D, -1), a["L0_cond2_r_w1"].transpose(2, 0, 1).reshape(D, -1),
               a["L0_cond2_s_w2"].reshape(SHARED, D, HID_S // P, P).transpose(3, 0, 2, 1).reshape(P, -1),
               a["L0_cond2_r_w2"].transpose(2, 0, 1).reshape(HID_R, -1)]
    arrays = {
        "xT": a["x"].reshape(NT, D).T, "condT": a["cond_1024"].T, "L0_cond_weight": a["L0_cond_weight"],
        "w_qkvT": wq.T, "w_rotT": swapped(wq[:2 * D]).T, "rotary": rotary, "consts": consts, "sel_e": sel_e,
        "small": small,
        "experts": np.concatenate(experts, axis=1),
        "L0_ffn_Wa": a["L0_ffn_Wa"], "L0_ffn_Wb": a["L0_ffn_Wb"],
    }
    return {k: np.ascontiguousarray(v) for k, v in arrays.items()}


def kernel(**inputs):
    import concourse.bacc as bacc
    from concourse.bass_utils import run_bass_kernel_spmd

    nc = bacc.Bacc("TRN2", target_bir_lowering=False, num_devices=1)
    arrays = laid_out(inputs)
    io = {n: nc.dram_tensor("in_" + n, a.shape, F32, kind="ExternalInput").ap() for n, a in arrays.items()}
    scratch = nc.dram_tensor("scratch", (GROUPS + 1, P, S), F32, kind="Internal").ap()
    out = nc.dram_tensor("out_0_dram", (D, NT), F32, kind="ExternalOutput").ap()
    program(nc, io, scratch, out)
    r = run_bass_kernel_spmd(nc, [{"in_" + n: a for n, a in arrays.items()}], core_ids=[0])
    return np.ascontiguousarray(r.results[0]["out_0_dram"].T).reshape(B, S, D)
```
